# Optimizing a Trainium2 kernel written in Bass

```python
import numpy as np
import jax
import jax.numpy as jnp

def _softmax(x, axis=-1):
    return jax.nn.softmax(x, axis=axis)

def _gelu(x):
    return jax.nn.gelu(x, approximate=True)

def _silu(x):
    return jax.nn.silu(x)

def _sigmoid(x):
    return jax.nn.sigmoid(x)

def _layernorm(x, axis=-1, eps=1e-05):
    m = jnp.mean(x, axis=axis, keepdims=True)
    v = jnp.var(x, axis=axis, keepdims=True)
    return (x - m) / jnp.sqrt(v + eps)

def _scatter_add(tgt, idx, src, axis=0):
    return tgt.at[idx].add(src)

def _segment_sum(src, seg, n):
    return jax.ops.segment_sum(src, seg, n)
kernel_name = 'mk_xattn_ffn_d2_seqx_r8_e1818b'

def setup_inputs(seed: int=0):
    np.random.seed(seed)
    _w = jnp.asarray

    def _rec_inputs():
        import jax
        import jax.numpy as jnp
        _rk = jax.random.key(seed)
        x = -0.0002928 + 1 * jax.random.normal(jax.random.fold_in(_rk, 1), (64, 64, 128), jnp.float32)
        _lenS = 64 - jax.random.randint(jax.random.fold_in(_rk, 7), (64,), 0, max(1, 64 // 4) + 1, jnp.int32)
        _lenS2 = 64 - jax.random.randint(jax.random.fold_in(_rk, 8), (64,), 0, max(1, 64 // 4) + 1, jnp.int32)
        _ctx_2048P = jax.random.normal(jax.random.fold_in(_rk, 11), (64, 16, 256), jnp.float32)
        _ctx_2048c = jax.random.dirichlet(jax.random.fold_in(_rk, 511), 0.3 * jnp.ones((16,), jnp.float32), (64, 64))
        _ctx_2048t = jnp.einsum('bsk,bkd->bsd', _ctx_2048c, _ctx_2048P)
        _ctx_2048t = _ctx_2048t * jax.lax.rsqrt(jnp.mean(jnp.square(_ctx_2048t)) + 1e-12) * 0.953939
        ctx_2048 = -0.000514642 + 1.00011 * (_ctx_2048t + 0.3 * jax.random.normal(jax.random.fold_in(_rk, 611), (64, 64, 256), jnp.float32))
        return (x, ctx_2048)
    x, ctx_2048 = _rec_inputs()

    def _L0_xattn_setup():
        import jax, jax.numpy as jnp
        import numpy as np
        NUM_HEADS = 16
        key = jax.random.key(seed)
        ks = jax.random.split(key, 5)
        dim = 128
        B, N, N_c = (4, 128, 32)
        x = jax.random.normal(ks[0], (B, N, dim), dtype=jnp.float32)
        context = jax.random.normal(ks[1], (B, N_c, 2 * dim), dtype=jnp.float32)
        w_qkv = jax.random.normal(ks[2], (3 * dim, dim), dtype=jnp.float32) * 0.02
        w_proj = jax.random.normal(ks[3], (dim, dim), dtype=jnp.float32) * 0.02
        b_proj = jax.random.normal(ks[4], (dim,), dtype=jnp.float32) * 0.02
        return {'x': x, 'context': context, 'w_qkv': w_qkv, 'w_proj': w_proj, 'b_proj': b_proj}
    _L0_xattn_all = _L0_xattn_setup()
    _L0_xattn_in = {k: v for k, v in _L0_xattn_all.items() if k in ('w_qkv', 'w_proj', 'b_proj')}
    del _L0_xattn_all

    def _L0_ffn_setup():
        import jax, jax.numpy as jnp
        import numpy as np
        B, S, H, E, I, MAX_K, A_HID = (2, 256, 128, 8, 336, 6, 50)
        key = jax.random.key(seed)
        ks = jax.random.split(key, 10)
        sc = 0.02
        return {'hidden_states': jax.random.normal(ks[0], (B, S, H), dtype=jnp.float32), 'router_w': jax.random.normal(ks[1], (E, H), dtype=jnp.float32) * sc, 'actor_w1': jax.random.normal(ks[2], (A_HID, H), dtype=jnp.float32) * sc, 'actor_b1': jnp.zeros((A_HID,), dtype=jnp.float32), 'actor_w2': jax.random.normal(ks[3], (MAX_K, A_HID), dtype=jnp.float32) * sc, 'actor_b2': jnp.zeros((MAX_K,), dtype=jnp.float32), 'gate_w': jax.random.normal(ks[4], (E, I, H), dtype=jnp.float32) * sc, 'up_w': jax.random.normal(ks[5], (E, I, H), dtype=jnp.float32) * sc, 'down_w': jax.random.normal(ks[6], (E, H, I), dtype=jnp.float32) * sc}
    _L0_ffn_all = _L0_ffn_setup()
    _L0_ffn_in = {k: v for k, v in _L0_ffn_all.items() if k in ('router_w', 'actor_w1', 'actor_b1', 'actor_w2', 'actor_b2', 'gate_w', 'up_w', 'down_w')}
    del _L0_ffn_all

    def _L1_xattn_setup():
        import jax, jax.numpy as jnp
        import numpy as np
        B, N, DIM = (8, 512, 128)
        M, CTX = (32, 256)
        HEADS, DH = (16, 64)
        INNER = HEADS * DH
        EPS = 1e-06

        def _split_heads(t):
            b, n, _ = t.shape
            return t.reshape(b, n, HEADS, DH).transpose(0, 2, 1, 3)
        key = jax.random.key(seed)
        ks = jax.random.split(key, 6)
        x = jax.random.normal(ks[0], (B, N, DIM), dtype=jnp.float32)
        context = jax.random.normal(ks[1], (B, M, CTX), dtype=jnp.float32)
        Wq = jax.random.normal(ks[2], (DIM, INNER), dtype=jnp.float32) / np.sqrt(DIM)
        Wkv = jax.random.normal(ks[3], (CTX, 2 * INNER), dtype=jnp.float32) / np.sqrt(CTX)
        null_kv = jax.random.normal(ks[4], (2, DH), dtype=jnp.float32) / np.sqrt(2.0)
        Wout = jax.random.normal(ks[5], (INNER, DIM), dtype=jnp.float32) / np.sqrt(INNER)
        ln_scale = jnp.ones((DIM,), dtype=jnp.float32)
        ln_bias = jnp.zeros((DIM,), dtype=jnp.float32)
        return {'x': x, 'context': context, 'Wq': Wq, 'Wkv': Wkv, 'null_kv': null_kv, 'Wout': Wout, 'ln_scale': ln_scale, 'ln_bias': ln_bias}
    _L1_xattn_all = _L1_xattn_setup()
    _L1_xattn_in = {k: v for k, v in _L1_xattn_all.items() if k in ('Wq', 'Wkv', 'null_kv', 'Wout', 'ln_scale', 'ln_bias')}
    del _L1_xattn_all

    def _L1_ffn_setup():
        import jax, jax.numpy as jnp
        import numpy as np
        D, H, O, E, TOPK = (128, 512, 128, 8, 2)
        B, S = (4, 128)
        key = jax.random.key(seed)
        ks = jax.random.split(key, 12)
        std = 0.02
        return {'hidden_states': jax.random.normal(ks[0], (B, S, D), dtype=jnp.float32), 'norm_weight': jnp.ones((D,), dtype=jnp.float32), 'router_w': jax.random.normal(ks[1], (E, D), dtype=jnp.float32) * std, 'sw1': jax.random.normal(ks[2], (D, H), dtype=jnp.float32) * (1.0 / np.sqrt(D)), 'sb1': jnp.zeros((H,), dtype=jnp.float32), 'sw2': jax.random.normal(ks[3], (H, O), dtype=jnp.float32) * (1.0 / np.sqrt(H)), 'sb2': jnp.zeros((O,), dtype=jnp.float32), 'ew1': jax.random.normal(ks[4], (E, D, H), dtype=jnp.float32) * (1.0 / np.sqrt(D)), 'eb1': jnp.zeros((E, H), dtype=jnp.float32), 'ew2': jax.random.normal(ks[5], (E, H, O), dtype=jnp.float32) * (1.0 / np.sqrt(H)), 'eb2': jnp.zeros((E, O), dtype=jnp.float32)}
    _L1_ffn_all = _L1_ffn_setup()
    _L1_ffn_in = {k: v for k, v in _L1_ffn_all.items() if k in ('norm_weight', 'router_w', 'sw1', 'sb1', 'sw2', 'sb2', 'ew1', 'eb1', 'ew2', 'eb2')}
    del _L1_ffn_all
    return {'x': x, 'ctx_2048': ctx_2048, 'L0_xattn_w_qkv': _L0_xattn_in['w_qkv'], 'L0_xattn_w_proj': _L0_xattn_in['w_proj'], 'L0_xattn_b_proj': _L0_xattn_in['b_proj'], 'L0_ffn_router_w': _L0_ffn_in['router_w'], 'L0_ffn_actor_w1': _L0_ffn_in['actor_w1'], 'L0_ffn_actor_b1': _L0_ffn_in['actor_b1'], 'L0_ffn_actor_w2': _L0_ffn_in['actor_w2'], 'L0_ffn_actor_b2': _L0_ffn_in['actor_b2'], 'L0_ffn_gate_w': _L0_ffn_in['gate_w'], 'L0_ffn_up_w': _L0_ffn_in['up_w'], 'L0_ffn_down_w': _L0_ffn_in['down_w'], 'L1_xattn_Wq': _L1_xattn_in['Wq'], 'L1_xattn_Wkv': _L1_xattn_in['Wkv'], 'L1_xattn_null_kv': _L1_xattn_in['null_kv'], 'L1_xattn_Wout': _L1_xattn_in['Wout'], 'L1_xattn_ln_scale': _L1_xattn_in['ln_scale'], 'L1_xattn_ln_bias': _L1_xattn_in['ln_bias'], 'L1_ffn_norm_weight': _L1_ffn_in['norm_weight'], 'L1_ffn_router_w': _L1_ffn_in['router_w'], 'L1_ffn_sw1': _L1_ffn_in['sw1'], 'L1_ffn_sb1': _L1_ffn_in['sb1'], 'L1_ffn_sw2': _L1_ffn_in['sw2'], 'L1_ffn_sb2': _L1_ffn_in['sb2'], 'L1_ffn_ew1': _L1_ffn_in['ew1'], 'L1_ffn_eb1': _L1_ffn_in['eb1'], 'L1_ffn_ew2': _L1_ffn_in['ew2'], 'L1_ffn_eb2': _L1_ffn_in['eb2']}

def reference(x, ctx_2048, L0_xattn_w_qkv, L0_xattn_w_proj, L0_xattn_b_proj, L0_ffn_router_w, L0_ffn_actor_w1, L0_ffn_actor_b1, L0_ffn_actor_w2, L0_ffn_actor_b2, L0_ffn_gate_w, L0_ffn_up_w, L0_ffn_down_w, L1_xattn_Wq, L1_xattn_Wkv, L1_xattn_null_kv, L1_xattn_Wout, L1_xattn_ln_scale, L1_xattn_ln_bias, L1_ffn_norm_weight, L1_ffn_router_w, L1_ffn_sw1, L1_ffn_sb1, L1_ffn_sw2, L1_ffn_sb2, L1_ffn_ew1, L1_ffn_eb1, L1_ffn_ew2, L1_ffn_eb2):
    import jax
    import jax.numpy as jnp

    def _L0_xattn_ref(x, context, w_qkv, w_proj, b_proj):
        import jax, jax.numpy as jnp
        import numpy as np
        NUM_HEADS = 16
        B, N, C = x.shape
        H = NUM_HEADS
        D = C // H
        scale = D ** (-0.5)
        qkv = (x @ w_qkv.T).reshape(B, N, 3, H, D).transpose(2, 0, 3, 1, 4)
        q, k, v = (qkv[0], qkv[1], qkv[2])
        N_c = context.shape[1]
        kv = context.reshape(B, N_c, 2, H, D).transpose(2, 0, 3, 1, 4)
        extra_k, extra_v = (kv[0], kv[1])
        k = jnp.concatenate([extra_k, k], axis=2)
        v = jnp.concatenate([extra_v, v], axis=2)
        dtype = q.dtype
        attn = jnp.einsum('bhnd,bhmd->bhnm', q * scale, k).astype(jnp.float32)
        attn = jax.nn.softmax(attn, axis=-1).astype(dtype)
        out = jnp.einsum('bhnm,bhmd->bhnd', attn, v)
        out = out.transpose(0, 2, 1, 3).reshape(B, N, C)
        return out @ w_proj.T + b_proj

    def _L0_ffn_ref(hidden_states, router_w, actor_w1, actor_b1, actor_w2, actor_b2, gate_w, up_w, down_w):
        import jax, jax.numpy as jnp
        import numpy as np
        B, S, H, E, I, MAX_K, A_HID = (2, 256, 128, 8, 336, 6, 50)
        probs = jax.nn.softmax(jnp.einsum('bsh,eh->bse', hidden_states, router_w).astype(jnp.float32), axis=-1)
        a_h = jax.nn.gelu(jnp.einsum('bsh,ah->bsa', hidden_states, actor_w1) + actor_b1)
        actor_logits = jnp.clip(jnp.einsum('bsa,ka->bsk', a_h, actor_w2) + actor_b2, -30.0, 30.0)
        sampled_k = jnp.argmax(actor_logits, axis=-1) + 1
        order = jnp.argsort(-probs, axis=-1)
        rank = jnp.argsort(order, axis=-1)
        mask = rank < sampled_k[..., None]
        scores = jnp.where(mask, probs, 0.0).astype(hidden_states.dtype)
        out = jnp.zeros_like(hidden_states)
        for e in range(E):
            g = jnp.einsum('bsh,ih->bsi', hidden_states, gate_w[e])
            u = jnp.einsum('bsh,ih->bsi', hidden_states, up_w[e])
            y = jnp.einsum('bsi,hi->bsh', jax.nn.silu(g) * u, down_w[e])
            out = out + scores[..., e:e + 1] * y
        return out

    def _L1_xattn_ref(x, context, Wq, Wkv, null_kv, Wout, ln_scale, ln_bias):
        import jax, jax.numpy as jnp
        import numpy as np
        B, N, DIM = (8, 512, 128)
        M, CTX = (32, 256)
        HEADS, DH = (16, 64)
        INNER = HEADS * DH
        EPS = 1e-06

        def _split_heads(t):
            b, n, _ = t.shape
            return t.reshape(b, n, HEADS, DH).transpose(0, 2, 1, 3)
        scale = DH ** (-0.5)
        b = x.shape[0]
        q = _split_heads(jnp.einsum('bnd,df->bnf', x, Wq))
        kv = jnp.einsum('bmc,cf->bmf', context, Wkv)
        k, v = jnp.split(kv, 2, axis=-1)
        k, v = (_split_heads(k), _split_heads(v))
        nk = jnp.broadcast_to(null_kv[0], (b, HEADS, 1, DH))
        nv = jnp.broadcast_to(null_kv[1], (b, HEADS, 1, DH))
        k = jnp.concatenate((nk, k), axis=-2)
        v = jnp.concatenate((nv, v), axis=-2)
        q = q * scale
        sim = jnp.einsum('bhid,bhjd->bhij', q, k)
        attn = jax.nn.softmax(sim, axis=-1)
        out = jnp.einsum('bhij,bhjd->bhid', attn, v)
        out = out.transpose(0, 2, 1, 3).reshape(b, -1, INNER)
        out = jnp.einsum('bnf,fd->bnd', out, Wout)
        mu = jnp.mean(out, axis=-1, keepdims=True)
        var = jnp.var(out, axis=-1, keepdims=True)
        out = (out - mu) * jax.lax.rsqrt(var + EPS) * ln_scale + ln_bias
        return out

    def _L1_ffn_ref(hidden_states, norm_weight, router_w, sw1, sb1, sw2, sb2, ew1, eb1, ew2, eb2):
        import jax, jax.numpy as jnp
        import numpy as np
        D, H, O, E, TOPK = (128, 512, 128, 8, 2)
        B, S = (4, 128)
        b, s, d = hidden_states.shape
        var = jnp.mean(jnp.square(hidden_states), axis=-1, keepdims=True)
        normed = hidden_states * jax.lax.rsqrt(var + 1e-08) * norm_weight
        shared = jnp.maximum(normed @ sw1 + sb1, 0.0) @ sw2 + sb2
        flat = normed.reshape(-1, d)
        T = flat.shape[0]
        probs = jax.nn.sigmoid(flat @ router_w.T)
        scores, idx = jax.lax.top_k(probs, TOPK)
        w = scores / (jnp.sum(scores, axis=-1, keepdims=True) + 1e-06)
        comb = jnp.zeros((T, E), dtype=flat.dtype)
        comb = comb.at[jnp.arange(T)[:, None], idx].add(w)
        h = jnp.maximum(jnp.einsum('td,edh->teh', flat, ew1) + eb1[None, :, :], 0.0)
        eo = jnp.einsum('teh,eho->teo', h, ew2) + eb2[None, :, :]
        routed = jnp.einsum('teo,te->to', eo, comb)
        return shared + routed.reshape(b, s, -1)
    x = x + _L0_xattn_ref(_layernorm(x, axis=-1), ctx_2048, L0_xattn_w_qkv, L0_xattn_w_proj, L0_xattn_b_proj)
    x = x + _L0_ffn_ref(_layernorm(x, axis=-1), L0_ffn_router_w, L0_ffn_actor_w1, L0_ffn_actor_b1, L0_ffn_actor_w2, L0_ffn_actor_b2, L0_ffn_gate_w, L0_ffn_up_w, L0_ffn_down_w)
    x = x + _L1_xattn_ref(_layernorm(x, axis=-1), ctx_2048, L1_xattn_Wq, L1_xattn_Wkv, L1_xattn_null_kv, L1_xattn_Wout, L1_xattn_ln_scale, L1_xattn_ln_bias)
    x = x + _L1_ffn_ref(_layernorm(x, axis=-1), L1_ffn_norm_weight, L1_ffn_router_w, L1_ffn_sw1, L1_ffn_sb1, L1_ffn_sw2, L1_ffn_sb2, L1_ffn_ew1, L1_ffn_eb1, L1_ffn_ew2, L1_ffn_eb2)
    return x

_drawn_inputs = setup_inputs


def setup_inputs(seed=0):
    import zlib

    import numpy as np

    out = dict(_drawn_inputs(seed))
    spreads = {'L0_ffn_actor_b1': (0.0, 0.8),
     'L0_ffn_actor_b2': (0.0, 0.8),
     'L1_xattn_ln_scale': (1.0, 0.2),
     'L1_xattn_ln_bias': (0.0, 0.1),
     'L1_ffn_norm_weight': (1.0, 0.2),
     'L1_ffn_sb1': (0.0, 0.1),
     'L1_ffn_sb2': (0.0, 0.1),
     'L1_ffn_eb1': (0.0, 0.293),
     'L1_ffn_eb2': (0.0, 0.1)}
    factors = {'L0_ffn_router_w': 4.497,
     'L0_ffn_actor_w1': 8.0,
     'L0_ffn_actor_w2': 8.0,
     'L0_ffn_gate_w': 4.051,
     'L0_ffn_up_w': 4.065,
     'L0_ffn_down_w': 3.869}
    for name, (base, spread) in spreads.items():
        noise = np.random.default_rng([zlib.crc32(name.encode()), seed]).standard_normal(out[name].shape)
        drawn = base * np.exp(spread * noise) if base else spread * noise
        out[name] = jnp.asarray(drawn.astype(out[name].dtype))
    for name, factor in factors.items():
        out[name] = (out[name] * factor).astype(out[name].dtype)
    return out
```

```python
from contextlib import ExitStack, contextmanager

import numpy as np

import concourse.bass as bass
from concourse import mybir

F32 = mybir.dt.float32
F32R = mybir.dt.float32r
ALU = mybir.AluOpType
ACT = mybir.ActivationFunctionType
AX = mybir.AxisListType

P = 128
B, N, C = 64, 64, 128
UNITS = B * N // P
GROUP = 4
GROUPS = UNITS // GROUP
COLS = GROUP * P
H = 16
PAIRS = H // 2
D0, D1 = 8, 64
KEYS0 = 2 * N
KEYS1 = N + 1
VW = D0 + 1
E = 8
LN_EPS = 1e-5


@contextmanager
def stage(nc):
    with ExitStack() as ctx:
        taken = []
        ctx.sem = lambda name: taken.append(ctx.enter_context(nc.semaphore(name))) or taken[-1]
        with ExitStack() as blocks:
            ctx.block = lambda: blocks.enter_context(nc.Block())
            yield ctx
        with nc.Block() as block:
            @block.sync
            def _(sp):
                for s in taken:
                    sp.sem_clear(s)


class Mark:

    def __init__(self, ctx, nc, name, per=1):
        self.sem, self.per = ctx.sem(name), per

    def credit(self, eng):
        eng.sem_inc(self.sem, 2 * self.per)

    def at(self, u, j=None):
        return u * self.per + (2 * self.per + (self.per if j is None else j))


class At:

    def __init__(self, k, j, lag):
        m = j - lag
        self.u, self.half, self.slot = 2 * k + m, k + m // 2, m % 2


def pipeline(eng, units, depth, step):
    for t in range(depth):
        step(lambda lag, t=t: At(t // 2, t % 2, lag), lambda lag, t=t: t - lag >= 0)
    with eng.Fori(depth // 2, units // 2) as k:
        for j in range(2):
            step(lambda lag, j=j: At(k, j, lag), lambda lag: True)
    for t in range(units, units + depth):
        step(lambda lag, t=t: At(t // 2, t % 2, lag), lambda lag, t=t: t - lag < units)


def finish_stats(nc, ctx, tag, stats, mean, rstd, rms):
    var = ctx.enter_context(nc.sbuf_tensor(f"{tag}_var", [P, UNITS], F32))
    tmp = ctx.enter_context(nc.sbuf_tensor(f"{tag}_tmp", [P, 2, UNITS], F32))
    root = ctx.enter_context(nc.sbuf_tensor(f"{tag}_root", [P, 2, UNITS], F32))
    chain = ctx.sem(f"{tag}_stat_steps")
    rooted = ctx.sem(f"{tag}_rooted")
    asked = ctx.sem(f"{tag}_root_asked")
    ready = ctx.sem(f"{tag}_stats_ready")

    def vector(dve):
        n = [0]

        def link(ins):
            n[0] += 1
            ins.then_inc(chain, 1)
            dve.wait_ge(chain, n[0])

        even_mean, even_m2 = stats[:, :, 1], stats[:, :, 2]
        odd_mean, odd_m2 = stats[:, :, 4], stats[:, :, 5]
        link(dve.tensor_tensor(mean[:, :], even_mean, odd_mean, ALU.add))
        link(dve.tensor_scalar(mean[:, :], mean[:, :], 0.5, None, ALU.mult))
        link(dve.tensor_tensor(tmp[:, 0, :], even_mean, odd_mean, ALU.subtract))
        link(dve.tensor_tensor(tmp[:, 0, :], tmp[:, 0, :], tmp[:, 0, :], ALU.mult))
        link(dve.tensor_tensor(tmp[:, 1, :], even_m2, odd_m2, ALU.add))
        link(dve.tensor_scalar(tmp[:, 1, :], tmp[:, 1, :], 1.0 / C, None, ALU.mult))
        link(dve.scalar_tensor_tensor(out=var[:, :], in0=tmp[:, 0, :], scalar=0.25, in1=tmp[:, 1, :],
                                      op0=ALU.mult, op1=ALU.add))
        dve.tensor_scalar(tmp[:, 0, :], var[:, :], LN_EPS, None, ALU.add).then_inc(asked, 1)
        dve.wait_ge(rooted, 1)
        if not rms:
            dve.reciprocal(rstd[:, :], root[:, 0, :]).then_inc(ready, 1)
            return
        link(dve.reciprocal(rstd[:, :], root[:, 0, :]))
        link(dve.tensor_tensor(tmp[:, 1, :], rstd[:, :], rstd[:, :], ALU.mult))
        link(dve.tensor_tensor(tmp[:, 1, :], tmp[:, 1, :], var[:, :], ALU.mult))
        dve.tensor_scalar(tmp[:, 1, :], tmp[:, 1, :], 1e-8, None, ALU.add).then_inc(asked, 1)
        dve.wait_ge(rooted, 2)
        link(dve.reciprocal(root[:, 0, :], root[:, 1, :]))
        dve.tensor_tensor(rstd[:, :], rstd[:, :], root[:, 0, :], ALU.mult).then_inc(ready, 1)

    def scalar(act):
        for i in range(2 if rms else 1):
            act.wait_ge(asked, i + 1)
            act.activation(root[:, i, :], tmp[:, i, :], ACT.Sqrt).then_inc(rooted, 1)

    return vector, scalar, ready


def attention0(nc, x, stats, ident, headmask, x_in, w_qkvT, w_projT, b_proj, ctx_kT, ctx_v, consts):
    with stage(nc) as ctx:
        def sb(name, shape, dt=F32):
            return ctx.enter_context(nc.sbuf_tensor("a_" + name, shape, dt))

        def ps(name, shape):
            return ctx.enter_context(nc.psum_tensor("a_" + name, shape, F32))

        def sem(name):
            return ctx.sem("a_" + name)

        def mark(name, per=1):
            return Mark(ctx, nc, "a_" + name, per)

        wqkv = sb("wqkv", [P, 3, P])
        wproj = sb("wproj", [P, 2, P])
        bias_bc = sb("bias_bc", [P, C])
        mean = sb("mean", [P, UNITS])
        rstd = sb("rstd", [P, UNITS])
        xn = sb("xn", [P, 2, C])
        xnT = sb("xnT", [P, 2, P])
        qT = sb("qT", [P, 2, P])
        qx = sb("qx", [P, 2, 2, H, N])
        kT = sb("kT", [P, 2, 2, KEYS0])
        cv = sb("cv", [P, 2, C])
        vx = sb("vx", [P, 2, 2, H, VW])
        top = sb("top", [P, 2, PAIRS])
        prob = sb("prob", [P, 2, PAIRS, KEYS0])
        probT = sb("probT", [P, 2, PAIRS, P])
        recip = sb("recip", [P, 2, PAIRS])
        o = sb("o", [P, 2, PAIRS, D0])
        oT = sb("oT", [P, P])

        score_ps = ps("score_ps", [P, 2, PAIRS, KEYS0])
        probT_ps = ps("probT_ps", [P, PAIRS, P])
        in_ps = ps("in_ps", [P, 4, P])
        out_ps = ps("out_ps", [P, 512])
        o_ps = out_ps[:, 0:2 * PAIRS * 2 * VW].rearrange("p (b r c) -> p b r c", b=2, r=PAIRS)
        y_ps = out_ps[:, 384:512]

        loaded, x_loaded, first_stats, zeroed = sem("loaded"), sem("x_loaded"), sem("first_stats"), sem("zeroed")
        k_in = [sem(f"k_in{s}") for s in range(2)]
        v_in = [sem(f"v_in{s}") for s in range(2)]
        xn_done, biased = mark("xn_done"), mark("biased")
        xnT_ps_done, xnT_done = mark("xnT_ps_done"), mark("xnT_done")
        qkv_done, qkv_out = mark("qkv_done"), mark("qkv_out", 4)
        qx_done, cv_done = mark("qx_done"), mark("cv_done")
        scores_done, max_done, sub_done, exp_done = mark("scores", 2), mark("max", 2), mark("sub", 2), mark("exp", 2)
        probT_ps_done, probT_done = mark("probT_ps", 2), mark("probT", 4)
        pv_done, recip_done, o_done = mark("pv", 2), mark("recip", 4), mark("o", 4)
        oT_ps_done, oT_done, y_done, resid_done = mark("oT_ps"), mark("oT"), mark("y"), mark("resid")
        vec_stats, act_stats, stats_ready = finish_stats(nc, ctx, "a", stats, mean, rstd, False)

        DEPTH = 4
        block = ctx.block()

        @block.sync
        def _(sp):
            for s in range(4):
                n = UNITS // 4
                sp.dma_start(x[:, s * n:(s + 1) * n, :],
                             x_in[s * n * P:(s + 1) * n * P, :].rearrange("(u p) f -> p u f", p=P)).then_inc(x_loaded, 16)
            for dst, src in ((wqkv[:, :, :], w_qkvT), (wproj[:, :, :], w_projT), (bias_bc[:, :], b_proj),
                             (ident[:, :], consts["ident"]), (headmask[:, :], consts["headmask"])):
                sp.dma_start(dst, src).then_inc(loaded, 16)

            def step(at, on):
                if on(0):
                    a = at(0)
                    sp.wait_ge(scores_done.sem, scores_done.at(a.u - 2))
                    sp.dma_start(kT[:, a.slot, :, :].rearrange("p b k -> p (b k)")[:, N:3 * N],
                                 ctx_kT[:, bass.ds(a.u * P, P)]).then_inc(k_in[a.slot], 16)
                    sp.wait_ge(cv_done.sem, cv_done.at(a.u - 2))
                    sp.dma_start(cv[:, a.slot, :], ctx_v[:, bass.ds(a.u * P, P)]).then_inc(v_in[a.slot], 16)

            pipeline(sp, UNITS, DEPTH, step)

        @block.gpsimd
        def _(pool):
            for m in (biased, qx_done, cv_done):
                m.credit(pool)
            pool.memset(vx[:, :, :, :, :], 1.0).then_inc(zeroed, 1)
            pool.wait_ge(loaded, 5 * 16)
            pool.wait_ge(zeroed, 1)

            def step(at, on):
                if on(0):
                    a = at(0)
                    pool.wait_ge(xn_done.sem, xn_done.at(a.u))
                    xu = x[:, bass.ds(a.u, 1), :].rearrange("p a f -> p (a f)")
                    pool.tensor_tensor(xu, xu, bias_bc[:, :], ALU.add).then_inc(biased.sem, 1)
                if on(1):
                    a = at(1)
                    pool.wait_ge(qkv_out.sem, qkv_out.at(a.u, 1))
                    pool.wait_ge(scores_done.sem, scores_done.at(a.u - 2))
                    for b in range(2):
                        if b == 1:
                            pool.wait_ge(v_in[a.slot], a.half * 16 + 16)
                            pool.wait_ge(pv_done.sem, pv_done.at(a.u - 2))
                        last = pool.tensor_tensor(
                            qx[:, a.slot, b, :, :],
                            qT[:, a.slot, b * N:(b + 1) * N].unsqueeze(1).to_broadcast([P, H, N]),
                            headmask[:, :].unsqueeze(2).to_broadcast([P, H, N]), ALU.mult)
                    last.then_inc(qx_done.sem, 1)
                    for b in range(2):
                        last = pool.tensor_copy(vx[:, a.slot, b, :, 0:D0],
                                                cv[:, a.slot, :].rearrange("p (h d) -> p h d", h=H))
                    last.then_inc(cv_done.sem, 1)

            pipeline(pool, UNITS, DEPTH, step)

        @block.scalar
        def _(act):
            for m in (xnT_done, qkv_out, exp_done, probT_done, oT_done):
                m.credit(act)
            act_stats(act)

            def copy_probs(a, b):
                act.wait_ge(pv_done.sem, pv_done.at(a.u - 1, b + 1))
                act.wait_ge(probT_ps_done.sem, probT_ps_done.at(a.u, b + 1))
                for h in range(2):
                    act.activation(probT[:, b, 4 * h:4 * h + 4, :], probT_ps[:, 4 * h:4 * h + 4, :],
                                   ACT.Copy).then_inc(probT_done.sem, 1)

            def exps(a, b):
                act.wait_ge(sub_done.sem, sub_done.at(a.u, b + 1))
                act.activation(prob[:, b, :, :], prob[:, b, :, :], ACT.Exp).then_inc(exp_done.sem, 1)

            def step(at, on):
                if on(3):
                    copy_probs(at(3), 1)
                if on(2):
                    exps(at(2), 0)
                if on(1):
                    a = at(1)
                    act.wait_ge(qkv_done.sem, qkv_done.at(a.u))
                    act.wait_ge(qx_done.sem, qx_done.at(a.u - 2))
                    act.activation(qT[:, a.slot, :], in_ps[:, 1, :], ACT.Copy,
                                   scale=float(D0) ** -0.5).then_inc(qkv_out.sem, 1)
                    act.wait_ge(scores_done.sem, scores_done.at(a.u - 2))
                    own = kT[:, a.slot, :, :].rearrange("p b (h k) -> p (b h) k", k=N)
                    act.activation(own[:, 0:4:3, :], in_ps[:, 2, :].rearrange("p (b k) -> p b k", b=2),
                                   ACT.Copy).then_inc(qkv_out.sem, 1)
                    act.wait_ge(pv_done.sem, pv_done.at(a.u - 2))
                    act.wait_ge(cv_done.sem, cv_done.at(a.u))
                    for b in range(2):
                        r = slice(b * N, (b + 1) * N)
                        act.activation(vx[r, a.slot, b, :, 0:D0],
                                       in_ps[r, 3, :].rearrange("p (h d) -> p h d", h=H),
                                       ACT.Copy).then_inc(qkv_out.sem, 1)
                if on(3):
                    a = at(3)
                    act.wait_ge(oT_ps_done.sem, oT_ps_done.at(a.u))
                    act.wait_ge(y_done.sem, y_done.at(a.u - 1))
                    act.activation(oT[:, :], y_ps, ACT.Copy).then_inc(oT_done.sem, 1)
                if on(2):
                    copy_probs(at(2), 0)
                    exps(at(2), 1)
                if on(0):
                    a = at(0)
                    act.wait_ge(xnT_ps_done.sem, xnT_ps_done.at(a.u))
                    act.wait_ge(qkv_done.sem, qkv_done.at(a.u - 2))
                    act.activation(xnT[:, a.slot, :], in_ps[:, 0, :], ACT.Copy).then_inc(xnT_done.sem, 1)

            pipeline(act, UNITS, DEPTH, step)

        @block.tensor
        def _(pe):
            for m in (xnT_ps_done, qkv_done, scores_done, probT_ps_done, pv_done, oT_ps_done, y_done):
                m.credit(pe)
            pe.wait_ge(loaded, 5 * 16)

            def scores(a, b):
                if b == 0:
                    pe.wait_ge(qx_done.sem, qx_done.at(a.u))
                    pe.wait_ge(qkv_out.sem, qkv_out.at(a.u, 2))
                    pe.wait_ge(k_in[a.slot], a.half * 16 + 16)
                pe.wait_ge(sub_done.sem, sub_done.at(a.u - 1, b + 1))
                for r in range(PAIRS):
                    m = pe.matmul(score_ps[:, b, r, :],
                                  qx[:, a.slot, b, 2 * r:2 * r + 2, :].rearrange("p h q -> p (h q)"),
                                  kT[:, a.slot, b, :], start=True, stop=True)
                m.then_inc(scores_done.sem, 1)

            def turn_probs(a, b):
                pe.wait_ge(exp_done.sem, exp_done.at(a.u, b + 1))
                pe.wait_ge(probT_done.sem, probT_done.at(a.u - 1 + b, 2 * (2 - b)))
                for r in range(PAIRS):
                    m = pe.transpose(probT_ps[:, r, :], prob[:, b, r, :], ident[:, :])
                m.then_inc(probT_ps_done.sem, 1)

            def values(a, b):
                pe.wait_ge(probT_done.sem, probT_done.at(a.u, 2 * b + 2))
                if b == 0:
                    pe.wait_ge(cv_done.sem, cv_done.at(a.u))
                    pe.wait_ge(qkv_out.sem, qkv_out.at(a.u))
                    pe.wait_ge(resid_done.sem, resid_done.at(a.u - 1))
                else:
                    pe.wait_ge(o_done.sem, o_done.at(a.u, 2))
                for r in range(PAIRS):
                    m = pe.matmul(o_ps[:, b, r, :], probT[:, b, r, :],
                                  vx[:, a.slot, b, 2 * r:2 * r + 2, :].rearrange("p h c -> p (h c)"),
                                  start=True, stop=True)
                m.then_inc(pv_done.sem, 1)

            def step(at, on):
                if on(2):
                    scores(at(2), 0)
                if on(3):
                    turn_probs(at(3), 1)
                if on(1):
                    a = at(1)
                    pe.wait_ge(xnT_done.sem, xnT_done.at(a.u))
                    xu = xnT[:, a.slot, :]
                    pe.matmul(in_ps[:, 1, :], wqkv[:, 0, :], xu, start=True, stop=True)
                    pe.matmul(in_ps[:, 2, :], wqkv[:, 1, :], xu, start=True, stop=True)
                    pe.matmul(in_ps[:, 3, :], xu, wqkv[:, 2, :], start=True, stop=True).then_inc(qkv_done.sem, 1)
                if on(3):
                    values(at(3), 1)
                if on(2):
                    scores(at(2), 1)
                if on(3):
                    a = at(3)
                    pe.wait_ge(o_done.sem, o_done.at(a.u))
                    pe.transpose(y_ps, o[:, :, :, :].rearrange("p b r d -> p (b r d)"), ident[:, :]).then_inc(oT_ps_done.sem, 1)
                if on(2):
                    turn_probs(at(2), 0)
                if on(0):
                    a = at(0)
                    pe.wait_ge(xn_done.sem, xn_done.at(a.u))
                    pe.wait_ge(qkv_out.sem, qkv_out.at(a.u - 1))
                    pe.transpose(in_ps[:, 0, :], xn[:, a.slot, :], ident[:, :]).then_inc(xnT_ps_done.sem, 1)
                if on(3):
                    a = at(3)
                    pe.wait_ge(loaded, 5 * 16)
                    pe.wait_ge(oT_done.sem, oT_done.at(a.u))
                    for b in range(2):
                        for par in range(2):
                            m = pe.matmul(y_ps[b * N:(b + 1) * N, :], oT[b * N:(b + 1) * N, par * N:(par + 1) * N],
                                          wproj[b * N:(b + 1) * N, par, :], start=(par == 0), stop=(par == 1))
                    m.then_inc(y_done.sem, 1)
                if on(2):
                    values(at(2), 0)

            pipeline(pe, UNITS, DEPTH, step)

        @block.vector
        def _(dve):
            for m in (xn_done, max_done, sub_done, recip_done, o_done, resid_done):
                m.credit(dve)
            dve.wait_ge(x_loaded, 4 * 16)
            with dve.Fori(0, UNITS) as u:
                dve.bn_stats(stats[:, bass.ds(u, 1), :].rearrange("p a s -> p (a s)"),
                             x[:, bass.ds(u, 1), :].rearrange("p a f -> p (a f)")).then_inc(first_stats, 1)
            dve.wait_ge(first_stats, UNITS)
            vec_stats(dve)
            dve.wait_ge(stats_ready, 1)

            def shift(a, b):
                dve.wait_ge(scores_done.sem, scores_done.at(a.u, b + 1))
                dve.tensor_reduce(top[:, b, :], score_ps[:, b, :, :], AX.X, ALU.max).then_inc(max_done.sem, 1)
                dve.wait_ge(max_done.sem, max_done.at(a.u, b + 1))
                dve.wait_ge(probT_ps_done.sem, probT_ps_done.at(a.u - 1, b + 1))
                dve.tensor_tensor(prob[:, b, :, :], score_ps[:, b, :, :],
                                  top[:, b, :].unsqueeze(2).to_broadcast([P, PAIRS, KEYS0]),
                                  ALU.subtract).then_inc(sub_done.sem, 1)

            def normalise(a, b):
                dve.wait_ge(pv_done.sem, pv_done.at(a.u, b + 1))
                if b == 0:
                    dve.wait_ge(oT_ps_done.sem, oT_ps_done.at(a.u - 1))
                for par in range(2):
                    r = slice(par * N, (par + 1) * N)
                    dve.reciprocal(recip[r, b, :], o_ps[r, b, :, par * VW + D0]).then_inc(recip_done.sem, 1)
                dve.wait_ge(recip_done.sem, recip_done.at(a.u, 2 * b + 2))
                for par in range(2):
                    r = slice(par * N, (par + 1) * N)
                    dve.tensor_tensor(o[r, b, :, :], o_ps[r, b, :, par * VW:par * VW + D0],
                                      recip[r, b, :].unsqueeze(2).to_broadcast([N, PAIRS, D0]),
                                      ALU.mult).then_inc(o_done.sem, 1)

            def step(at, on):
                if on(0):
                    a = at(0)
                    dve.wait_ge(xnT_ps_done.sem, xnT_ps_done.at(a.u - 2))
                    dve.tensor_scalar(xn[:, a.slot, :], x[:, bass.ds(a.u, 1), :].rearrange("p a f -> p (a f)"),
                                      mean[:, bass.ds(a.u, 1)], rstd[:, bass.ds(a.u, 1)],
                                      ALU.subtract, ALU.mult).then_inc(xn_done.sem, 1)
                if on(2):
                    shift(at(2), 0)
                if on(3):
                    normalise(at(3), 1)
                if on(2):
                    shift(at(2), 1)
                if on(3):
                    a = at(3)
                    xu = x[:, bass.ds(a.u, 1), :].rearrange("p a f -> p (a f)")
                    dve.wait_ge(y_done.sem, y_done.at(a.u))
                    dve.wait_ge(biased.sem, biased.at(a.u))
                    dve.tensor_tensor(xu, y_ps, xu, ALU.add).then_inc(resid_done.sem, 1)
                    dve.wait_ge(resid_done.sem, resid_done.at(a.u))
                    dve.bn_stats(stats[:, bass.ds(a.u, 1), :].rearrange("p a s -> p (a s)"), xu)
                if on(2):
                    normalise(at(2), 0)

            pipeline(dve, UNITS, DEPTH, step)


def split_weights(nc, ctx, tag, jobs):
    STAGE, SLOTS = 1024, 3
    raw = ctx.enter_context(nc.sbuf_tensor(f"{tag}_raw", [P, SLOTS, STAGE], F32))
    landed = [ctx.sem(f"{tag}_w_landed{s}") for s in range(SLOTS)]
    hi_made = ctx.sem(f"{tag}_w_hi")
    split = ctx.sem(f"{tag}_w_split")

    def sync(sp):
        for i, (hi, lo, src) in enumerate(jobs):
            rows, n = src.shape
            if i >= SLOTS:
                sp.wait_ge(split, i - SLOTS + 1)
            sp.dma_start(raw[0:rows, i % SLOTS, 0:n], src).then_inc(landed[i % SLOTS], 16)

    def scalar(act):
        for i, (hi, lo, src) in enumerate(jobs):
            rows, n = src.shape
            act.wait_ge(landed[i % SLOTS], 16 * (i // SLOTS + 1))
            act.activation(hi, raw[0:rows, i % SLOTS, 0:n], ACT.Copy).then_inc(hi_made, 1)

    def rest(eng):
        for i, (hi, lo, src) in enumerate(jobs):
            rows, n = src.shape
            eng.wait_ge(hi_made, i + 1)
            eng.tensor_tensor(lo, raw[0:rows, i % SLOTS, 0:n], hi.bitcast(F32), ALU.subtract).then_inc(split, 1)

    return sync, scalar, rest, split


def pieces(hi, lo, src, most=1024):
    n = src.shape[1]
    return [(hi[:, i:min(i + most, n)], lo[:, i:min(i + most, n)], src[:, i:min(i + most, n)])
            for i in range(0, n, most)]


def experts(nc, x, stats, ident, a, shared, out):
    tag = "d_" if shared else "b_"
    CH = 4 if shared else 3
    R = 512 // CH if shared else 336 // CH
    NE = E + 1 if shared else E
    FIRST = NE - E
    S = NE * CH
    MATS = 1 if shared else 2
    ZS = 4 // MATS
    LAG = 3
    HS = 4
    AH = 50
    KMAX = 6
    hook = {name: p * S // 24 for name, p in dict(xT=1, router=5, hidden=8, logits=11, scT=16, finish=20).items()}

    with stage(nc) as ctx:
        def sb(name, shape, dt=F32):
            return ctx.enter_context(nc.sbuf_tensor(tag + name, shape, dt))

        def ps(name, shape):
            return ctx.enter_context(nc.psum_tensor(tag + name, shape, F32))

        def sem(name):
            return ctx.sem(tag + name)

        def mark(name, per=1):
            return Mark(ctx, nc, tag + name, per)

        w_hi, w_lo = (sb(f"w_{n}", [P, MATS, S, R], F32R) for n in ("hi", "lo"))
        wd_hi, wd_lo = (sb(f"wd_{n}", [P, S, C], F32R) for n in ("hi", "lo"))
        rw_hi, rw_lo = (sb(f"rw_{n}", [P, E], F32R) for n in ("hi", "lo"))
        sel_hi, sel_lo = (sb(f"sel_{n}", [P, E, P], F32R) for n in ("hi", "lo"))
        before = sb("before", [P, E, E])
        mean, rstd = sb("mean", [P, UNITS]), sb("rstd", [P, UNITS])
        xn = sb("xn", [P, GROUP, C])
        xf = sb("xf", [P, COLS])
        x_hi, x_lo = (sb(f"x_{n}", [P, 2, COLS], F32R) for n in ("hi", "lo"))
        h = sb("h", [P, 2, COLS])
        h_hi, h_lo = (sb(f"h_{n}", [P, HS, COLS], F32R) for n in ("hi", "lo"))
        cB = sb("cB", [P, 2, COLS])
        part = sb("part", [P, 2, COLS])
        acc = sb("acc", [P, 2, COLS])
        probs = sb("probs", [P, GROUP, E])
        red = sb("red", [P, GROUP])
        inv = sb("inv", [P, GROUP])
        gt, ge = sb("gt", [P, GROUP, E, E]), sb("ge", [P, GROUP, E, E])
        rank = sb("rank", [P, GROUP, E])
        mask = sb("mask", [P, GROUP, E])
        score = sb("score", [P, GROUP, E])
        score_hi = sb("score_hi", [P, GROUP, E], F32R)
        split_score = sb("split_score", [P, GROUP, P])
        scT = sb("scT", [P, 2, COLS], F32R)
        if shared:
            norm_w = sb("norm_w", [P, 1])
            b1, b2 = sb("b1", [P, S]), sb("b2", [P, NE])
            small = ((norm_w[:, :], a["d_norm"]), (b1[:, :], a["d_b1"]), (b2[:, :], a["d_b2"]))
        else:
            sg = sb("sg", [P, 2, COLS])
            aw_hi, aw_lo = (sb(f"aw_{n}", [P, P], F32R) for n in ("hi", "lo"))
            ab1, aw2, ab2 = sb("ab1", [AH, 1]), sb("aw2", [AH, KMAX]), sb("ab2", [P, KMAX])
            kcode = sb("kcode", [P, KMAX])
            ah = sb("ah", [AH, COLS])
            al, amax = sb("al", [P, GROUP, KMAX]), sb("amax", [P, GROUP])
            small = ((ab1[:, :], a["b_ab1"]), (aw2[:, :], a["b_aw2T"]), (ab2[:, :], a["b_ab2"]),
                     (kcode[:, :], a["kcode"]))
        small += ((before[:, :, :], a["before"]),)

        z_ps = ps("z", [P, MATS, ZS, COLS])
        y_ps = ps("y", [P, 2, COLS])
        t_ps = ps("t", [P, COLS])
        c_ps = ps("c", [P, COLS])

        loaded, zeroed = sem("loaded"), sem("zeroed")
        xn_done, xT_ps_done, xf_done, xhi_done, xlo_done = (mark(n) for n in ("xn", "xT_ps", "xf", "xhi", "xlo"))
        router_done, soft_done = mark("router"), mark("soft")
        hidden_done, gelu_done, logits_done, al_done = (mark(n) for n in ("hidden", "gelu", "logits", "al"))
        exp_done, scored, scT_ps_done, scT_done = (mark(n) for n in ("exp", "scored", "scT_ps", "scT"))
        hi_scored, max_done = mark("hi_scored"), mark("max")
        STEPS_R = 11 if shared else 16
        r_step = mark("r_step", STEPS_R)
        z_done, sg_done, h_done, hi_done = (mark(n, S) for n in ("z", "sg", "h", "hi"))
        lo_pool, lo_dve = mark("lo_pool", S // 2), mark("lo_dve", S // 2)
        down_done = mark("down", S)
        c_ps_done, cB_done = mark("c_ps", E), mark("cB", E)
        weighed, added = mark("weighed", NE), mark("added", NE - 1)
        fin_ps_done, resid_done = mark("fin_ps"), mark("resid")
        stored = sem("stored")
        vec_stats, act_stats, stats_ready = finish_stats(nc, ctx, tag + "s", stats, mean, rstd, shared)

        jobs = pieces(rw_hi[:, :], rw_lo[:, :], a[tag + "rw"])
        jobs += pieces(sel_hi[:, :, :].rearrange("p e c -> p (e c)"), sel_lo[:, :, :].rearrange("p e c -> p (e c)"), a["sel"])
        if not shared:
            jobs += pieces(aw_hi[:, :], aw_lo[:, :], a["b_aw1T"])
        PREP_JOBS = len(jobs)
        flat = lambda t, m: t[:, m, :, :].rearrange("p s r -> p (s r)")
        down_flat = lambda t: t[0:R, :, :].rearrange("p s c -> p (s c)")
        for q in range(3):
            lo_c, hi_c = q * S * R // 3, (q + 1) * S * R // 3
            for m in range(MATS):
                jobs += pieces(flat(w_hi, m)[:, lo_c:hi_c], flat(w_lo, m)[:, lo_c:hi_c], a[tag + "w"][m][:, lo_c:hi_c])
            lo_c, hi_c = q * S * C // 3, (q + 1) * S * C // 3
            jobs += pieces(down_flat(wd_hi)[:, lo_c:hi_c], down_flat(wd_lo)[:, lo_c:hi_c], a[tag + "wd"][:, lo_c:hi_c])
        load_w, hi_w, lo_w, split = split_weights(nc, ctx, tag + "sw", jobs)

        DEPTH = 2
        block = ctx.block()

        def y_slot(g, e):
            return (g.slot * NE + e) % 2

        def behind(at, on, s, lag):
            n = 1 if s >= lag else 2
            return (at(n), (s - lag) % S) if on(n) else None

        def wait_lo(eng, g, s):
            m = lo_dve if s % 2 else lo_pool
            eng.wait_ge(m.sem, m.at(g.u, s // 2 + 1))

        def unit_tiles(g):
            return x[:, bass.ds(g.u * GROUP, GROUP), :]

        @block.sync
        def _(sp):
            for dst, src in small:
                sp.dma_start(dst, src).then_inc(loaded, 16)
            load_w(sp)
            if shared:
                def step(at, on):
                    if on(0):
                        g = at(0)
                        sp.wait_ge(resid_done.sem, resid_done.at(g.u))
                        sp.dma_start(out[bass.ds(g.u * COLS, COLS), :].rearrange("(u p) f -> p u f", p=P),
                                     unit_tiles(g)).then_inc(stored, 16)
                pipeline(sp, GROUPS, 0, step)
                sp.wait_ge(stored, 16 * GROUPS)

        @block.gpsimd
        def _(pool):
            for m in (lo_pool, added):
                m.credit(pool)
            pool.memset(split_score[:, :, :], 0.0).then_inc(zeroed, 1)
            lo_w(pool)

            def step(at, on):
                for s in range(S):
                    if s % 2 == 0 and on(1):
                        g = at(1)
                        pool.wait_ge(hi_done.sem, hi_done.at(g.u, s + 1))
                        pool.wait_ge(down_done.sem, down_done.at(g.u, s + 1 - HS))
                        pool.tensor_tensor(h_lo[0:R, s % HS, :], h[0:R, s % 2, :],
                                           h_hi[0:R, s % HS, :].bitcast(F32), ALU.subtract).then_inc(lo_pool.sem, 1)
                    found = behind(at, on, s, LAG + CH)
                    if found and found[1] % CH == 0 and found[1]:
                        g, e = found[0], found[1] // CH
                        pool.wait_ge(added.sem, added.at(g.u, e - 1))
                        pool.wait_ge(weighed.sem, weighed.at(g.u, e + 1))
                        pool.tensor_tensor(acc[:, g.slot, :], acc[:, g.slot, :], part[:, y_slot(g, e), :],
                                           ALU.add).then_inc(added.sem, 1)

            pipeline(pool, GROUPS, DEPTH, step)

        @block.scalar
        def _(act):
            for m in (xf_done, xhi_done, gelu_done, exp_done, hi_scored, scT_done, sg_done, hi_done, cB_done):
                m.credit(act)
            act_stats(act)
            hi_w(act)

            def step(at, on):
                for s in range(S):
                    prev = behind(at, on, s, 1)
                    if prev:
                        g, q = prev
                        act.wait_ge(h_done.sem, h_done.at(g.u, q + 1))
                        act.wait_ge(down_done.sem, down_done.at(g.u, q + 1 - HS))
                        act.activation(h_hi[0:R, q % HS, :], h[0:R, q % 2, :], ACT.Copy).then_inc(hi_done.sem, 1)
                    if on(1) and not shared:
                        g = at(1)
                        act.wait_ge(z_done.sem, z_done.at(g.u, s + 1))
                        act.wait_ge(h_done.sem, h_done.at(g.u, s - 1))
                        act.activation(sg[0:R, s % 2, :], z_ps[0:R, 0, s % ZS, :], ACT.Silu).then_inc(sg_done.sem, 1)
                    if on(1) and s % CH == 0 and s // CH >= FIRST:
                        g, r = at(1), s // CH - FIRST
                        act.wait_ge(c_ps_done.sem, c_ps_done.at(g.u, r + 1))
                        act.wait_ge(weighed.sem, weighed.at(g.u, r + FIRST - 1))
                        act.activation(cB[:, r % 2, :], c_ps[:, :], ACT.Copy).then_inc(cB_done.sem, 1)
                    if not on(0):
                        continue
                    g = at(0)
                    if s == hook["xT"]:
                        act.wait_ge(xT_ps_done.sem, xT_ps_done.at(g.u))
                        act.wait_ge(xlo_done.sem, xlo_done.at(g.u - 1))
                        act.activation(xf[:, :], t_ps[:, :], ACT.Copy,
                                       scale=norm_w[:, 0:1] if shared else 1.0).then_inc(xf_done.sem, 1)
                        act.wait_ge(xf_done.sem, xf_done.at(g.u))
                        act.wait_ge(z_done.sem, z_done.at(g.u - 2))
                        act.activation(x_hi[:, g.slot, :], xf[:, :], ACT.Copy).then_inc(xhi_done.sem, 1)
                    if s == hook["router"] and shared:
                        act.wait_ge(router_done.sem, router_done.at(g.u))
                        act.wait_ge(scored.sem, scored.at(g.u - 1))
                        act.activation(probs[:, :, :], t_ps[:, 0:GROUP * E].rearrange("p (u e) -> p u e", e=E),
                                       ACT.Sigmoid).then_inc(exp_done.sem, 1)
                    if s == hook["hidden"] and not shared:
                        act.wait_ge(hidden_done.sem, hidden_done.at(g.u))
                        act.wait_ge(logits_done.sem, logits_done.at(g.u - 1))
                        act.activation(ah[:, :], t_ps[0:AH, :], ACT.Gelu_apprx_tanh,
                                       bias=ab1[:, 0:1]).then_inc(gelu_done.sem, 1)
                        act.wait_ge(soft_done.sem, soft_done.at(g.u))
                        act.activation(probs[:, :, :], probs[:, :, :], ACT.Exp).then_inc(exp_done.sem, 1)
                    if s == hook["scT"] - 1:
                        act.wait_ge(r_step.sem, r_step.at(g.u))
                        act.activation(score_hi[:, :, :], score[:, :, :], ACT.Copy).then_inc(hi_scored.sem, 1)
                    if s == hook["scT"]:
                        act.wait_ge(scT_ps_done.sem, scT_ps_done.at(g.u))
                        act.wait_ge(c_ps_done.sem, c_ps_done.at(g.u - 2))
                        act.activation(scT[:, g.slot, :], t_ps[:, :], ACT.Copy).then_inc(scT_done.sem, 1)

            pipeline(act, GROUPS, DEPTH, step)

        @block.tensor
        def _(pe):
            for m in (xT_ps_done, router_done, hidden_done, logits_done, scT_ps_done, z_done, down_done, c_ps_done,
                      fin_ps_done):
                m.credit(pe)
            pe.wait_ge(loaded, 16 * len(small))

            def three(dst, hi, lo, m_hi, m_lo, start=True, stop=True):
                pe.matmul(dst, hi, m_hi, start=start, stop=False)
                pe.matmul(dst, hi, m_lo, start=False, stop=False)
                return pe.matmul(dst, lo, m_hi, start=False, stop=stop)

            def up(g, s):
                pe.wait_ge(h_done.sem, h_done.at(g.u, s + 1 - ZS))
                for m in range(MATS):
                    last = three(z_ps[0:R, m, s % ZS, :], w_hi[:, m, s, :], w_lo[:, m, s, :],
                                 x_hi[:, g.slot, :], x_lo[:, g.slot, :])
                last.then_inc(z_done.sem, 1)

            def down(g, s):
                e = s // CH
                if s % CH == 0:
                    pe.wait_ge(weighed.sem, weighed.at(g.u, e - 1))
                wait_lo(pe, g, s)
                three(y_ps[:, y_slot(g, e), :], wd_hi[0:R, s, :], wd_lo[0:R, s, :], h_hi[0:R, s % HS, :],
                      h_lo[0:R, s % HS, :], s % CH == 0, s % CH == CH - 1).then_inc(down_done.sem, 1)

            def prepare(g, s):
                x_of = lambda t, i: t[:, g.slot, i * P:(i + 1) * P]
                if s == hook["xT"]:
                    pe.wait_ge(xn_done.sem, xn_done.at(g.u))
                    pe.wait_ge(resid_done.sem, resid_done.at(g.u - 3))
                    pe.wait_ge(scT_done.sem, scT_done.at(g.u - 1))
                    for i in range(GROUP):
                        m = pe.transpose(t_ps[:, i * P:(i + 1) * P], xn[:, i, :], ident[:, :])
                    m.then_inc(xT_ps_done.sem, 1)
                if s == hook["router"]:
                    pe.wait_ge(split, PREP_JOBS)
                    pe.wait_ge(xlo_done.sem, xlo_done.at(g.u))
                    for i in range(GROUP):
                        m = three(t_ps[:, i * E:(i + 1) * E], x_of(x_hi, i), x_of(x_lo, i), rw_hi[:, :], rw_lo[:, :])
                    m.then_inc(router_done.sem, 1)
                if s == hook["hidden"] and not shared:
                    pe.wait_ge(soft_done.sem, soft_done.at(g.u))
                    three(t_ps[:, :], aw_hi[:, :], aw_lo[:, :], x_hi[:, g.slot, :], x_lo[:, g.slot, :]
                          ).then_inc(hidden_done.sem, 1)
                if s == hook["logits"] and not shared:
                    pe.wait_ge(gelu_done.sem, gelu_done.at(g.u))
                    for i in range(GROUP):
                        m = pe.matmul(t_ps[:, i * KMAX:(i + 1) * KMAX], ah[:, i * P:(i + 1) * P], aw2[:, :],
                                      start=True, stop=True)
                    m.then_inc(logits_done.sem, 1)
                if s == hook["scT"]:
                    pe.wait_ge(scored.sem, scored.at(g.u))
                    for i in range(GROUP):
                        m = pe.transpose(t_ps[:, i * P:(i + 1) * P], split_score[:, i, :], ident[:, :])
                    m.then_inc(scT_ps_done.sem, 1)

            def step(at, on):
                for s in range(S):
                    if on(0):
                        prepare(at(0), s)
                    if on(2) and s == hook["finish"]:
                        g = at(2)
                        pe.wait_ge(added.sem, added.at(g.u))
                        pe.wait_ge(scT_done.sem, scT_done.at(g.u + 2) if on(0) else scT_done.at(GROUPS - 1))
                        for i in range(GROUP):
                            m = pe.transpose(t_ps[:, i * P:(i + 1) * P], acc[:, g.slot, i * P:(i + 1) * P], ident[:, :])
                        m.then_inc(fin_ps_done.sem, 1)
                    if on(1):
                        g = at(1)
                        if s % CH == 0 and s // CH >= FIRST:
                            r = s // CH - FIRST
                            pe.wait_ge(scT_done.sem, scT_done.at(g.u))
                            pe.wait_ge(cB_done.sem, cB_done.at(g.u, r))
                            pe.matmul(c_ps[:, :], sel_hi[:, r, :], scT[:, g.slot, :], start=True, stop=True
                                      ).then_inc(c_ps_done.sem, 1)
                        if s % (S // 3) == 0:
                            pe.wait_ge(split, PREP_JOBS + (len(jobs) - PREP_JOBS) // 3 * (s // (S // 3) + 1))
                        up(g, s)
                    found = behind(at, on, s, LAG)
                    if found:
                        down(*found)

            pipeline(pe, GROUPS, DEPTH, step)

        @block.vector
        def _(dve):
            for m in (xn_done, xlo_done, soft_done, max_done, al_done, scored, r_step, h_done, lo_dve, weighed, resid_done):
                m.credit(dve)
            vec_stats(dve)
            dve.wait_ge(stats_ready, 1)
            dve.wait_ge(loaded, 16 * len(small))
            dve.wait_ge(zeroed, 1)

            def route(g, n):
                count = [route.done if n else 0]

                def link(ins):
                    count[0] += 1
                    ins.then_inc(r_step.sem, 1)
                    dve.wait_ge(r_step.sem, r_step.at(g.u, count[0]))

                wide = lambda t: t.unsqueeze(2).to_broadcast([P, GROUP, E])
                by_j = probs[:, :, :].unsqueeze(2).to_broadcast([P, GROUP, E, E])
                by_e = probs[:, :, :].unsqueeze(3).to_broadcast([P, GROUP, E, E])
                first = before[:, :, :].unsqueeze(1).to_broadcast([P, GROUP, E, E])
                if n == 0:
                    dve.wait_ge(exp_done.sem, exp_done.at(g.u))
                    if not shared:
                        link(dve.tensor_reduce(red[:, :], probs[:, :, :], AX.X, ALU.add))
                        link(dve.reciprocal(inv[:, :], red[:, :]))
                        link(dve.tensor_tensor(probs[:, :, :], probs[:, :, :], wide(inv[:, :]), ALU.mult))
                    link(dve.tensor_tensor(ge[:, :, :, :], by_j, by_e, ALU.is_ge))
                    link(dve.tensor_tensor(ge[:, :, :, :], ge[:, :, :, :], first, ALU.mult))
                    link(dve.tensor_tensor(gt[:, :, :, :], by_j, by_e, ALU.is_gt))
                    link(dve.tensor_tensor(gt[:, :, :, :], gt[:, :, :, :], ge[:, :, :, :], ALU.max))
                    link(dve.tensor_reduce(rank[:, :, :], gt[:, :, :, :], AX.X, ALU.add))
                    if shared:
                        link(dve.tensor_scalar(mask[:, :, :], rank[:, :, :], 2.0, None, ALU.is_lt))
                        link(dve.tensor_tensor(mask[:, :, :], mask[:, :, :], probs[:, :, :], ALU.mult))
                        link(dve.tensor_reduce(red[:, :], mask[:, :, :], AX.X, ALU.add))
                        link(dve.tensor_scalar(red[:, :], red[:, :], 1e-6, None, ALU.add))
                    route.done = count[0]
                    return
                if shared:
                    link(dve.reciprocal(inv[:, :], red[:, :]))
                    dve.tensor_tensor(score[:, :, :], mask[:, :, :], wide(inv[:, :]), ALU.mult).then_inc(r_step.sem, 1)
                else:
                    wide_k = lambda t: t.unsqueeze(2).to_broadcast([P, GROUP, KMAX])
                    over = lambda t: t.unsqueeze(1).to_broadcast([P, GROUP, KMAX])
                    dve.wait_ge(logits_done.sem, logits_done.at(g.u))
                    dve.tensor_tensor(al[:, :, :], t_ps[:, 0:GROUP * KMAX].rearrange("p (u k) -> p u k", k=KMAX),
                                      over(ab2[:, :]), ALU.add).then_inc(al_done.sem, 1)
                    dve.wait_ge(al_done.sem, al_done.at(g.u))
                    link(dve.tensor_scalar(al[:, :, :], al[:, :, :], -30.0, 30.0, ALU.max, ALU.min))
                    link(dve.tensor_reduce(amax[:, :], al[:, :, :], AX.X, ALU.max))
                    link(dve.tensor_tensor(al[:, :, :], al[:, :, :], wide_k(amax[:, :]), ALU.is_equal))
                    link(dve.tensor_tensor(al[:, :, :], al[:, :, :], over(kcode[:, :]), ALU.mult))
                    link(dve.tensor_reduce(amax[:, :], al[:, :, :], AX.X, ALU.min))
                    link(dve.tensor_scalar(rank[:, :, :], rank[:, :, :], -100.0, None, ALU.add))
                    link(dve.tensor_tensor(mask[:, :, :], rank[:, :, :], wide(amax[:, :]), ALU.is_lt))
                    dve.tensor_tensor(score[:, :, :], mask[:, :, :], probs[:, :, :], ALU.mult).then_inc(r_step.sem, 1)
                assert count[0] + 1 == STEPS_R, count

            def step(at, on):
                for s in range(S):
                    if on(1):
                        g = at(1)
                        dve.wait_ge(hi_done.sem, hi_done.at(g.u, s - 1))
                        wait_lo(dve, g, s - 2)
                        if shared:
                            dve.wait_ge(z_done.sem, z_done.at(g.u, s + 1))
                            dve.tensor_scalar(h[:, s % 2, :], z_ps[:, 0, s % ZS, :], b1[:, s:s + 1], 0.0,
                                              ALU.add, ALU.max).then_inc(h_done.sem, 1)
                        else:
                            dve.wait_ge(sg_done.sem, sg_done.at(g.u, s + 1))
                            dve.tensor_tensor(h[0:R, s % 2, :], z_ps[0:R, 1, s % ZS, :], sg[0:R, s % 2, :],
                                              ALU.mult).then_inc(h_done.sem, 1)
                    prev = behind(at, on, s, 1)
                    if prev and prev[1] % 2:
                        g, q = prev
                        dve.wait_ge(hi_done.sem, hi_done.at(g.u, q + 1))
                        dve.wait_ge(down_done.sem, down_done.at(g.u, q + 1 - HS))
                        dve.tensor_tensor(h_lo[0:R, q % HS, :], h[0:R, q % 2, :],
                                          h_hi[0:R, q % HS, :].bitcast(F32), ALU.subtract).then_inc(lo_dve.sem, 1)
                    found = behind(at, on, s, LAG)
                    if found and found[1] % CH == CH - 1:
                        g, e = found[0], found[1] // CH
                        yy = y_ps[:, y_slot(g, e), :]
                        dve.wait_ge(down_done.sem, down_done.at(g.u, found[1] + 1))
                        if e >= FIRST:
                            dve.wait_ge(cB_done.sem, cB_done.at(g.u, e - FIRST + 1))
                        if e == 0:
                            dve.wait_ge(fin_ps_done.sem, fin_ps_done.at(g.u - 2))
                            to = acc[:, g.slot, :]
                        else:
                            dve.wait_ge(added.sem, added.at(g.u, max(e - 2, 0)))
                            to = part[:, y_slot(g, e), :]
                        if not shared:
                            m = dve.tensor_tensor(to, yy, cB[:, e % 2, :], ALU.mult)
                        elif e == 0:
                            m = dve.tensor_scalar(to, yy, b2[:, 0:1], None, ALU.add)
                        else:
                            m = dve.scalar_tensor_tensor(out=to, in0=yy, scalar=b2[:, e:e + 1],
                                                         in1=cB[:, (e - FIRST) % 2, :], op0=ALU.add, op1=ALU.mult)
                        m.then_inc(weighed.sem, 1)
                    if on(2) and s == hook["finish"]:
                        g = at(2)
                        dve.wait_ge(fin_ps_done.sem, fin_ps_done.at(g.u))
                        tiles = unit_tiles(g)
                        dve.tensor_tensor(tiles, t_ps[:, :].rearrange("p (u f) -> p u f", f=C), tiles,
                                          ALU.add).then_inc(resid_done.sem, 1)
                        if not shared:
                            dve.wait_ge(resid_done.sem, resid_done.at(g.u))
                            for i in range(GROUP):
                                dve.bn_stats(stats[:, bass.ds(g.u * GROUP + i, 1), :].rearrange("p a s -> p (a s)"),
                                             x[:, bass.ds(g.u * GROUP + i, 1), :].rearrange("p a f -> p (a f)"))
                    if not on(0):
                        continue
                    g = at(0)
                    if s == 0:
                        dve.wait_ge(xT_ps_done.sem, xT_ps_done.at(g.u - 1))
                        for i in range(GROUP):
                            u = g.u * GROUP + i
                            m = dve.tensor_scalar(xn[:, i, :], x[:, bass.ds(u, 1), :].rearrange("p a f -> p (a f)"),
                                                  mean[:, bass.ds(u, 1)], rstd[:, bass.ds(u, 1)],
                                                  ALU.subtract, ALU.mult)
                        m.then_inc(xn_done.sem, 1)
                    if s == hook["xT"]:
                        dve.wait_ge(xhi_done.sem, xhi_done.at(g.u))
                        dve.wait_ge(z_done.sem, z_done.at(g.u - 2))
                        dve.tensor_tensor(x_lo[:, g.slot, :], xf[:, :], x_hi[:, g.slot, :].bitcast(F32),
                                          ALU.subtract).then_inc(xlo_done.sem, 1)
                    if s == hook["router"] and not shared:
                        logit = t_ps[:, 0:GROUP * E].rearrange("p (u e) -> p u e", e=E)
                        dve.wait_ge(router_done.sem, router_done.at(g.u))
                        dve.tensor_reduce(red[:, :], logit, AX.X, ALU.max).then_inc(max_done.sem, 1)
                        dve.wait_ge(max_done.sem, max_done.at(g.u))
                        dve.tensor_tensor(probs[:, :, :], logit, red[:, :].unsqueeze(2).to_broadcast([P, GROUP, E]),
                                          ALU.subtract).then_inc(soft_done.sem, 1)
                    if s == hook["hidden"]:
                        route(g, 0)
                    if s == hook["logits"]:
                        route(g, 1)
                    if s == hook["scT"] - 1:
                        dve.wait_ge(hi_scored.sem, hi_scored.at(g.u))
                        dve.wait_ge(scT_ps_done.sem, scT_ps_done.at(g.u - 1))
                        hi = score_hi[:, :, :].bitcast(F32)
                        dve.tensor_copy(split_score[:, :, 0:E], hi)
                        dve.tensor_tensor(split_score[:, :, E:2 * E], score[:, :, :], hi, ALU.subtract
                                          ).then_inc(scored.sem, 1)

            pipeline(dve, GROUPS, DEPTH, step)


def attention1(nc, x, stats, ident, a):
    with stage(nc) as ctx:
        def sb(name, shape, dt=F32):
            return ctx.enter_context(nc.sbuf_tensor("c_" + name, shape, dt))

        def ps(name, shape):
            return ctx.enter_context(nc.psum_tensor("c_" + name, shape, F32))

        def sem(name):
            return ctx.sem("c_" + name)

        def mark(name, per=1):
            return Mark(ctx, nc, "c_" + name, per)

        def split(name, shape):
            return sb(name + "_hi", shape, F32R), sb(name + "_lo", shape, F32R)

        CC = 2
        HALF = PAIRS // 2
        INNER = H * D1
        wq_hi, wq_lo = split("wq", [P, PAIRS, P])
        wk_hi, wk_lo = split("wk", [P, CC, PAIRS, P])
        wv_hi, wv_lo = split("wv", [P, CC, INNER])
        wo_hi, wo_lo = split("wo", [P, PAIRS, C])
        ln_w, ln_b = sb("ln_w", [P, C]), sb("ln_b", [P, C])
        mean, rstd = sb("mean", [P, UNITS]), sb("rstd", [P, UNITS])
        xn = sb("xn", [P, 2, C])
        x_hi, x_lo = split("x", [P, 2, P])
        craw = sb("craw", [P, 2, CC, P])
        c_hi, c_lo = split("c", [P, 2, CC, P])
        qx = sb("qx", [P, 2, PAIRS, 2, 2, N])
        kx = sb("kx", [P, 2, PAIRS, 2 * KEYS1])
        v = sb("v", [P, 2, 2, INNER])
        top, total, recip = (sb(n, [P, 2, PAIRS]) for n in ("top", "total", "recip"))
        prob = sb("prob", [P, 2, PAIRS, P])
        probT = sb("probT", [P, 2, PAIRS, P])
        oT_hi, oT_lo = split("oT", [P, PAIRS, 2, N])
        y_stats, y_agg = sb("y_stats", [P, 6]), sb("y_agg", [P, 2])
        ln, r0, newton, y_rstd = (sb(n, [P, 1]) for n in ("ln", "r0", "newton", "y_rstd"))
        zero = sb("zero", [P, 1])
        yn = sb("yn", [P, 2, C])

        s_ps = ps("s", [P, 2, PAIRS, P])
        p_ps = ps("p", [P, 2, 512])
        t_ps = ps("t", [P, 512])
        o_ps = ps("o", [P, PAIRS, N])
        xT_ps, y_ps = t_ps[:, 0:P], t_ps[:, 128:128 + C]

        small = ((ln_w[:, :], a["c_ln_w"]), (ln_b[:, :], a["c_ln_b"]))
        late = [(kx[:, s, :, N:N + 2], a["c_null_k"]) for s in range(2)]
        late += [(v[row:row + 1, s, b, :], a["c_null_v"]) for s in range(2) for b, row in ((0, N), (1, N - 1))]
        late = tuple(late)
        loaded, late_loaded, zeroed = sem("loaded"), sem("late_loaded"), sem("zeroed")
        c_in = [sem(f"c_in{s}") for s in range(2)]
        xn_done, xT_done, xhi_done, xlo_done = (mark(n) for n in ("xn", "xT", "xhi", "xlo"))
        chi_done, clo_done = mark("chi"), mark("clo")
        p_done = mark("p", 6)
        q_out, k_out, v_out = mark("q_out", 4), mark("k_out", 2), mark("v_out", 4)
        scores_done, max_done, sub_done, exp_done = mark("scores", 2), mark("max", 2), mark("sub", 2), mark("exp", 2)
        sum_done, recip_done, prob_done = mark("sum", 2), mark("recip", 2), mark("prob", 2)
        turned, probT_done = mark("turned", 2), mark("probT", 2)
        pv_done, ohi_done, olo_done = mark("pv", 2), mark("ohi", 2), mark("olo", 2)
        y_done, ln_step, ln_done, root_done, yn_done = mark("y"), mark("ln_step", 6), mark("ln"), mark("root"), mark("yn")
        scaled, resid_done = mark("scaled", 2), mark("resid")
        vec_stats, act_stats, stats_ready = finish_stats(nc, ctx, "c_s", stats, mean, rstd, False)

        flat = lambda t: t.rearrange("p r c -> p (r c)")
        jobs = pieces(flat(wq_hi[:, :, :]), flat(wq_lo[:, :, :]), a["c_wq"])
        for cc in range(CC):
            jobs += pieces(flat(wk_hi[:, cc, :, :]), flat(wk_lo[:, cc, :, :]), a["c_wk"][cc])
        for cc in range(CC):
            jobs += pieces(wv_hi[:, cc, :], wv_lo[:, cc, :], a["c_wv"][cc])
        jobs += pieces(flat(wo_hi[:, :, :]), flat(wo_lo[:, :, :]), a["c_wo"])
        load_w, hi_w, lo_w, w_split = split_weights(nc, ctx, "c_sw", jobs)

        DEPTH = 4
        block = ctx.block()
        keys = (slice(0, KEYS1), slice(P - KEYS1, P))

        @block.sync
        def _(sp):
            for dst, src in small:
                sp.dma_start(dst, src).then_inc(loaded, 16)
            sp.wait_ge(zeroed, 4)
            for dst, src in late:
                sp.dma_start(dst, src).then_inc(late_loaded, 16)
            load_w(sp)

            def step(at, on):
                if on(0):
                    g = at(0)
                    sp.wait_ge(clo_done.sem, clo_done.at(g.u - 2))
                    sp.dma_start(craw[:, g.slot, :, :], a["c_ctxT"][:, :, bass.ds(g.u * P, P)]
                                 ).then_inc(c_in[g.slot], 16)

            pipeline(sp, UNITS, DEPTH, step)

        @block.gpsimd
        def _(pool):
            for m in (chi_done, clo_done, prob_done, scaled, resid_done):
                m.credit(pool)
            pool.memset(zero[:, :], 0.0).then_inc(zeroed, 1)
            pool.memset(v[:, :, :, :], 0.0).then_inc(zeroed, 1)
            pool.memset(qx[:, :, :, :, :, :], 0.0).then_inc(zeroed, 1)
            pool.memset(prob[:, :, :, :], 0.0).then_inc(zeroed, 1)
            lo_w(pool)
            pool.wait_ge(zeroed, 4)

            def normalise(g, b):
                pool.wait_ge(recip_done.sem, recip_done.at(g.u, b + 1))
                pool.tensor_tensor(prob[:, b, :, keys[b]], prob[:, b, :, keys[b]],
                                   recip[:, b, :].unsqueeze(2).to_broadcast([P, PAIRS, KEYS1]),
                                   ALU.mult).then_inc(prob_done.sem, 1)

            def step(at, on):
                if on(2):
                    normalise(at(2), 0)
                if on(0):
                    g = at(0)
                    pool.wait_ge(c_in[g.slot], g.half * 16 + 16)
                    pool.wait_ge(p_done.sem, p_done.at(g.u - 2))
                    flat_c = lambda t: t[:, g.slot, :, :].rearrange("p c t -> p (c t)")
                    pool.tensor_tensor(flat_c(c_hi), flat_c(craw), zero[:, 0:1].to_broadcast([P, CC * P]),
                                       ALU.subtract).then_inc(chi_done.sem, 1)
                    pool.wait_ge(chi_done.sem, chi_done.at(g.u))
                    pool.tensor_tensor(flat_c(c_lo), flat_c(craw), flat_c(c_hi).bitcast(F32),
                                       ALU.subtract).then_inc(clo_done.sem, 1)
                if on(2):
                    normalise(at(2), 1)
                if on(3):
                    g = at(3)
                    yu = yn[:, g.slot, :]
                    xu = x[:, bass.ds(g.u, 1), :].rearrange("p a f -> p (a f)")
                    pool.wait_ge(loaded, 16 * len(small))
                    pool.wait_ge(yn_done.sem, yn_done.at(g.u))
                    pool.tensor_tensor(yu, yu, ln_w[:, :], ALU.mult).then_inc(scaled.sem, 1)
                    pool.wait_ge(scaled.sem, scaled.at(g.u, 1))
                    pool.tensor_tensor(yu, yu, ln_b[:, :], ALU.add).then_inc(scaled.sem, 1)
                    pool.wait_ge(scaled.sem, scaled.at(g.u))
                    pool.tensor_tensor(xu, xu, yu, ALU.add).then_inc(resid_done.sem, 1)

            pipeline(pool, UNITS, DEPTH, step)

        @block.scalar
        def _(act):
            for m in (xhi_done, q_out, k_out, exp_done, probT_done, ohi_done, ln_done, root_done):
                m.credit(act)
            act_stats(act)
            hi_w(act)
            act.wait_ge(zeroed, 4)

            def copy_probs(g, b):
                act.wait_ge(turned.sem, turned.at(g.u, b + 1))
                act.wait_ge(pv_done.sem, pv_done.at(g.u - 1, b + 1))
                act.activation(probT[:, b, :, :], s_ps[:, b, :, :], ACT.Copy).then_inc(probT_done.sem, 1)

            def exps(g, b):
                act.wait_ge(sub_done.sem, sub_done.at(g.u, b + 1))
                act.activation(prob[:, b, :, keys[b]], prob[:, b, :, keys[b]], ACT.Exp).then_inc(exp_done.sem, 1)

            def output_hi(g, b):
                act.wait_ge(pv_done.sem, pv_done.at(g.u, b + 1))
                act.wait_ge(y_done.sem, y_done.at(g.u - 1))
                act.activation(oT_hi[:, :, b, :], o_ps[:, :, :], ACT.Copy).then_inc(ohi_done.sem, 1)

            def q_half(g, n):
                act.wait_ge(p_done.sem, p_done.at(g.u, n + 1))
                act.wait_ge(scores_done.sem, scores_done.at(g.u - 2))
                for par in range(2):
                    r = slice(par * N, (par + 1) * N)
                    act.activation(qx[r, g.slot, n * HALF:(n + 1) * HALF, :, par, :],
                                   p_ps[r, n, :].rearrange("p (r b q) -> p r b q", r=HALF, b=2), ACT.Copy,
                                   scale=float(D1) ** -0.5).then_inc(q_out.sem, 1)

            def k_half(g, n):
                act.wait_ge(p_done.sem, p_done.at(g.u, n + 3))
                act.wait_ge(scores_done.sem, scores_done.at(g.u - 2))
                src = p_ps[:, n, :].rearrange("p (r b k) -> p r b k", r=HALF, b=2)
                dst = kx[:, g.slot, n * HALF:(n + 1) * HALF, :]
                for b in range(2):
                    last = act.activation(dst[:, :, b * (N + 2):b * (N + 2) + N], src[:, :, b, :], ACT.Copy)
                last.then_inc(k_out.sem, 1)

            def step(at, on):
                if on(3):
                    copy_probs(at(3), 1)
                if on(1):
                    q_half(at(1), 0)
                if on(2):
                    exps(at(2), 0)
                if on(3):
                    output_hi(at(3), 1)
                if on(1):
                    q_half(at(1), 1)
                    k_half(at(1), 0)
                    k_half(at(1), 1)
                if on(2):
                    copy_probs(at(2), 0)
                    exps(at(2), 1)
                    output_hi(at(2), 0)
                if on(3):
                    g = at(3)
                    act.wait_ge(ln_step.sem, ln_step.at(g.u, 3))
                    act.activation(ln[:, :], newton[:, :], ACT.Ln).then_inc(ln_done.sem, 1)
                    act.wait_ge(ln_done.sem, ln_done.at(g.u))
                    act.activation(r0[:, :], ln[:, :], ACT.Exp, scale=-0.5).then_inc(root_done.sem, 1)
                if on(0):
                    g = at(0)
                    act.wait_ge(xT_done.sem, xT_done.at(g.u))
                    act.wait_ge(p_done.sem, p_done.at(g.u - 2, 2))
                    act.activation(x_hi[:, g.slot, :], xT_ps, ACT.Copy).then_inc(xhi_done.sem, 1)

            pipeline(act, UNITS, DEPTH, step)

        @block.tensor
        def _(pe):
            for m in (xT_done, p_done, scores_done, turned, pv_done, y_done):
                m.credit(pe)
            pe.wait_ge(late_loaded, 16 * len(late))
            pe.wait_ge(w_split, len(jobs))

            def three(dst, hi, lo, m_hi, m_lo, start=True, stop=True):
                pe.matmul(dst, hi, m_hi, start=start, stop=False)
                pe.matmul(dst, hi, m_lo, start=False, stop=False)
                return pe.matmul(dst, lo, m_hi, start=False, stop=stop)

            def q_product(g, n):
                if n == 0:
                    pe.wait_ge(xlo_done.sem, xlo_done.at(g.u))
                pe.wait_ge(v_out.sem, v_out.at(g.u - 1, 2 * n + 2))
                for r in range(HALF):
                    m = three(p_ps[:, n, r * P:(r + 1) * P], wq_hi[:, n * HALF + r, :], wq_lo[:, n * HALF + r, :],
                              x_hi[:, g.slot, :], x_lo[:, g.slot, :])
                m.then_inc(p_done.sem, 1)

            def k_product(g, n):
                if n == 0:
                    pe.wait_ge(clo_done.sem, clo_done.at(g.u))
                pe.wait_ge(q_out.sem, q_out.at(g.u, 2 * n + 2))
                for r in range(HALF):
                    for cc in range(CC):
                        m = three(p_ps[:, n, r * P:(r + 1) * P], wk_hi[:, cc, n * HALF + r, :],
                                  wk_lo[:, cc, n * HALF + r, :], c_hi[:, g.slot, cc, :], c_lo[:, g.slot, cc, :],
                                  cc == 0, cc == CC - 1)
                m.then_inc(p_done.sem, 1)

            def v_product(g, n):
                pe.wait_ge(k_out.sem, k_out.at(g.u, n + 1))
                for cc in range(CC):
                    cols = slice(n * 512, (n + 1) * 512)
                    m = three(p_ps[:, n, :], c_hi[:, g.slot, cc, :], c_lo[:, g.slot, cc, :],
                              wv_hi[:, cc, cols], wv_lo[:, cc, cols], cc == 0, cc == CC - 1)
                m.then_inc(p_done.sem, 1)

            def scores(g, b):
                pe.wait_ge(k_out.sem, k_out.at(g.u))
                pe.wait_ge(probT_done.sem, probT_done.at(g.u - 1, b + 1))
                for r in range(PAIRS):
                    m = pe.matmul(s_ps[:, b, r, 0:KEYS1], qx[:, g.slot, r, b, :, :].rearrange("p h q -> p (h q)"),
                                  kx[:, g.slot, r, b * KEYS1:(b + 1) * KEYS1], start=True, stop=True)
                m.then_inc(scores_done.sem, 1)

            def turn_probs(g, b):
                pe.wait_ge(prob_done.sem, prob_done.at(g.u, b + 1))
                for r in range(PAIRS):
                    m = pe.transpose(s_ps[:, b, r, :], prob[:, b, r, :], ident[:, :])
                m.then_inc(turned.sem, 1)

            def values(g, b):
                pe.wait_ge(probT_done.sem, probT_done.at(g.u, b + 1))
                pe.wait_ge(v_out.sem, v_out.at(g.u))
                pe.wait_ge(olo_done.sem, olo_done.at(g.u, b))
                for r in range(PAIRS):
                    for par in range(2):
                        h = 2 * r + par
                        m = pe.matmul(o_ps[par * N:(par + 1) * N, r, :], v[:, g.slot, b, h * D1:(h + 1) * D1],
                                      probT[:, b, r, par * N:(par + 1) * N], start=True, stop=True)
                m.then_inc(pv_done.sem, 1)

            def step(at, on):
                if on(2):
                    scores(at(2), 0)
                if on(1):
                    q_product(at(1), 0)
                    q_product(at(1), 1)
                if on(3):
                    values(at(3), 1)
                if on(1):
                    k_product(at(1), 0)
                    k_product(at(1), 1)
                if on(2):
                    turn_probs(at(2), 0)
                    scores(at(2), 1)
                if on(1):
                    v_product(at(1), 0)
                    v_product(at(1), 1)
                if on(2):
                    values(at(2), 0)
                if on(3):
                    g = at(3)
                    pe.wait_ge(olo_done.sem, olo_done.at(g.u))
                    pe.wait_ge(yn_done.sem, yn_done.at(g.u - 1))
                    for r in range(PAIRS):
                        m = three(y_ps, oT_hi[:, r, :, :].rearrange("p b q -> p (b q)"),
                                  oT_lo[:, r, :, :].rearrange("p b q -> p (b q)"), wo_hi[:, r, :], wo_lo[:, r, :],
                                  r == 0, r == PAIRS - 1)
                    m.then_inc(y_done.sem, 1)
                if on(0):
                    g = at(0)
                    pe.wait_ge(xn_done.sem, xn_done.at(g.u))
                    if on(3):
                        pe.wait_ge(yn_done.sem, yn_done.at(at(3).u))
                    pe.transpose(xT_ps, xn[:, g.slot, :], ident[:, :]).then_inc(xT_done.sem, 1)
                if on(2):
                    turn_probs(at(2), 1)

            pipeline(pe, UNITS, DEPTH, step)

        @block.vector
        def _(dve):
            for m in (xn_done, xlo_done, v_out, max_done, sub_done, sum_done, recip_done, olo_done, ln_step, yn_done):
                m.credit(dve)
            vec_stats(dve)
            dve.wait_ge(stats_ready, 1)
            dve.wait_ge(late_loaded, 16 * len(late))

            def shift(g, b):
                raw = s_ps[:, b, :, 0:KEYS1]
                dve.wait_ge(scores_done.sem, scores_done.at(g.u, b + 1))
                dve.tensor_reduce(top[:, b, :], raw, AX.X, ALU.max).then_inc(max_done.sem, 1)
                dve.wait_ge(max_done.sem, max_done.at(g.u, b + 1))
                dve.wait_ge(turned.sem, turned.at(g.u - 1, b + 1))
                dve.tensor_tensor(prob[:, b, :, keys[b]], raw, top[:, b, :].unsqueeze(2).to_broadcast([P, PAIRS, KEYS1]),
                                  ALU.subtract).then_inc(sub_done.sem, 1)

            def denominators(g, b):
                dve.wait_ge(exp_done.sem, exp_done.at(g.u, b + 1))
                dve.tensor_reduce(total[:, b, :], prob[:, b, :, keys[b]], AX.X, ALU.add).then_inc(sum_done.sem, 1)
                dve.wait_ge(sum_done.sem, sum_done.at(g.u, b + 1))
                dve.wait_ge(prob_done.sem, prob_done.at(g.u - 1, b + 1))
                dve.reciprocal(recip[:, b, :], total[:, b, :]).then_inc(recip_done.sem, 1)

            def output_lo(g, b):
                dve.wait_ge(ohi_done.sem, ohi_done.at(g.u, b + 1))
                dve.tensor_tensor(oT_lo[:, :, b, :], o_ps[:, :, :], oT_hi[:, :, b, :].bitcast(F32),
                                  ALU.subtract).then_inc(olo_done.sem, 1)

            def step(at, on):
                if on(0):
                    g = at(0)
                    dve.wait_ge(xT_done.sem, xT_done.at(g.u - 2))
                    dve.tensor_scalar(xn[:, g.slot, :], x[:, bass.ds(g.u, 1), :].rearrange("p a f -> p (a f)"),
                                      mean[:, bass.ds(g.u, 1)], rstd[:, bass.ds(g.u, 1)],
                                      ALU.subtract, ALU.mult).then_inc(xn_done.sem, 1)
                if on(2):
                    shift(at(2), 0)
                if on(3):
                    output_lo(at(3), 1)
                if on(2):
                    denominators(at(2), 0)
                    shift(at(2), 1)
                if on(1):
                    g = at(1)
                    for n in range(2):
                        dve.wait_ge(p_done.sem, p_done.at(g.u, n + 5))
                        dve.wait_ge(pv_done.sem, pv_done.at(g.u - 2))
                        for b in range(2):
                            r = slice(b * N, (b + 1) * N)
                            dve.tensor_copy(v[r, g.slot, b, n * 512:(n + 1) * 512], p_ps[r, n, :]
                                            ).then_inc(v_out.sem, 1)
                if on(2):
                    denominators(at(2), 1)
                    output_lo(at(2), 0)
                if on(3):
                    g = at(3)

                    def after(n):
                        dve.wait_ge(ln_step.sem, ln_step.at(g.u, n))

                    dve.wait_ge(y_done.sem, y_done.at(g.u))
                    dve.bn_stats(y_stats[:, :], y_ps).then_inc(ln_step.sem, 1)
                    after(1)
                    dve.memset(newton[:, :], 0.0)
                    dve.bn_aggr(y_agg[:, :], y_stats[:, :]).then_inc(ln_step.sem, 1)
                    after(2)
                    dve.tensor_scalar(newton[:, :], y_agg[:, 1:2], 1e-6, None, ALU.add).then_inc(ln_step.sem, 1)
                    dve.wait_ge(root_done.sem, root_done.at(g.u))
                    dve.scalar_tensor_tensor(out=ln[:, :], in0=newton[:, :], scalar=r0[:, 0:1], in1=r0[:, :],
                                             op0=ALU.mult, op1=ALU.mult).then_inc(ln_step.sem, 1)
                    after(4)
                    dve.tensor_scalar(ln[:, :], ln[:, :], -0.5, 1.5, ALU.mult, ALU.add).then_inc(ln_step.sem, 1)
                    after(5)
                    dve.tensor_tensor(y_rstd[:, :], ln[:, :], r0[:, :], ALU.mult).then_inc(ln_step.sem, 1)
                    after(6)
                    dve.wait_ge(resid_done.sem, resid_done.at(g.u - 2))
                    dve.tensor_scalar(yn[:, g.slot, :], y_ps, y_agg[:, 0:1], y_rstd[:, 0:1],
                                      ALU.subtract, ALU.mult).then_inc(yn_done.sem, 1)
                if on(0):
                    g = at(0)
                    dve.wait_ge(xhi_done.sem, xhi_done.at(g.u))
                    dve.wait_ge(p_done.sem, p_done.at(g.u - 2, 2))
                    dve.tensor_tensor(x_lo[:, g.slot, :], xT_ps, x_hi[:, g.slot, :].bitcast(F32),
                                      ALU.subtract).then_inc(xlo_done.sem, 1)
                if on(4):
                    g = at(4)
                    dve.wait_ge(resid_done.sem, resid_done.at(g.u))
                    dve.bn_stats(stats[:, bass.ds(g.u, 1), :].rearrange("p a s -> p (a s)"),
                                 x[:, bass.ds(g.u, 1), :].rearrange("p a f -> p (a f)"))

            pipeline(dve, UNITS, DEPTH, step)


def program(nc, a, out):
    with ExitStack() as ctx:
        x = ctx.enter_context(nc.sbuf_tensor("x_resid", [P, UNITS, C], F32))
        stats = ctx.enter_context(nc.sbuf_tensor("x_stats", [P, UNITS, 6], F32))
        ident = ctx.enter_context(nc.sbuf_tensor("identity", [P, P], F32))
        headmask = ctx.enter_context(nc.sbuf_tensor("headmask", [P, H], F32))
        attention0(nc, x, stats, ident, headmask, a["x"], a["a_wqkvT"], a["a_wprojT"], a["a_bproj"],
                   a["a_ctx_kT"], a["a_ctx_v"], a)
        experts(nc, x, stats, ident, a, False, out)
        attention1(nc, x, stats, ident, a)
        experts(nc, x, stats, ident, a, True, out)


def layout(inp):
    f = lambda n: np.asarray(inp[n])
    x, c = f("x"), f("ctx_2048")
    d = {"x": x.reshape(B * N, C)}
    d["a_wqkvT"] = f("L0_xattn_w_qkv").reshape(3, P, C).transpose(2, 0, 1)
    wp = f("L0_xattn_w_proj").T.reshape(PAIRS, 2, D0, C).transpose(0, 2, 1, 3).reshape(N, 2, C)
    d["a_wprojT"] = np.concatenate([wp, wp])
    d["a_bproj"] = np.broadcast_to(f("L0_xattn_b_proj"), (P, C))
    d["a_ctx_kT"] = c[:, :, :C].reshape(B * N, C).T
    v = c[:, :, C:].reshape(UNITS, 2, N, C)[:, ::-1]
    d["a_ctx_v"] = v.reshape(UNITS, P, C).transpose(1, 0, 2).reshape(P, UNITS * C)
    gate, up = (f(n).reshape(E * 336, C).T for n in ("L0_ffn_gate_w", "L0_ffn_up_w"))
    d["b_w"] = np.stack([gate, up])
    d["b_wd"] = f("L0_ffn_down_w").transpose(0, 2, 1).reshape(E * 3, 112, C).transpose(1, 0, 2).reshape(112, -1)
    d["b_rw"] = f("L0_ffn_router_w").T
    aw1 = np.zeros((C, P), np.float32)
    aw1[:, :50] = f("L0_ffn_actor_w1").T
    d["b_aw1T"] = aw1
    d["b_ab1"] = f("L0_ffn_actor_b1").reshape(50, 1)
    d["b_aw2T"] = f("L0_ffn_actor_w2").T
    d["b_ab2"] = np.broadcast_to(f("L0_ffn_actor_b2"), (P, 6))
    d["kcode"] = np.broadcast_to(np.arange(1, 7, dtype=np.float32) - 100, (P, 6))
    d["before"] = np.broadcast_to(np.tril(np.ones((E, E), np.float32), -1), (P, E, E))
    sel = np.zeros((P, E, P), np.float32)
    for e in range(E):
        sel[e, e] = sel[E + e, e] = 1
    d["sel"] = sel.reshape(P, E * P)
    d["c_wq"] = f("L1_xattn_Wq")
    wkv = f("L1_xattn_Wkv").reshape(2, P, 2, H * 64)
    d["c_wk"], d["c_wv"] = wkv[:, :, 0], wkv[:, :, 1]
    d["c_wo"] = f("L1_xattn_Wout").reshape(PAIRS, P, C).transpose(1, 0, 2).reshape(P, PAIRS * C)
    null = f("L1_xattn_null_kv")
    d["c_null_k"] = np.broadcast_to(np.tile(null[0], 2)[:, None, None], (P, PAIRS, 2))
    d["c_null_v"] = np.tile(null[1], H)[None]
    d["c_ln_w"] = np.broadcast_to(f("L1_xattn_ln_scale"), (P, C))
    d["c_ln_b"] = np.broadcast_to(f("L1_xattn_ln_bias"), (P, C))
    d["c_ctxT"] = c.reshape(B * N, 2, P).transpose(2, 1, 0)
    w1 = np.concatenate([f("L1_ffn_sw1")[None], f("L1_ffn_ew1")])
    w2 = np.concatenate([f("L1_ffn_sw2")[None], f("L1_ffn_ew2")])
    d["d_w"] = w1.transpose(1, 0, 2).reshape(1, P, -1)
    d["d_wd"] = w2.reshape((E + 1) * 4, P, C).transpose(1, 0, 2).reshape(P, -1)
    d["d_rw"] = f("L1_ffn_router_w").T
    d["d_b1"] = np.concatenate([f("L1_ffn_sb1")[None], f("L1_ffn_eb1")]).reshape((E + 1) * 4, P).T
    d["d_b2"] = np.concatenate([f("L1_ffn_sb2")[None], f("L1_ffn_eb2")]).T
    d["d_norm"] = f("L1_ffn_norm_weight").reshape(P, 1)
    d["ident"] = np.eye(P, dtype=np.float32)
    d["headmask"] = np.repeat(np.eye(H, dtype=np.float32), D0, axis=0)
    return {k: np.ascontiguousarray(v) for k, v in d.items()}


def kernel(**inputs):
    import concourse.bacc as bacc
    from concourse.bass_utils import run_bass_kernel_spmd

    nc = bacc.Bacc("TRN2", target_bir_lowering=False, num_devices=1)
    arrays = {f"in_{k}_dram": v for k, v in layout(inputs).items()}
    args = {k[3:-5]: nc.dram_tensor(k, v.shape, mybir.dt.from_np(v.dtype), kind="ExternalInput").ap()
            for k, v in arrays.items()}
    out = nc.dram_tensor("out_dram", (B * N, C), F32, kind="ExternalOutput").ap()
    program(nc, args, out)
    got = run_bass_kernel_spmd(nc, [arrays], core_ids=[0])
    return got.results[0]["out_dram"].reshape(B, N, C)
```

```python
from contextlib import ExitStack, contextmanager

import numpy as np

import concourse.bass as bass
from concourse import mybir

F32 = mybir.dt.float32
F32R = mybir.dt.float32r
ALU = mybir.AluOpType
ACT = mybir.ActivationFunctionType
AX = mybir.AxisListType

P = 128
B, N, C = 64, 64, 128
UNITS = B * N // P
GROUP = 4
GROUPS = UNITS // GROUP
COLS = GROUP * P
H = 16
PAIRS = H // 2
D0, D1 = 8, 64
KEYS0 = 2 * N
KEYS1 = N + 1
VW = D0 + 1
E = 8
LN_EPS = 1e-5


@contextmanager
def stage(nc):
    with ExitStack() as ctx:
        taken = []
        ctx.sem = lambda name: taken.append(ctx.enter_context(nc.semaphore(name))) or taken[-1]
        with ExitStack() as blocks:
            ctx.block = lambda: blocks.enter_context(nc.Block())
            yield ctx
        with nc.Block() as block:
            @block.sync
            def _(sp):
                for s in taken:
                    sp.sem_clear(s)


class Mark:

    def __init__(self, ctx, nc, name, per=1):
        self.sem, self.per = ctx.sem(name), per

    def credit(self, eng):
        eng.sem_inc(self.sem, 2 * self.per)

    def at(self, u, j=None):
        return u * self.per + (2 * self.per + (self.per if j is None else j))


class At:

    def __init__(self, k, j, lag, width):
        m = j - lag
        self.u, self.half = width * k + m, width // 2 * k + m // 2
        self.slot, self.slot4 = m % 2, m % 4


def pipeline(eng, units, depth, step, width=2):
    for t in range(depth):
        step(lambda lag, t=t: At(t // width, t % width, lag, width), lambda lag, t=t: t - lag >= 0)
    with eng.Fori(depth // width, units // width) as k:
        for j in range(width):
            step(lambda lag, j=j: At(k, j, lag, width), lambda lag: True)
    for t in range(units, units + depth):
        step(lambda lag, t=t: At(t // width, t % width, lag, width), lambda lag, t=t: t - lag < units)


class Turn:

    def __init__(self, k, lag):
        self.u = k - lag


def turns(eng, groups, depth, step):
    for t in range(depth):
        step(lambda lag, t=t: Turn(t, lag), lambda lag, t=t: t - lag >= 0)
    with eng.Fori(depth, groups) as k:
        step(lambda lag: Turn(k, lag), lambda lag: True)
    for t in range(groups, groups + depth):
        step(lambda lag, t=t: Turn(t, lag), lambda lag, t=t: t - lag < groups)


def finish_stats(nc, ctx, tag, stats, mean, rstd, rms):
    var = ctx.enter_context(nc.sbuf_tensor(f"{tag}_var", [P, UNITS], F32))
    tmp = ctx.enter_context(nc.sbuf_tensor(f"{tag}_tmp", [P, 2, UNITS], F32))
    root = ctx.enter_context(nc.sbuf_tensor(f"{tag}_root", [P, 2, UNITS], F32))
    chain = ctx.sem(f"{tag}_stat_steps")
    rooted = ctx.sem(f"{tag}_rooted")
    asked = ctx.sem(f"{tag}_root_asked")
    ready = ctx.sem(f"{tag}_stats_ready")

    def vector(dve):
        n = [0]

        def link(ins):
            n[0] += 1
            ins.then_inc(chain, 1)
            dve.wait_ge(chain, n[0])

        even_mean, even_m2 = stats[:, :, 1], stats[:, :, 2]
        odd_mean, odd_m2 = stats[:, :, 4], stats[:, :, 5]
        link(dve.tensor_tensor(mean[:, :], even_mean, odd_mean, ALU.add))
        link(dve.tensor_scalar(mean[:, :], mean[:, :], 0.5, None, ALU.mult))
        link(dve.tensor_tensor(tmp[:, 0, :], even_mean, odd_mean, ALU.subtract))
        link(dve.tensor_tensor(tmp[:, 0, :], tmp[:, 0, :], tmp[:, 0, :], ALU.mult))
        link(dve.tensor_tensor(tmp[:, 1, :], even_m2, odd_m2, ALU.add))
        link(dve.tensor_scalar(tmp[:, 1, :], tmp[:, 1, :], 1.0 / C, None, ALU.mult))
        link(dve.scalar_tensor_tensor(out=var[:, :], in0=tmp[:, 0, :], scalar=0.25, in1=tmp[:, 1, :],
                                      op0=ALU.mult, op1=ALU.add))
        dve.tensor_scalar(tmp[:, 0, :], var[:, :], LN_EPS, None, ALU.add).then_inc(asked, 1)
        dve.wait_ge(rooted, 1)
        if not rms:
            dve.reciprocal(rstd[:, :], root[:, 0, :]).then_inc(ready, 1)
            return
        link(dve.reciprocal(rstd[:, :], root[:, 0, :]))
        link(dve.tensor_tensor(tmp[:, 1, :], rstd[:, :], rstd[:, :], ALU.mult))
        link(dve.tensor_tensor(tmp[:, 1, :], tmp[:, 1, :], var[:, :], ALU.mult))
        dve.tensor_scalar(tmp[:, 1, :], tmp[:, 1, :], 1e-8, None, ALU.add).then_inc(asked, 1)
        dve.wait_ge(rooted, 2)
        link(dve.reciprocal(root[:, 0, :], root[:, 1, :]))
        dve.tensor_tensor(rstd[:, :], rstd[:, :], root[:, 0, :], ALU.mult).then_inc(ready, 1)

    def scalar(act):
        for i in range(2 if rms else 1):
            act.wait_ge(asked, i + 1)
            act.activation(root[:, i, :], tmp[:, i, :], ACT.Sqrt).then_inc(rooted, 1)

    return vector, scalar, ready


def attention0(nc, x, stats, ident, headmask, x_in, w_qkvT, w_projT, b_proj, ctx_kT, ctx_v, consts):
    with stage(nc) as ctx:
        def sb(name, shape, dt=F32):
            return ctx.enter_context(nc.sbuf_tensor("a_" + name, shape, dt))

        def ps(name, shape):
            return ctx.enter_context(nc.psum_tensor("a_" + name, shape, F32))

        def sem(name):
            return ctx.sem("a_" + name)

        def mark(name, per=1):
            return Mark(ctx, nc, "a_" + name, per)

        wqkv = sb("wqkv", [P, 3, P])
        wproj = sb("wproj", [P, 2, P])
        bias_bc = sb("bias_bc", [P, C])
        mean = sb("mean", [P, UNITS])
        rstd = sb("rstd", [P, UNITS])
        xn = sb("xn", [P, 2, C])
        xnT = sb("xnT", [P, 2, P])
        qT = sb("qT", [P, 2, P])
        qx = sb("qx", [P, 2, 2, H, N])
        kT = sb("kT", [P, 2, 2, KEYS0])
        cv = sb("cv", [P, 2, C])
        vx = sb("vx", [P, 4, 2, H, VW])
        top = sb("top", [P, 2, PAIRS])
        prob = sb("prob", [P, 2, PAIRS, KEYS0])
        probT = sb("probT", [P, 2, PAIRS, P])
        recip = sb("recip", [P, 2, PAIRS])
        o = sb("o", [P, 2, PAIRS, D0])
        oT = sb("oT", [P, P])

        score_ps = ps("score_ps", [P, 2, PAIRS, KEYS0])
        probT_ps = ps("probT_ps", [P, PAIRS, P])
        in_ps = ps("in_ps", [P, 4, P])
        out_ps = ps("out_ps", [P, 512])
        o_ps = out_ps[:, 0:2 * PAIRS * 2 * VW].rearrange("p (b r c) -> p b r c", b=2, r=PAIRS)
        y_ps = out_ps[:, 384:512]

        loaded, x_loaded, first_stats, zeroed = sem("loaded"), sem("x_loaded"), sem("first_stats"), sem("zeroed")
        k_in = [sem(f"k_in{s}") for s in range(2)]
        v_in = [sem(f"v_in{s}") for s in range(2)]
        xn_done, biased = mark("xn_done"), mark("biased")
        xnT_ps_done, xnT_done = mark("xnT_ps_done"), mark("xnT_done")
        qkv_done, qkv_out = mark("qkv_done"), mark("qkv_out", 4)
        qx_done, cv_done = mark("qx_done"), mark("cv_done")
        scores_done, max_done, sub_done, exp_done = mark("scores", 2), mark("max", 2), mark("sub", 2), mark("exp", 2)
        probT_ps_done, probT_done = mark("probT_ps", 2), mark("probT", 4)
        pv_done, recip_done, o_done = mark("pv", 2), mark("recip", 4), mark("o", 4)
        oT_ps_done, oT_done, y_done, resid_done = mark("oT_ps"), mark("oT"), mark("y"), mark("resid")
        vec_stats, act_stats, stats_ready = finish_stats(nc, ctx, "a", stats, mean, rstd, False)

        DEPTH = 4
        block = ctx.block()

        @block.sync
        def _(sp):
            for s in range(4):
                n = UNITS // 4
                sp.dma_start(x[:, s * n:(s + 1) * n, :],
                             x_in[s * n * P:(s + 1) * n * P, :].rearrange("(u p) f -> p u f", p=P)).then_inc(x_loaded, 16)
            for dst, src in ((wqkv[:, :, :], w_qkvT), (wproj[:, :, :], w_projT), (bias_bc[:, :], b_proj),
                             (ident[:, :], consts["ident"]), (headmask[:, :], consts["headmask"])):
                sp.dma_start(dst, src).then_inc(loaded, 16)

            def step(at, on):
                if on(0):
                    a = at(0)
                    sp.wait_ge(scores_done.sem, scores_done.at(a.u - 2))
                    sp.dma_start(kT[:, a.slot, :, :].rearrange("p b k -> p (b k)")[:, N:3 * N],
                                 ctx_kT[:, bass.ds(a.u * P, P)]).then_inc(k_in[a.slot], 16)
                    sp.wait_ge(cv_done.sem, cv_done.at(a.u - 2))
                    sp.dma_start(cv[:, a.slot, :], ctx_v[:, bass.ds(a.u * P, P)]).then_inc(v_in[a.slot], 16)

            pipeline(sp, UNITS, DEPTH, step, 4)

        @block.gpsimd
        def _(pool):
            for m in (biased, qx_done, cv_done):
                m.credit(pool)
            pool.memset(vx[:, :, :, :, :], 1.0).then_inc(zeroed, 1)
            pool.wait_ge(loaded, 5 * 16)
            pool.wait_ge(zeroed, 1)

            def step(at, on):
                if on(1):
                    a = at(1)
                    pool.wait_ge(v_in[a.slot], a.half * 16 + 16)
                    pool.wait_ge(pv_done.sem, pv_done.at(a.u - 2, 1))
                if on(0):
                    a = at(0)
                    pool.wait_ge(xn_done.sem, xn_done.at(a.u))
                    xu = x[:, bass.ds(a.u, 1), :].rearrange("p a f -> p (a f)")
                    pool.tensor_tensor(xu, xu, bias_bc[:, :], ALU.add).then_inc(biased.sem, 1)
                if on(1):
                    a = at(1)
                    for b in range(2):
                        last = pool.tensor_copy(vx[:, a.slot4, b, :, 0:D0],
                                                cv[:, a.slot, :].rearrange("p (h d) -> p h d", h=H))
                    last.then_inc(cv_done.sem, 1)
                    pool.wait_ge(qkv_out.sem, qkv_out.at(a.u, 1))
                    pool.wait_ge(scores_done.sem, scores_done.at(a.u - 2))
                    for b in range(2):
                        last = pool.tensor_tensor(
                            qx[:, a.slot, b, :, :],
                            qT[:, a.slot, b * N:(b + 1) * N].unsqueeze(1).to_broadcast([P, H, N]),
                            headmask[:, :].unsqueeze(2).to_broadcast([P, H, N]), ALU.mult)
                    last.then_inc(qx_done.sem, 1)

            pipeline(pool, UNITS, DEPTH, step, 4)

        @block.scalar
        def _(act):
            for m in (xnT_done, qkv_out, exp_done, probT_done, oT_done):
                m.credit(act)
            act_stats(act)

            def copy_probs(a, b):
                act.wait_ge(pv_done.sem, pv_done.at(a.u - 1, b + 1))
                act.wait_ge(probT_ps_done.sem, probT_ps_done.at(a.u, b + 1))
                for h in range(2):
                    act.activation(probT[:, b, 4 * h:4 * h + 4, :], probT_ps[:, 4 * h:4 * h + 4, :],
                                   ACT.Copy).then_inc(probT_done.sem, 1)

            def exps(a, b):
                act.wait_ge(sub_done.sem, sub_done.at(a.u, b + 1))
                act.activation(prob[:, b, :, :], prob[:, b, :, :], ACT.Exp).then_inc(exp_done.sem, 1)

            def step(at, on):
                if on(1):
                    a = at(1)
                    act.wait_ge(qkv_done.sem, qkv_done.at(a.u))
                    act.wait_ge(qx_done.sem, qx_done.at(a.u - 2))
                    act.activation(qT[:, a.slot, :], in_ps[:, 1, :], ACT.Copy,
                                   scale=float(D0) ** -0.5).then_inc(qkv_out.sem, 1)
                    act.wait_ge(scores_done.sem, scores_done.at(a.u - 2))
                    own = kT[:, a.slot, :, :].rearrange("p b (h k) -> p (b h) k", k=N)
                    act.activation(own[:, 0:4:3, :], in_ps[:, 2, :].rearrange("p (b k) -> p b k", b=2),
                                   ACT.Copy).then_inc(qkv_out.sem, 1)
                if on(3):
                    copy_probs(at(3), 1)
                if on(2):
                    exps(at(2), 0)
                if on(1):
                    a = at(1)
                    act.wait_ge(cv_done.sem, cv_done.at(a.u))
                    for b in range(2):
                        r = slice(b * N, (b + 1) * N)
                        act.activation(vx[r, a.slot4, b, :, 0:D0],
                                       in_ps[r, 3, :].rearrange("p (h d) -> p h d", h=H),
                                       ACT.Copy).then_inc(qkv_out.sem, 1)
                if on(2):
                    copy_probs(at(2), 0)
                if on(3):
                    a = at(3)
                    act.wait_ge(oT_ps_done.sem, oT_ps_done.at(a.u))
                    act.wait_ge(y_done.sem, y_done.at(a.u - 1))
                    act.activation(oT[:, :], y_ps, ACT.Copy).then_inc(oT_done.sem, 1)
                if on(2):
                    exps(at(2), 1)
                if on(0):
                    a = at(0)
                    act.wait_ge(xnT_ps_done.sem, xnT_ps_done.at(a.u))
                    act.wait_ge(qkv_done.sem, qkv_done.at(a.u - 2))
                    act.activation(xnT[:, a.slot, :], in_ps[:, 0, :], ACT.Copy).then_inc(xnT_done.sem, 1)

            pipeline(act, UNITS, DEPTH, step, 4)

        @block.tensor
        def _(pe):
            for m in (xnT_ps_done, qkv_done, scores_done, probT_ps_done, pv_done, oT_ps_done, y_done):
                m.credit(pe)
            pe.wait_ge(loaded, 5 * 16)

            def scores(a, b):
                if b == 0:
                    pe.wait_ge(qx_done.sem, qx_done.at(a.u))
                    pe.wait_ge(qkv_out.sem, qkv_out.at(a.u, 2))
                    pe.wait_ge(k_in[a.slot], a.half * 16 + 16)
                pe.wait_ge(sub_done.sem, sub_done.at(a.u - 1, b + 1))
                for r in range(PAIRS):
                    m = pe.matmul(score_ps[:, b, r, :],
                                  qx[:, a.slot, b, 2 * r:2 * r + 2, :].rearrange("p h q -> p (h q)"),
                                  kT[:, a.slot, b, :], start=True, stop=True)
                m.then_inc(scores_done.sem, 1)

            def turn_probs(a, b):
                pe.wait_ge(exp_done.sem, exp_done.at(a.u, b + 1))
                pe.wait_ge(probT_done.sem, probT_done.at(a.u - 1 + b, 2 * (2 - b)))
                for r in range(PAIRS):
                    m = pe.transpose(probT_ps[:, r, :], prob[:, b, r, :], ident[:, :])
                m.then_inc(probT_ps_done.sem, 1)

            def values(a, b):
                pe.wait_ge(probT_done.sem, probT_done.at(a.u, 2 * b + 2))
                if b == 0:
                    pe.wait_ge(cv_done.sem, cv_done.at(a.u))
                    pe.wait_ge(qkv_out.sem, qkv_out.at(a.u))
                    pe.wait_ge(oT_done.sem, oT_done.at(a.u - 1))
                else:
                    pe.wait_ge(o_done.sem, o_done.at(a.u, 2))
                    pe.wait_ge(resid_done.sem, resid_done.at(a.u - 1))
                for r in range(PAIRS):
                    m = pe.matmul(o_ps[:, b, r, :], probT[:, b, r, :],
                                  vx[:, a.slot4, b, 2 * r:2 * r + 2, :].rearrange("p h c -> p (h c)"),
                                  start=True, stop=True)
                m.then_inc(pv_done.sem, 1)

            def step(at, on):
                if on(2):
                    scores(at(2), 0)
                if on(4):
                    a = at(4)
                    if on(3):
                        pe.wait_ge(o_done.sem, o_done.at(a.u + 1, 2))
                    pe.wait_ge(oT_done.sem, oT_done.at(a.u))
                if on(1):
                    a = at(1)
                    pe.wait_ge(xnT_done.sem, xnT_done.at(a.u))
                    xu = xnT[:, a.slot, :]
                    pe.matmul(in_ps[:, 1, :], wqkv[:, 0, :], xu, start=True, stop=True)
                    pe.matmul(in_ps[:, 2, :], wqkv[:, 1, :], xu, start=True, stop=True)
                    pe.matmul(in_ps[:, 3, :], xu, wqkv[:, 2, :], start=True, stop=True).then_inc(qkv_done.sem, 1)
                if on(4):
                    for b in range(2):
                        for par in range(2):
                            m = pe.matmul(y_ps[b * N:(b + 1) * N, :], oT[b * N:(b + 1) * N, par * N:(par + 1) * N],
                                          wproj[b * N:(b + 1) * N, par, :], start=(par == 0), stop=(par == 1))
                    m.then_inc(y_done.sem, 1)
                if on(3):
                    turn_probs(at(3), 1)
                if on(2):
                    scores(at(2), 1)
                if on(3):
                    values(at(3), 1)
                if on(2):
                    turn_probs(at(2), 0)
                if on(0):
                    a = at(0)
                    pe.wait_ge(xn_done.sem, xn_done.at(a.u))
                    pe.wait_ge(qkv_out.sem, qkv_out.at(a.u - 1))
                    pe.transpose(in_ps[:, 0, :], xn[:, a.slot, :], ident[:, :]).then_inc(xnT_ps_done.sem, 1)
                if on(3):
                    a = at(3)
                    pe.wait_ge(o_done.sem, o_done.at(a.u))
                    pe.transpose(y_ps, o[:, :, :, :].rearrange("p b r d -> p (b r d)"), ident[:, :]).then_inc(oT_ps_done.sem, 1)
                if on(2):
                    values(at(2), 0)

            pipeline(pe, UNITS, DEPTH, step, 4)

        @block.vector
        def _(dve):
            for m in (xn_done, max_done, sub_done, recip_done, o_done, resid_done):
                m.credit(dve)
            dve.wait_ge(x_loaded, 4 * 16)
            with dve.Fori(0, UNITS) as u:
                dve.bn_stats(stats[:, bass.ds(u, 1), :].rearrange("p a s -> p (a s)"),
                             x[:, bass.ds(u, 1), :].rearrange("p a f -> p (a f)")).then_inc(first_stats, 1)
            dve.wait_ge(first_stats, UNITS)
            vec_stats(dve)
            dve.wait_ge(stats_ready, 1)

            def shift(a, b):
                dve.wait_ge(scores_done.sem, scores_done.at(a.u, b + 1))
                dve.tensor_reduce(top[:, b, :], score_ps[:, b, :, :], AX.X, ALU.max).then_inc(max_done.sem, 1)
                dve.wait_ge(max_done.sem, max_done.at(a.u, b + 1))
                dve.wait_ge(probT_ps_done.sem, probT_ps_done.at(a.u - 1, b + 1))
                dve.tensor_tensor(prob[:, b, :, :], score_ps[:, b, :, :],
                                  top[:, b, :].unsqueeze(2).to_broadcast([P, PAIRS, KEYS0]),
                                  ALU.subtract).then_inc(sub_done.sem, 1)

            def normalise(a, b):
                dve.wait_ge(pv_done.sem, pv_done.at(a.u, b + 1))
                if b == 0:
                    dve.wait_ge(oT_ps_done.sem, oT_ps_done.at(a.u - 1))
                for par in range(2):
                    r = slice(par * N, (par + 1) * N)
                    dve.reciprocal(recip[r, b, :], o_ps[r, b, :, par * VW + D0]).then_inc(recip_done.sem, 1)
                dve.wait_ge(recip_done.sem, recip_done.at(a.u, 2 * b + 2))
                for par in range(2):
                    r = slice(par * N, (par + 1) * N)
                    dve.tensor_tensor(o[r, b, :, :], o_ps[r, b, :, par * VW:par * VW + D0],
                                      recip[r, b, :].unsqueeze(2).to_broadcast([N, PAIRS, D0]),
                                      ALU.mult).then_inc(o_done.sem, 1)

            def step(at, on):
                if on(0):
                    a = at(0)
                    dve.wait_ge(xnT_ps_done.sem, xnT_ps_done.at(a.u - 2))
                    dve.tensor_scalar(xn[:, a.slot, :], x[:, bass.ds(a.u, 1), :].rearrange("p a f -> p (a f)"),
                                      mean[:, bass.ds(a.u, 1)], rstd[:, bass.ds(a.u, 1)],
                                      ALU.subtract, ALU.mult).then_inc(xn_done.sem, 1)
                if on(2):
                    shift(at(2), 0)
                if on(4):
                    a = at(4)
                    xu = x[:, bass.ds(a.u, 1), :].rearrange("p a f -> p (a f)")
                    dve.wait_ge(y_done.sem, y_done.at(a.u))
                    dve.wait_ge(biased.sem, biased.at(a.u))
                    dve.tensor_tensor(xu, y_ps, xu, ALU.add).then_inc(resid_done.sem, 1)
                    dve.wait_ge(resid_done.sem, resid_done.at(a.u))
                    dve.bn_stats(stats[:, bass.ds(a.u, 1), :].rearrange("p a s -> p (a s)"), xu)
                if on(2):
                    shift(at(2), 1)
                if on(3):
                    normalise(at(3), 1)
                if on(2):
                    normalise(at(2), 0)

            pipeline(dve, UNITS, DEPTH, step, 4)


def split_weights(nc, ctx, tag, jobs):
    STAGE, SLOTS = max(src.shape[1] for _, _, src in jobs), 3
    raw = ctx.enter_context(nc.sbuf_tensor(f"{tag}_raw", [P, SLOTS, STAGE], F32))
    landed = [ctx.sem(f"{tag}_w_landed{s}") for s in range(SLOTS)]
    hi_made = ctx.sem(f"{tag}_w_hi")
    split = ctx.sem(f"{tag}_w_split")

    def sync(sp):
        for i, (hi, lo, src) in enumerate(jobs):
            rows, n = src.shape
            if i >= SLOTS:
                sp.wait_ge(split, i - SLOTS + 1)
            sp.dma_start(raw[0:rows, i % SLOTS, 0:n], src).then_inc(landed[i % SLOTS], 16)

    def scalar(act):
        for i, (hi, lo, src) in enumerate(jobs):
            rows, n = src.shape
            act.wait_ge(landed[i % SLOTS], 16 * (i // SLOTS + 1))
            act.activation(hi, raw[0:rows, i % SLOTS, 0:n], ACT.Copy).then_inc(hi_made, 1)

    def rest(eng):
        for i, (hi, lo, src) in enumerate(jobs):
            rows, n = src.shape
            eng.wait_ge(hi_made, i + 1)
            eng.tensor_tensor(lo, raw[0:rows, i % SLOTS, 0:n], hi.bitcast(F32), ALU.subtract).then_inc(split, 1)

    return sync, scalar, rest, split


def pieces(hi, lo, src, most=1024):
    n = src.shape[1]
    return [(hi[:, i:min(i + most, n)], lo[:, i:min(i + most, n)], src[:, i:min(i + most, n)])
            for i in range(0, n, most)]


def experts(nc, x, stats, ident, a, shared, out):
    tag = "d_" if shared else "b_"
    CH = 4 if shared else 3
    R = 512 // CH if shared else 336 // CH
    NE = E + 1 if shared else E
    FIRST = NE - E
    S = NE * CH
    MATS = 1 if shared else 2
    ZS = 4 // MATS
    LAG = 5 if shared else 4
    WEIGH = LAG + 1
    HF, HS = 4, 6
    CS = 4
    AH = 50
    KMAX = 6
    hook = {name: p * S // 24 for name, p in dict(xT=3, router=6, hidden=9, logits=12, scT=19, finish=22).items()}
    hook.update(rank=hook["hidden"] + 1, count=hook["logits"] + 1, choose=hook["logits"] + 2,
                hi_score=hook["logits"] + 4, split_score=hook["logits"] + 5)

    with stage(nc) as ctx:
        def sb(name, shape, dt=F32):
            return ctx.enter_context(nc.sbuf_tensor(tag + name, shape, dt))

        def ps(name, shape):
            return ctx.enter_context(nc.psum_tensor(tag + name, shape, F32))

        def sem(name):
            return ctx.sem(tag + name)

        def mark(name, per=1):
            return Mark(ctx, nc, tag + name, per)

        w_hi, w_lo = (sb(f"w_{n}", [P, MATS, S, R], F32R) for n in ("hi", "lo"))
        wd_hi, wd_lo = (sb(f"wd_{n}", [P, S, C], F32R) for n in ("hi", "lo"))
        rw_hi, rw_lo = (sb(f"rw_{n}", [P, E], F32R) for n in ("hi", "lo"))
        sel_hi, sel_lo = (sb(f"sel_{n}", [P, E, P], F32R) for n in ("hi", "lo"))
        before = sb("before", [P, E, E])
        mean, rstd = sb("mean", [P, UNITS]), sb("rstd", [P, UNITS])
        xn = sb("xn", [P, GROUP, C])
        xf = sb("xf", [P, COLS])
        x_hi, x_lo = (sb(f"x_{n}", [P, 2, COLS], F32R) for n in ("hi", "lo"))
        h = sb("h", [P, HF, COLS])
        h_hi, h_lo = (sb(f"h_{n}", [P, HS, COLS], F32R) for n in ("hi", "lo"))
        cB = sb("cB", [P, CS, COLS])
        part = sb("part", [P, 2, COLS])
        acc = sb("acc", [P, 2, COLS])
        probs = sb("probs", [P, GROUP, E])
        red = sb("red", [P, GROUP])
        inv = sb("inv", [P, GROUP])
        gt, ge = sb("gt", [P, GROUP, E, E]), sb("ge", [P, GROUP, E, E])
        rank = sb("rank", [P, GROUP, E])
        mask = sb("mask", [P, GROUP, E])
        score = sb("score", [P, GROUP, E])
        score_hi = sb("score_hi", [P, GROUP, E], F32R)
        split_score = sb("split_score", [P, GROUP, P])
        scT = sb("scT", [P, 2, COLS], F32R)
        if shared:
            norm_w = sb("norm_w", [P, 1])
            b1, b2 = sb("b1", [P, S]), sb("b2", [P, NE])
            small = ((norm_w[:, :], a["d_norm"]), (b1[:, :], a["d_b1"]), (b2[:, :], a["d_b2"]))
        else:
            sg = sb("sg", [P, 2, COLS])
            aw_hi, aw_lo = (sb(f"aw_{n}", [P, P], F32R) for n in ("hi", "lo"))
            ab1, aw2, ab2 = sb("ab1", [AH, 1]), sb("aw2", [AH, KMAX]), sb("ab2", [P, KMAX])
            kcode = sb("kcode", [P, KMAX])
            ah = sb("ah", [AH, COLS])
            al, amax = sb("al", [P, GROUP, KMAX]), sb("amax", [P, GROUP])
            small = ((ab1[:, :], a["b_ab1"]), (aw2[:, :], a["b_aw2T"]), (ab2[:, :], a["b_ab2"]),
                     (kcode[:, :], a["kcode"]))
        small += ((before[:, :, :], a["before"]),)

        z_ps = ps("z", [P, MATS, ZS, COLS])
        y_ps = ps("y", [P, 2, COLS])
        t_ps = ps("t", [P, COLS])
        c_ps = ps("c", [P, COLS])

        loaded, zeroed = sem("loaded"), sem("zeroed")
        xn_done, xT_ps_done, xf_done, xhi_done, xlo_done = (mark(n) for n in ("xn", "xT_ps", "xf", "xhi", "xlo"))
        router_done, soft_done = mark("router"), mark("soft")
        hidden_done, gelu_done, logits_done, al_done = (mark(n) for n in ("hidden", "gelu", "logits", "al"))
        exp_done, scored, scT_ps_done, scT_done = (mark(n) for n in ("exp", "scored", "scT_ps", "scT"))
        hi_scored, max_done = mark("hi_scored"), mark("max")
        STEPS_R = 11 if shared else 16
        r_step = mark("r_step", STEPS_R)
        z_done, sg_done, h_done, hi_done = (mark(n, S) for n in ("z", "sg", "h", "hi"))
        lo_pool, lo_dve = mark("lo_pool", S // 2), mark("lo_dve", S // 2)
        down_done = mark("down", S)
        c_ps_done, cB_done = mark("c_ps", E), mark("cB", E)
        weighed, added = mark("weighed", NE), mark("added", NE - 1)
        fin_ps_done, resid_done = mark("fin_ps"), mark("resid")
        stored = sem("stored")
        vec_stats, act_stats, stats_ready = finish_stats(nc, ctx, tag + "s", stats, mean, rstd, shared)

        jobs = pieces(rw_hi[:, :], rw_lo[:, :], a[tag + "rw"])
        jobs += pieces(sel_hi[:, :, :].rearrange("p e c -> p (e c)"), sel_lo[:, :, :].rearrange("p e c -> p (e c)"), a["sel"])
        if not shared:
            jobs += pieces(aw_hi[:, :], aw_lo[:, :], a["b_aw1T"])
        PREP_JOBS = len(jobs)
        flat = lambda t, m: t[:, m, :, :].rearrange("p s r -> p (s r)")
        down_flat = lambda t: t[0:R, :, :].rearrange("p s c -> p (s c)")
        for q in range(3):
            lo_c, hi_c = q * S * R // 3, (q + 1) * S * R // 3
            for m in range(MATS):
                jobs += pieces(flat(w_hi, m)[:, lo_c:hi_c], flat(w_lo, m)[:, lo_c:hi_c], a[tag + "w"][m][:, lo_c:hi_c])
            lo_c, hi_c = q * S * C // 3, (q + 1) * S * C // 3
            jobs += pieces(down_flat(wd_hi)[:, lo_c:hi_c], down_flat(wd_lo)[:, lo_c:hi_c], a[tag + "wd"][:, lo_c:hi_c])
        load_w, hi_w, lo_w, split = split_weights(nc, ctx, tag + "sw", jobs)

        DEPTH = 2
        block = ctx.block()

        def y_slot(g, e):
            return (g.slot * NE + e) % 2

        def behind(at, on, s, lag):
            n = 1 if s >= lag else 2
            return (at(n), (s - lag) % S) if on(n) else None

        def wait_lo(eng, g, s):
            m = lo_dve if s % 2 else lo_pool
            eng.wait_ge(m.sem, m.at(g.u, s // 2 + 1))

        def unit_tiles(g):
            return x[:, bass.ds(g.u * GROUP, GROUP), :]

        @block.sync
        def _(sp):
            for dst, src in small:
                sp.dma_start(dst, src).then_inc(loaded, 16)
            load_w(sp)
            if shared:
                def step(at, on):
                    if on(0):
                        g = at(0)
                        sp.wait_ge(resid_done.sem, resid_done.at(g.u))
                        sp.dma_start(out[bass.ds(g.u * COLS, COLS), :].rearrange("(u p) f -> p u f", p=P),
                                     unit_tiles(g)).then_inc(stored, 16)
                pipeline(sp, GROUPS, 0, step)
                sp.wait_ge(stored, 16 * GROUPS)

        @block.gpsimd
        def _(pool):
            for m in (lo_pool, added):
                m.credit(pool)
            pool.memset(split_score[:, :, :], 0.0).then_inc(zeroed, 1)
            lo_w(pool)

            def step(at, on):
                for s in range(S):
                    if s % 2 == 0 and on(1):
                        g = at(1)
                        pool.wait_ge(hi_done.sem, hi_done.at(g.u, s + 1))
                        pool.wait_ge(down_done.sem, down_done.at(g.u, s + 1 - HS))
                        pool.tensor_tensor(h_lo[0:R, s % HS, :], h[0:R, s % HF, :],
                                           h_hi[0:R, s % HS, :].bitcast(F32), ALU.subtract).then_inc(lo_pool.sem, 1)
                    found = behind(at, on, s, LAG + CH)
                    if found and found[1] % CH == 0 and found[1]:
                        g, e = found[0], found[1] // CH
                        pool.wait_ge(added.sem, added.at(g.u, e - 1))
                        pool.wait_ge(weighed.sem, weighed.at(g.u, e + 1))
                        pool.tensor_tensor(acc[:, g.slot, :], acc[:, g.slot, :], part[:, y_slot(g, e), :],
                                           ALU.add).then_inc(added.sem, 1)

            pipeline(pool, GROUPS, DEPTH, step)

        @block.scalar
        def _(act):
            for m in (xf_done, xhi_done, gelu_done, exp_done, hi_scored, scT_done, sg_done, hi_done, cB_done):
                m.credit(act)
            act_stats(act)
            hi_w(act)

            def step(at, on):
                for s in range(S):
                    prev = behind(at, on, s, 1)
                    if prev:
                        g, q = prev
                        act.wait_ge(h_done.sem, h_done.at(g.u, q + 1))
                        act.wait_ge(down_done.sem, down_done.at(g.u, q + 1 - HS))
                        act.activation(h_hi[0:R, q % HS, :], h[0:R, q % HF, :], ACT.Copy).then_inc(hi_done.sem, 1)
                    if on(1) and not shared:
                        g = at(1)
                        act.wait_ge(z_done.sem, z_done.at(g.u, s + 1))
                        act.wait_ge(h_done.sem, h_done.at(g.u, s - 1))
                        act.activation(sg[0:R, s % 2, :], z_ps[0:R, 0, s % ZS, :], ACT.Silu).then_inc(sg_done.sem, 1)
                    if on(1) and s % CH == 0 and s // CH >= FIRST:
                        g, r = at(1), s // CH - FIRST
                        act.wait_ge(c_ps_done.sem, c_ps_done.at(g.u, r + 1))
                        act.wait_ge(weighed.sem, weighed.at(g.u, r + FIRST + 1 - CS))
                        act.activation(cB[:, r % CS, :], c_ps[:, :], ACT.Copy).then_inc(cB_done.sem, 1)
                    if not on(0):
                        continue
                    g = at(0)
                    if s == hook["xT"]:
                        act.wait_ge(xT_ps_done.sem, xT_ps_done.at(g.u))
                        act.wait_ge(xlo_done.sem, xlo_done.at(g.u - 1))
                        act.activation(xf[:, :], t_ps[:, :], ACT.Copy,
                                       scale=norm_w[:, 0:1] if shared else 1.0).then_inc(xf_done.sem, 1)
                        act.wait_ge(xf_done.sem, xf_done.at(g.u))
                        act.wait_ge(z_done.sem, z_done.at(g.u - 2))
                        act.activation(x_hi[:, g.slot, :], xf[:, :], ACT.Copy).then_inc(xhi_done.sem, 1)
                    if s == hook["router"] and shared:
                        act.wait_ge(router_done.sem, router_done.at(g.u))
                        act.wait_ge(scored.sem, scored.at(g.u - 1))
                        act.activation(probs[:, :, :], t_ps[:, 0:GROUP * E].rearrange("p (u e) -> p u e", e=E),
                                       ACT.Sigmoid).then_inc(exp_done.sem, 1)
                    if s == hook["hidden"] and not shared:
                        act.wait_ge(hidden_done.sem, hidden_done.at(g.u))
                        act.wait_ge(logits_done.sem, logits_done.at(g.u - 1))
                        act.activation(ah[:, :], t_ps[0:AH, :], ACT.Gelu_apprx_tanh,
                                       bias=ab1[:, 0:1]).then_inc(gelu_done.sem, 1)
                        act.wait_ge(soft_done.sem, soft_done.at(g.u))
                        act.activation(probs[:, :, :], probs[:, :, :], ACT.Exp).then_inc(exp_done.sem, 1)
                    if s == hook["hi_score"]:
                        act.wait_ge(r_step.sem, r_step.at(g.u))
                        act.activation(score_hi[:, :, :], score[:, :, :], ACT.Copy).then_inc(hi_scored.sem, 1)
                    if s == hook["scT"]:
                        act.wait_ge(scT_ps_done.sem, scT_ps_done.at(g.u))
                        act.wait_ge(c_ps_done.sem, c_ps_done.at(g.u - 2))
                        act.activation(scT[:, g.slot, :], t_ps[:, :], ACT.Copy).then_inc(scT_done.sem, 1)

            pipeline(act, GROUPS, DEPTH, step)

        @block.tensor
        def _(pe):
            for m in (xT_ps_done, router_done, hidden_done, logits_done, scT_ps_done, z_done, down_done, c_ps_done,
                      fin_ps_done):
                m.credit(pe)
            pe.wait_ge(loaded, 16 * len(small))

            def three(dst, hi, lo, m_hi, m_lo, start=True, stop=True):
                pe.matmul(dst, hi, m_hi, start=start, stop=False)
                pe.matmul(dst, hi, m_lo, start=False, stop=False)
                return pe.matmul(dst, lo, m_hi, start=False, stop=stop)

            def up(g, s):
                pe.wait_ge(h_done.sem, h_done.at(g.u, s + 1 - ZS))
                for m in range(MATS):
                    last = three(z_ps[0:R, m, s % ZS, :], w_hi[:, m, s, :], w_lo[:, m, s, :],
                                 x_hi[:, g.slot, :], x_lo[:, g.slot, :])
                last.then_inc(z_done.sem, 1)

            def down(g, s):
                e = s // CH
                if s % CH == 0:
                    pe.wait_ge(weighed.sem, weighed.at(g.u, e - 1))
                wait_lo(pe, g, s)
                three(y_ps[:, y_slot(g, e), :], wd_hi[0:R, s, :], wd_lo[0:R, s, :], h_hi[0:R, s % HS, :],
                      h_lo[0:R, s % HS, :], s % CH == 0, s % CH == CH - 1).then_inc(down_done.sem, 1)

            def prepare(g, s):
                x_of = lambda t, i: t[:, g.slot, i * P:(i + 1) * P]
                if s == hook["xT"]:
                    pe.wait_ge(xn_done.sem, xn_done.at(g.u))
                    pe.wait_ge(resid_done.sem, resid_done.at(g.u - 3))
                    pe.wait_ge(scT_done.sem, scT_done.at(g.u - 1))
                    for i in range(GROUP):
                        m = pe.transpose(t_ps[:, i * P:(i + 1) * P], xn[:, i, :], ident[:, :])
                    m.then_inc(xT_ps_done.sem, 1)
                if s == hook["router"]:
                    pe.wait_ge(split, PREP_JOBS)
                    pe.wait_ge(xlo_done.sem, xlo_done.at(g.u))
                    for i in range(GROUP):
                        m = three(t_ps[:, i * E:(i + 1) * E], x_of(x_hi, i), x_of(x_lo, i), rw_hi[:, :], rw_lo[:, :])
                    m.then_inc(router_done.sem, 1)
                if s == hook["hidden"] and not shared:
                    pe.wait_ge(soft_done.sem, soft_done.at(g.u))
                    three(t_ps[:, :], aw_hi[:, :], aw_lo[:, :], x_hi[:, g.slot, :], x_lo[:, g.slot, :]
                          ).then_inc(hidden_done.sem, 1)
                if s == hook["logits"] and not shared:
                    pe.wait_ge(gelu_done.sem, gelu_done.at(g.u))
                    for i in range(GROUP):
                        m = pe.matmul(t_ps[:, i * KMAX:(i + 1) * KMAX], ah[:, i * P:(i + 1) * P], aw2[:, :],
                                      start=True, stop=True)
                    m.then_inc(logits_done.sem, 1)
                if s == hook["scT"]:
                    pe.wait_ge(scored.sem, scored.at(g.u))
                    for i in range(GROUP):
                        m = pe.transpose(t_ps[:, i * P:(i + 1) * P], split_score[:, i, :], ident[:, :])
                    m.then_inc(scT_ps_done.sem, 1)

            def step(at, on):
                for s in range(S):
                    if on(0):
                        prepare(at(0), s)
                    if on(2) and s == hook["finish"]:
                        g = at(2)
                        pe.wait_ge(added.sem, added.at(g.u))
                        pe.wait_ge(scT_done.sem, scT_done.at(g.u + 2) if on(0) else scT_done.at(GROUPS - 1))
                        for i in range(GROUP):
                            m = pe.transpose(t_ps[:, i * P:(i + 1) * P], acc[:, g.slot, i * P:(i + 1) * P], ident[:, :])
                        m.then_inc(fin_ps_done.sem, 1)
                    if on(1):
                        g = at(1)
                        if s % CH == 0 and s // CH >= FIRST:
                            r = s // CH - FIRST
                            pe.wait_ge(scT_done.sem, scT_done.at(g.u))
                            pe.wait_ge(cB_done.sem, cB_done.at(g.u, r))
                            pe.matmul(c_ps[:, :], sel_hi[:, r, :], scT[:, g.slot, :], start=True, stop=True
                                      ).then_inc(c_ps_done.sem, 1)
                        if s % (S // 3) == 0:
                            pe.wait_ge(split, PREP_JOBS + (len(jobs) - PREP_JOBS) // 3 * (s // (S // 3) + 1))
                        up(g, s)
                    found = behind(at, on, s, LAG)
                    if found:
                        down(*found)

            pipeline(pe, GROUPS, DEPTH, step)

        @block.vector
        def _(dve):
            for m in (xn_done, xlo_done, soft_done, max_done, al_done, scored, r_step, h_done, lo_dve, weighed, resid_done):
                m.credit(dve)
            vec_stats(dve)
            dve.wait_ge(stats_ready, 1)
            dve.wait_ge(loaded, 16 * len(small))
            dve.wait_ge(zeroed, 1)

            steps_before = (0, 2, 5, 8) if shared else (0, 5, 8, 12)

            def route(g, n):
                count = [steps_before[n]]

                def link(ins):
                    count[0] += 1
                    ins.then_inc(r_step.sem, 1)
                    dve.wait_ge(r_step.sem, r_step.at(g.u, count[0]))

                wide = lambda t: t.unsqueeze(2).to_broadcast([P, GROUP, E])
                by_j = probs[:, :, :].unsqueeze(2).to_broadcast([P, GROUP, E, E])
                by_e = probs[:, :, :].unsqueeze(3).to_broadcast([P, GROUP, E, E])
                first = before[:, :, :].unsqueeze(1).to_broadcast([P, GROUP, E, E])
                if n == 0:
                    dve.wait_ge(exp_done.sem, exp_done.at(g.u))
                    if not shared:
                        link(dve.tensor_reduce(red[:, :], probs[:, :, :], AX.X, ALU.add))
                        link(dve.reciprocal(inv[:, :], red[:, :]))
                        link(dve.tensor_tensor(probs[:, :, :], probs[:, :, :], wide(inv[:, :]), ALU.mult))
                    link(dve.tensor_tensor(ge[:, :, :, :], by_j, by_e, ALU.is_ge))
                    link(dve.tensor_tensor(ge[:, :, :, :], ge[:, :, :, :], first, ALU.mult))
                if n == 1:
                    link(dve.tensor_tensor(gt[:, :, :, :], by_j, by_e, ALU.is_gt))
                    link(dve.tensor_tensor(gt[:, :, :, :], gt[:, :, :, :], ge[:, :, :, :], ALU.max))
                    link(dve.tensor_reduce(rank[:, :, :], gt[:, :, :, :], AX.X, ALU.add))
                if n == 2 and shared:
                    link(dve.tensor_scalar(mask[:, :, :], rank[:, :, :], 2.0, None, ALU.is_lt))
                    link(dve.tensor_tensor(mask[:, :, :], mask[:, :, :], probs[:, :, :], ALU.mult))
                    link(dve.tensor_reduce(red[:, :], mask[:, :, :], AX.X, ALU.add))
                if n == 3 and shared:
                    link(dve.tensor_scalar(red[:, :], red[:, :], 1e-6, None, ALU.add))
                    link(dve.reciprocal(inv[:, :], red[:, :]))
                    dve.tensor_tensor(score[:, :, :], mask[:, :, :], wide(inv[:, :]), ALU.mult).then_inc(r_step.sem, 1)
                wide_k = lambda t: t.unsqueeze(2).to_broadcast([P, GROUP, KMAX])
                over = lambda t: t.unsqueeze(1).to_broadcast([P, GROUP, KMAX])
                if n == 2 and not shared:
                    dve.wait_ge(logits_done.sem, logits_done.at(g.u))
                    dve.tensor_tensor(al[:, :, :], t_ps[:, 0:GROUP * KMAX].rearrange("p (u k) -> p u k", k=KMAX),
                                      over(ab2[:, :]), ALU.add).then_inc(al_done.sem, 1)
                    dve.wait_ge(al_done.sem, al_done.at(g.u))
                    link(dve.tensor_scalar(al[:, :, :], al[:, :, :], -30.0, 30.0, ALU.max, ALU.min))
                    link(dve.tensor_reduce(amax[:, :], al[:, :, :], AX.X, ALU.max))
                    link(dve.tensor_tensor(al[:, :, :], al[:, :, :], wide_k(amax[:, :]), ALU.is_equal))
                    link(dve.tensor_tensor(al[:, :, :], al[:, :, :], over(kcode[:, :]), ALU.mult))
                if n == 3 and not shared:
                    link(dve.tensor_reduce(amax[:, :], al[:, :, :], AX.X, ALU.min))
                    link(dve.tensor_scalar(rank[:, :, :], rank[:, :, :], -100.0, None, ALU.add))
                    link(dve.tensor_tensor(mask[:, :, :], rank[:, :, :], wide(amax[:, :]), ALU.is_lt))
                    dve.tensor_tensor(score[:, :, :], mask[:, :, :], probs[:, :, :], ALU.mult).then_inc(r_step.sem, 1)
                assert n == 3 or count[0] == steps_before[n + 1], (n, count)
                assert n < 3 or count[0] + 1 == STEPS_R, count

            def step(at, on):
                for s in range(S):
                    if on(1):
                        g = at(1)
                        dve.wait_ge(hi_done.sem, hi_done.at(g.u, s + 1 - HF))
                        wait_lo(dve, g, s - HF)
                        if shared:
                            dve.wait_ge(z_done.sem, z_done.at(g.u, s + 1))
                            dve.tensor_scalar(h[:, s % HF, :], z_ps[:, 0, s % ZS, :], b1[:, s:s + 1], 0.0,
                                              ALU.add, ALU.max).then_inc(h_done.sem, 1)
                        else:
                            dve.wait_ge(sg_done.sem, sg_done.at(g.u, s + 1))
                            dve.tensor_tensor(h[0:R, s % HF, :], z_ps[0:R, 1, s % ZS, :], sg[0:R, s % 2, :],
                                              ALU.mult).then_inc(h_done.sem, 1)
                    prev = behind(at, on, s, 1)
                    if prev and prev[1] % 2:
                        g, q = prev
                        dve.wait_ge(hi_done.sem, hi_done.at(g.u, q + 1))
                        dve.wait_ge(down_done.sem, down_done.at(g.u, q + 1 - HS))
                        dve.tensor_tensor(h_lo[0:R, q % HS, :], h[0:R, q % HF, :],
                                          h_hi[0:R, q % HS, :].bitcast(F32), ALU.subtract).then_inc(lo_dve.sem, 1)
                    found = behind(at, on, s, WEIGH)
                    if found and found[1] % CH == CH - 1:
                        g, e = found[0], found[1] // CH
                        yy = y_ps[:, y_slot(g, e), :]
                        dve.wait_ge(down_done.sem, down_done.at(g.u, found[1] + 1))
                        if e >= FIRST:
                            dve.wait_ge(cB_done.sem, cB_done.at(g.u, e - FIRST + 1))
                        if e == 0:
                            dve.wait_ge(fin_ps_done.sem, fin_ps_done.at(g.u - 2))
                            to = acc[:, g.slot, :]
                        else:
                            dve.wait_ge(added.sem, added.at(g.u, max(e - 2, 0)))
                            to = part[:, y_slot(g, e), :]
                        if not shared:
                            m = dve.tensor_tensor(to, yy, cB[:, e % CS, :], ALU.mult)
                        elif e == 0:
                            m = dve.tensor_scalar(to, yy, b2[:, 0:1], None, ALU.add)
                        else:
                            m = dve.scalar_tensor_tensor(out=to, in0=yy, scalar=b2[:, e:e + 1],
                                                         in1=cB[:, (e - FIRST) % CS, :], op0=ALU.add, op1=ALU.mult)
                        m.then_inc(weighed.sem, 1)
                    if on(2) and s == hook["finish"]:
                        g = at(2)
                        dve.wait_ge(fin_ps_done.sem, fin_ps_done.at(g.u))
                        tiles = unit_tiles(g)
                        dve.tensor_tensor(tiles, t_ps[:, :].rearrange("p (u f) -> p u f", f=C), tiles,
                                          ALU.add).then_inc(resid_done.sem, 1)
                        if not shared:
                            dve.wait_ge(resid_done.sem, resid_done.at(g.u))
                            for i in range(GROUP):
                                dve.bn_stats(stats[:, bass.ds(g.u * GROUP + i, 1), :].rearrange("p a s -> p (a s)"),
                                             x[:, bass.ds(g.u * GROUP + i, 1), :].rearrange("p a f -> p (a f)"))
                    if not on(0):
                        continue
                    g = at(0)
                    if s == 0:
                        dve.wait_ge(xT_ps_done.sem, xT_ps_done.at(g.u - 1))
                        for i in range(GROUP):
                            u = g.u * GROUP + i
                            m = dve.tensor_scalar(xn[:, i, :], x[:, bass.ds(u, 1), :].rearrange("p a f -> p (a f)"),
                                                  mean[:, bass.ds(u, 1)], rstd[:, bass.ds(u, 1)],
                                                  ALU.subtract, ALU.mult)
                        m.then_inc(xn_done.sem, 1)
                    if s == hook["xT"]:
                        dve.wait_ge(xhi_done.sem, xhi_done.at(g.u))
                        dve.wait_ge(z_done.sem, z_done.at(g.u - 2))
                        dve.tensor_tensor(x_lo[:, g.slot, :], xf[:, :], x_hi[:, g.slot, :].bitcast(F32),
                                          ALU.subtract).then_inc(xlo_done.sem, 1)
                    if s == hook["router"] and not shared:
                        logit = t_ps[:, 0:GROUP * E].rearrange("p (u e) -> p u e", e=E)
                        dve.wait_ge(router_done.sem, router_done.at(g.u))
                        dve.tensor_reduce(red[:, :], logit, AX.X, ALU.max).then_inc(max_done.sem, 1)
                        dve.wait_ge(max_done.sem, max_done.at(g.u))
                        dve.tensor_tensor(probs[:, :, :], logit, red[:, :].unsqueeze(2).to_broadcast([P, GROUP, E]),
                                          ALU.subtract).then_inc(soft_done.sem, 1)
                    for n, name in enumerate(("hidden", "rank", "count", "choose")):
                        if s == hook[name]:
                            route(g, n)
                    if s == hook["split_score"]:
                        dve.wait_ge(hi_scored.sem, hi_scored.at(g.u))
                        dve.wait_ge(scT_ps_done.sem, scT_ps_done.at(g.u - 1))
                        hi = score_hi[:, :, :].bitcast(F32)
                        dve.tensor_copy(split_score[:, :, 0:E], hi)
                        dve.tensor_tensor(split_score[:, :, E:2 * E], score[:, :, :], hi, ALU.subtract
                                          ).then_inc(scored.sem, 1)

            pipeline(dve, GROUPS, DEPTH, step)


def attention1(nc, x, stats, ident, a):
    with stage(nc) as ctx:
        def sb(name, shape, dt=F32):
            return ctx.enter_context(nc.sbuf_tensor("c_" + name, shape, dt))

        def ps(name, shape):
            return ctx.enter_context(nc.psum_tensor("c_" + name, shape, F32))

        def sem(name):
            return ctx.sem("c_" + name)

        def mark(name, per=1):
            return Mark(ctx, nc, "c_" + name, per)

        def split(name, shape):
            return sb(name + "_hi", shape, F32R), sb(name + "_lo", shape, F32R)

        CC = 2
        INNER = H * D1
        KW = N + 2
        wq_hi, wq_lo = split("wq", [P, PAIRS, P])
        wk_hi, wk_lo = split("wk", [P, CC, PAIRS, P])
        wv_hi, wv_lo = split("wv", [P, CC, INNER])
        wo_hi, wo_lo = split("wo", [P, PAIRS, C])
        ln_w, ln_b = sb("ln_w", [P, C]), sb("ln_b", [P, C])
        mean, rstd = sb("mean", [P, UNITS]), sb("rstd", [P, UNITS])
        xn = sb("xn", [P, GROUP, C])
        x_hi, x_lo = split("x", [P, GROUP, P])
        craw = sb("craw", [P, CC, COLS])
        c_hi, c_lo = split("c", [P, CC, GROUP, P])
        qx = sb("qx", [P, GROUP, PAIRS, 2, 2, N])
        kx = sb("kx", [P, GROUP, PAIRS, 2 * KW])
        v = sb("v", [P, 2, 2, INNER])
        top, total, recip = (sb(n, [P, 2, PAIRS]) for n in ("top", "total", "recip"))
        prob = sb("prob", [P, 2, PAIRS, P])
        probT = sb("probT", [P, 2, PAIRS, P])
        oT_hi, oT_lo = split("oT", [P, PAIRS, 2, N])
        y_sb = sb("y_sb", [P, GROUP, C])
        y_stats, y_agg = sb("y_stats", [P, 6]), sb("y_agg", [P, GROUP, 2])
        y_var, y_root, y_rstd = (sb(n, [P, GROUP]) for n in ("y_var", "y_root", "y_rstd"))
        scratch, zero = sb("scratch", [P, 1]), sb("zero", [P, 1])

        s_ps = ps("s", [P, 2, PAIRS, P])
        p_ps = ps("p", [P, 2, COLS])
        t_ps = ps("t", [P, 512])
        o_ps = ps("o", [P, PAIRS, N])
        xT_ps, y_ps = t_ps[:, 0:P], t_ps[:, 128:128 + C]

        small = ((ln_w[:, :], a["c_ln_w"]), (ln_b[:, :], a["c_ln_b"]))
        late = [(kx[:, j, :, N:N + 2], a["c_null_k"]) for j in range(GROUP)]
        late += [(v[row:row + 1, s, b, :], a["c_null_v"]) for s in range(2) for b, row in ((0, N), (1, N - 1))]
        late = tuple(late)
        loaded, late_loaded, zeroed, c_in = sem("loaded"), sem("late_loaded"), sem("zeroed"), sem("c_in")
        xn_done, xT_done, xhi_done, xlo_done = mark("xn"), mark("xT", 4), mark("xhi", 4), mark("xlo", 4)
        chi_done, clo_done = mark("chi", 4), mark("clo", 4)
        q_done, k_done, v_done = mark("q", PAIRS), mark("k", PAIRS), mark("v", 8)
        q_act, q_dve, k_out = mark("q_act", PAIRS), mark("q_dve", PAIRS), mark("k_out", PAIRS)
        v_act, v_dve = mark("v_act", 8), mark("v_dve", 8)
        scores_done, max_done, sub_done, exp_done = mark("scores", 8), mark("max", 8), mark("sub", 8), mark("exp", 8)
        sum_done, recip_done, prob_done = mark("sum", 8), mark("recip", 8), mark("prob", 8)
        turned, probT_done = mark("turned", 8), mark("probT", 8)
        pv_done, ohi_done, olo_done = mark("pv", 8), mark("ohi", 8), mark("olo", 8)
        y_done, y_read, ln_step = mark("y", 4), mark("y_read", 4), mark("ln_step", 9)
        var_done, root_done, yn_done = mark("var"), mark("root"), mark("yn")
        scaled, resid_done = mark("scaled", 2), mark("resid")
        vec_stats, act_stats, stats_ready = finish_stats(nc, ctx, "c_s", stats, mean, rstd, False)

        flat = lambda t: t.rearrange("p r c -> p (r c)")
        jobs = pieces(flat(wq_hi[:, :, :]), flat(wq_lo[:, :, :]), a["c_wq"], 512)
        for cc in range(CC):
            jobs += pieces(flat(wk_hi[:, cc, :, :]), flat(wk_lo[:, cc, :, :]), a["c_wk"][cc], 512)
        EARLY = len(jobs)
        for cc in range(CC):
            jobs += pieces(wv_hi[:, cc, :], wv_lo[:, cc, :], a["c_wv"][cc], 512)
        jobs += pieces(flat(wo_hi[:, :, :]), flat(wo_lo[:, :, :]), a["c_wo"], 512)
        load_w, hi_w, lo_w, w_split = split_weights(nc, ctx, "c_sw", jobs)

        DEPTH = 2
        block = ctx.block()
        keys = (slice(0, KEYS1), slice(P - KEYS1, P))

        def batch(j, b):
            return 2 * j + b + 1

        def group_x(g):
            return x[:, bass.ds(g.u * GROUP, GROUP), :]

        @block.sync
        def _(sp):
            load_w(sp)
            for dst, src in small:
                sp.dma_start(dst, src).then_inc(loaded, 16)
            sp.wait_ge(zeroed, 4)
            for dst, src in late:
                sp.dma_start(dst, src).then_inc(late_loaded, 16)

            def step(at, on):
                if on(0):
                    g = at(0)
                    sp.wait_ge(clo_done.sem, clo_done.at(g.u - 1))
                    sp.dma_start(craw[:, :, :], a["c_ctxT"][:, :, bass.ds(g.u * COLS, COLS)]).then_inc(c_in, 16)

            turns(sp, GROUPS, DEPTH, step)

        @block.gpsimd
        def _(pool):
            for m in (chi_done, clo_done, prob_done, scaled, resid_done):
                m.credit(pool)
            pool.memset(zero[:, :], 0.0).then_inc(zeroed, 1)
            pool.memset(v[:, :, :, :], 0.0).then_inc(zeroed, 1)
            pool.memset(qx[:, :, :, :, :, :], 0.0).then_inc(zeroed, 1)
            pool.memset(prob[:, :, :, :], 0.0).then_inc(zeroed, 1)
            lo_w(pool)
            pool.wait_ge(zeroed, 4)

            def normalise(g, j, b):
                pool.wait_ge(recip_done.sem, recip_done.at(g.u, batch(j, b)))
                pool.tensor_tensor(prob[:, b, :, keys[b]], prob[:, b, :, keys[b]],
                                   recip[:, b, :].unsqueeze(2).to_broadcast([P, PAIRS, KEYS1]),
                                   ALU.mult).then_inc(prob_done.sem, 1)

            def context(g, j):
                raw = craw[:, :, j * P:(j + 1) * P]
                pool.wait_ge(v_done.sem, v_done.at(g.u - 1, 2 * j + 2))
                pool.wait_ge(k_done.sem, k_done.at(g.u - 1))
                pool.wait_ge(c_in, g.u * 16 + 16)
                pool.tensor_tensor(c_hi[:, :, j, :], raw, zero[:, 0:1].unsqueeze(2).to_broadcast([P, CC, P]),
                                   ALU.subtract).then_inc(chi_done.sem, 1)
                pool.wait_ge(chi_done.sem, chi_done.at(g.u, j + 1))
                pool.tensor_tensor(c_lo[:, :, j, :], raw, c_hi[:, :, j, :].bitcast(F32),
                                   ALU.subtract).then_inc(clo_done.sem, 1)

            def step(at, on):
                for j in range(GROUP):
                    if j == 0 and on(2):
                        g = at(2)
                        wide = lambda t: t[:, :].unsqueeze(1).to_broadcast([P, GROUP, C])
                        pool.wait_ge(loaded, 16 * len(small))
                        pool.wait_ge(yn_done.sem, yn_done.at(g.u))
                        pool.tensor_tensor(y_sb[:, :, :], y_sb[:, :, :], wide(ln_w), ALU.mult).then_inc(scaled.sem, 1)
                        pool.wait_ge(scaled.sem, scaled.at(g.u, 1))
                        pool.tensor_tensor(y_sb[:, :, :], y_sb[:, :, :], wide(ln_b), ALU.add).then_inc(scaled.sem, 1)
                        pool.wait_ge(scaled.sem, scaled.at(g.u))
                        pool.tensor_tensor(group_x(g), group_x(g), y_sb[:, :, :], ALU.add).then_inc(resid_done.sem, 1)
                    for b in range(2):
                        if on(1):
                            normalise(at(1), j, b)
                        if on(0) and j == 1:
                            context(at(0), b)
                    if on(0) and j > 1:
                        context(at(0), j)

            turns(pool, GROUPS, DEPTH, step)

        @block.scalar
        def _(act):
            for m in (xhi_done, q_act, k_out, v_act, exp_done, probT_done, ohi_done, root_done):
                m.credit(act)
            act_stats(act)
            hi_w(act)
            act.wait_ge(zeroed, 4)

            def copy_probs(g, j, b):
                act.wait_ge(turned.sem, turned.at(g.u, batch(j, b)))
                act.wait_ge(pv_done.sem, pv_done.at(g.u, batch(j - 1, b)))
                act.activation(probT[:, b, :, :], s_ps[:, b, :, :], ACT.Copy).then_inc(probT_done.sem, 1)

            def exps(g, j, b):
                act.wait_ge(sub_done.sem, sub_done.at(g.u, batch(j, b)))
                act.activation(prob[:, b, :, keys[b]], prob[:, b, :, keys[b]], ACT.Exp).then_inc(exp_done.sem, 1)

            def output_hi(g, j, b):
                act.wait_ge(pv_done.sem, pv_done.at(g.u, batch(j, b)))
                act.wait_ge(y_done.sem, y_done.at(g.u, j))
                act.activation(oT_hi[:, :, b, :], o_ps[:, :, :], ACT.Copy).then_inc(ohi_done.sem, 1)

            def queries_keys(g, r):
                act.wait_ge(q_done.sem, q_done.at(g.u, r + 1))
                act.wait_ge(scores_done.sem, scores_done.at(g.u - 1))
                act.activation(qx[0:N, :, r, :, 0, :], p_ps[0:N, 0, :].rearrange("p (u b q) -> p u b q", u=GROUP, b=2),
                               ACT.Copy, scale=float(D1) ** -0.5).then_inc(q_act.sem, 1)
                act.wait_ge(k_done.sem, k_done.at(g.u, r + 1))
                act.activation(kx[:, :, r, :].rearrange("p u (b k) -> p u b k", b=2)[:, :, :, 0:N],
                               p_ps[:, 1, :].rearrange("p (u b k) -> p u b k", u=GROUP, b=2), ACT.Copy
                               ).then_inc(k_out.sem, 1)

            def values_out(g, j):
                act.wait_ge(v_done.sem, v_done.at(g.u, 2 * j + 1))
                act.wait_ge(pv_done.sem, pv_done.at(g.u, batch(j - 2, 1)))
                for b in range(2):
                    r = slice(b * N, (b + 1) * N)
                    act.activation(v[r, j % 2, b, 0:512], p_ps[r, 0, :], ACT.Copy).then_inc(v_act.sem, 1)

            def x_part(g, j):
                act.wait_ge(xT_done.sem, xT_done.at(g.u, j + 1))
                act.wait_ge(q_done.sem, q_done.at(g.u - 1))
                act.activation(x_hi[:, j, :], xT_ps, ACT.Copy).then_inc(xhi_done.sem, 1)

            def step(at, on):
                if on(2):
                    output_hi(at(2), 3, 0)
                for r in range(PAIRS):
                    if on(1):
                        queries_keys(at(1), r)
                    if r == 1 and on(2):
                        output_hi(at(2), 3, 1)
                    if r == 5 and on(2):
                        g = at(2)
                        act.wait_ge(var_done.sem, var_done.at(g.u))
                        act.activation(y_root[:, :], y_var[:, :], ACT.Sqrt).then_inc(root_done.sem, 1)
                for j in range(GROUP):
                    if j and on(0):
                        x_part(at(0), j)
                    if j and on(1):
                        output_hi(at(1), j - 1, 0)
                    if on(1):
                        exps(at(1), j, 0)
                        if j:
                            output_hi(at(1), j - 1, 1)
                        else:
                            values_out(at(1), 0)
                        exps(at(1), j, 1)
                        if j < 3:
                            values_out(at(1), j + 1)
                    if j == 0 and on(0):
                        x_part(at(0), 0)
                    if on(1):
                        copy_probs(at(1), j, 0)
                        copy_probs(at(1), j, 1)

            turns(act, GROUPS, DEPTH, step)

        @block.tensor
        def _(pe):
            for m in (xT_done, q_done, k_done, v_done, scores_done, turned, pv_done, y_done):
                m.credit(pe)

            def three(dst, hi, lo, m_hi, m_lo, start=True, stop=True):
                pe.matmul(dst, hi, m_hi, start=start, stop=False)
                pe.matmul(dst, hi, m_lo, start=False, stop=False)
                return pe.matmul(dst, lo, m_hi, start=False, stop=stop)

            def queries_keys(g, r):
                if r == 0:
                    pe.wait_ge(w_split, EARLY)
                    pe.wait_ge(xlo_done.sem, xlo_done.at(g.u))
                    pe.wait_ge(v_act.sem, v_act.at(g.u - 1))
                else:
                    pe.wait_ge(q_act.sem, q_act.at(g.u, r))
                    pe.wait_ge(q_dve.sem, q_dve.at(g.u, r))
                tokens = lambda t: t[:, :, :].rearrange("p u t -> p (u t)")
                three(p_ps[:, 0, :], wq_hi[:, r, :], wq_lo[:, r, :], tokens(x_hi), tokens(x_lo)).then_inc(q_done.sem, 1)
                if r == 0:
                    pe.wait_ge(clo_done.sem, clo_done.at(g.u))
                    pe.wait_ge(v_dve.sem, v_dve.at(g.u - 1))
                else:
                    pe.wait_ge(k_out.sem, k_out.at(g.u, r))
                for cc in range(CC):
                    m = three(p_ps[:, 1, :], wk_hi[:, cc, r, :], wk_lo[:, cc, r, :], tokens(c_hi[:, cc, :, :]),
                              tokens(c_lo[:, cc, :, :]), cc == 0, cc == CC - 1)
                m.then_inc(k_done.sem, 1)

            def v_product(g, j):
                for n in range(2):
                    if j == 0:
                        if n == 0:
                            pe.wait_ge(q_act.sem, q_act.at(g.u))
                            pe.wait_ge(q_dve.sem, q_dve.at(g.u))
                        else:
                            pe.wait_ge(k_out.sem, k_out.at(g.u))
                    else:
                        m = v_dve if n else v_act
                        pe.wait_ge(m.sem, m.at(g.u, 2 * j))
                    for cc in range(CC):
                        cols = slice(n * 512, (n + 1) * 512)
                        m = three(p_ps[:, n, :], c_hi[:, cc, j, :], c_lo[:, cc, j, :],
                                  wv_hi[:, cc, cols], wv_lo[:, cc, cols], cc == 0, cc == CC - 1)
                    m.then_inc(v_done.sem, 1)

            def scores(g, j, b):
                if j == 0 and b == 0:
                    pe.wait_ge(late_loaded, 16 * len(late))
                    pe.wait_ge(q_act.sem, q_act.at(g.u))
                    pe.wait_ge(q_dve.sem, q_dve.at(g.u))
                    pe.wait_ge(k_out.sem, k_out.at(g.u))
                pe.wait_ge(probT_done.sem, probT_done.at(g.u, batch(j - 1, b)))
                first = b * (KW - 1)
                for r in range(PAIRS):
                    m = pe.matmul(s_ps[:, b, r, 0:KEYS1], qx[:, j, r, b, :, :].rearrange("p h q -> p (h q)"),
                                  kx[:, j, r, first:first + KEYS1], start=True, stop=True)
                m.then_inc(scores_done.sem, 1)

            def turn_probs(g, j, b):
                pe.wait_ge(prob_done.sem, prob_done.at(g.u, batch(j, b)))
                for r in range(PAIRS):
                    m = pe.transpose(s_ps[:, b, r, :], prob[:, b, r, :], ident[:, :])
                m.then_inc(turned.sem, 1)

            def values(g, j, b):
                pe.wait_ge(probT_done.sem, probT_done.at(g.u, batch(j, b)))
                pe.wait_ge(v_act.sem, v_act.at(g.u, 2 * j + 2))
                pe.wait_ge(v_dve.sem, v_dve.at(g.u, 2 * j + 2))
                pe.wait_ge(olo_done.sem, olo_done.at(g.u, batch(j, b) - 1))
                for r in range(PAIRS):
                    for par in range(2):
                        h = 2 * r + par
                        m = pe.matmul(o_ps[par * N:(par + 1) * N, r, :], v[:, j % 2, b, h * D1:(h + 1) * D1],
                                      probT[:, b, r, par * N:(par + 1) * N], start=True, stop=True)
                m.then_inc(pv_done.sem, 1)

            def output(g, j, following):
                pe.wait_ge(olo_done.sem, olo_done.at(g.u, batch(j, 1)))
                pe.wait_ge(y_read.sem, y_read.at(g.u, j))
                if following:
                    pe.wait_ge(xlo_done.sem, xlo_done.at(following.u, j + 2))
                for r in range(PAIRS):
                    m = three(y_ps, oT_hi[:, r, :, :].rearrange("p b q -> p (b q)"),
                              oT_lo[:, r, :, :].rearrange("p b q -> p (b q)"), wo_hi[:, r, :], wo_lo[:, r, :],
                              r == 0, r == PAIRS - 1)
                m.then_inc(y_done.sem, 1)

            def turn_x(g, j):
                pe.wait_ge(xn_done.sem, xn_done.at(g.u))
                pe.wait_ge(y_read.sem, y_read.at(g.u - 1, max(j - 1, 0)))
                pe.wait_ge(xlo_done.sem, xlo_done.at(g.u, j))
                pe.transpose(xT_ps, xn[:, j, :], ident[:, :]).then_inc(xT_done.sem, 1)

            def step(at, on):
                if on(2):
                    values(at(2), 3, 0)
                for r in range(PAIRS):
                    if on(1):
                        queries_keys(at(1), r)
                    if r == 1 and on(2):
                        values(at(2), 3, 1)
                    if r == 3 and on(2):
                        output(at(2), 3, None)
                for j in range(GROUP):
                    if on(1):
                        scores(at(1), j, 0)
                    if j and on(0):
                        turn_x(at(0), j)
                    if on(1):
                        if j:
                            values(at(1), j - 1, 0)
                        scores(at(1), j, 1)
                        if j:
                            values(at(1), j - 1, 1)
                        else:
                            pe.wait_ge(w_split, len(jobs))
                            v_product(at(1), 0)
                        if j < 3:
                            v_product(at(1), j + 1)
                        if j:
                            output(at(1), j - 1, at(0) if on(0) else None)
                    if j == 0 and on(0):
                        turn_x(at(0), 0)
                    if on(1):
                        turn_probs(at(1), j, 0)
                        turn_probs(at(1), j, 1)

            turns(pe, GROUPS, DEPTH, step)

        @block.vector
        def _(dve):
            for m in (xn_done, xlo_done, q_dve, v_dve, max_done, sub_done, sum_done, recip_done, olo_done, y_read,
                      ln_step, var_done, yn_done):
                m.credit(dve)
            vec_stats(dve)
            dve.wait_ge(stats_ready, 1)
            dve.wait_ge(zeroed, 4)

            def shift(g, j, b):
                raw = s_ps[:, b, :, 0:KEYS1]
                n = batch(j, b)
                dve.wait_ge(scores_done.sem, scores_done.at(g.u, n))
                dve.tensor_reduce(top[:, b, :], raw, AX.X, ALU.max).then_inc(max_done.sem, 1)
                dve.wait_ge(max_done.sem, max_done.at(g.u, n))
                dve.wait_ge(turned.sem, turned.at(g.u, batch(j - 1, b)))
                dve.tensor_tensor(prob[:, b, :, keys[b]], raw, top[:, b, :].unsqueeze(2).to_broadcast([P, PAIRS, KEYS1]),
                                  ALU.subtract).then_inc(sub_done.sem, 1)

            def denominators(g, j, b):
                n = batch(j, b)
                dve.wait_ge(exp_done.sem, exp_done.at(g.u, n))
                dve.tensor_reduce(total[:, b, :], prob[:, b, :, keys[b]], AX.X, ALU.add).then_inc(sum_done.sem, 1)
                dve.wait_ge(sum_done.sem, sum_done.at(g.u, n))
                dve.wait_ge(prob_done.sem, prob_done.at(g.u, batch(j - 1, b)))
                dve.reciprocal(recip[:, b, :], total[:, b, :]).then_inc(recip_done.sem, 1)

            def output_lo(g, j, b):
                dve.wait_ge(ohi_done.sem, ohi_done.at(g.u, batch(j, b)))
                dve.tensor_tensor(oT_lo[:, :, b, :], o_ps[:, :, :], oT_hi[:, :, b, :].bitcast(F32),
                                  ALU.subtract).then_inc(olo_done.sem, 1)

            def queries(g, r):
                dve.wait_ge(q_done.sem, q_done.at(g.u, r + 1))
                dve.wait_ge(scores_done.sem, scores_done.at(g.u - 1))
                dve.tensor_scalar(qx[N:P, :, r, :, 1, :], p_ps[N:P, 0, :].rearrange("p (u b q) -> p u b q", u=GROUP, b=2),
                                  float(D1) ** -0.5, None, ALU.mult).then_inc(q_dve.sem, 1)

            def values_out(g, j):
                dve.wait_ge(v_done.sem, v_done.at(g.u, 2 * j + 2))
                dve.wait_ge(pv_done.sem, pv_done.at(g.u, batch(j - 2, 1)))
                for b in range(2):
                    r = slice(b * N, (b + 1) * N)
                    dve.tensor_copy(v[r, j % 2, b, 512:1024], p_ps[r, 1, :]).then_inc(v_dve.sem, 1)

            def y_out(g, j):
                dve.wait_ge(y_done.sem, y_done.at(g.u, j + 1))
                dve.bn_stats(y_stats[:, :], y_ps).then_inc(ln_step.sem, 1)
                dve.wait_ge(ln_step.sem, ln_step.at(g.u, 2 * j + 1))
                dve.memset(scratch[:, :], 0.0)
                dve.bn_aggr(y_agg[:, j, :], y_stats[:, :]).then_inc(ln_step.sem, 1)
                dve.wait_ge(resid_done.sem, resid_done.at(g.u - 1))
                dve.tensor_copy(y_sb[:, j, :], y_ps).then_inc(y_read.sem, 1)

            def step(at, on):
                if on(2):
                    output_lo(at(2), 3, 0)
                if on(0):
                    g = at(0)
                    dve.wait_ge(xT_done.sem, xT_done.at(g.u - 1))
                    for j in range(GROUP):
                        u = g.u * GROUP + j
                        m = dve.tensor_scalar(xn[:, j, :], x[:, bass.ds(u, 1), :].rearrange("p a f -> p (a f)"),
                                              mean[:, bass.ds(u, 1)], rstd[:, bass.ds(u, 1)],
                                              ALU.subtract, ALU.mult)
                    m.then_inc(xn_done.sem, 1)
                for r in range(PAIRS):
                    if on(1):
                        queries(at(1), r)
                    if r == 1 and on(2):
                        output_lo(at(2), 3, 1)
                    if r == 4 and on(2):
                        g = at(2)
                        y_out(g, 3)
                        dve.wait_ge(ln_step.sem, ln_step.at(g.u, 8))
                        dve.tensor_scalar(y_var[:, :], y_agg[:, :, 1], 1e-6, None, ALU.add).then_inc(var_done.sem, 1)
                    if r == 6 and on(2):
                        g = at(2)
                        dve.wait_ge(root_done.sem, root_done.at(g.u))
                        dve.reciprocal(y_rstd[:, :], y_root[:, :]).then_inc(ln_step.sem, 1)
                        dve.wait_ge(ln_step.sem, ln_step.at(g.u))
                        dve.wait_ge(y_read.sem, y_read.at(g.u))
                        for j in range(GROUP):
                            m = dve.tensor_scalar(y_sb[:, j, :], y_sb[:, j, :], y_agg[:, j, 0:1], y_rstd[:, j:j + 1],
                                                  ALU.subtract, ALU.mult)
                        m.then_inc(yn_done.sem, 1)
                for j in range(GROUP):
                    if on(1):
                        shift(at(1), j, 0)
                    if j and on(0):
                        x_lo_part(dve, at(0), j)
                    if on(1):
                        g = at(1)
                        if j:
                            output_lo(g, j - 1, 0)
                        shift(g, j, 1)
                        denominators(g, j, 0)
                        if j:
                            output_lo(g, j - 1, 1)
                        else:
                            values_out(g, 0)
                        denominators(g, j, 1)
                        if j < 3:
                            values_out(g, j + 1)
                        if j:
                            y_out(g, j - 1)
                    if j == 0 and on(0):
                        x_lo_part(dve, at(0), 0)
                    if j == 2 and on(2):
                        g = at(2)
                        dve.wait_ge(resid_done.sem, resid_done.at(g.u))
                        for i in range(GROUP):
                            u = g.u * GROUP + i
                            dve.bn_stats(stats[:, bass.ds(u, 1), :].rearrange("p a s -> p (a s)"),
                                         x[:, bass.ds(u, 1), :].rearrange("p a f -> p (a f)"))

            def x_lo_part(dve, g, j):
                dve.wait_ge(xhi_done.sem, xhi_done.at(g.u, j + 1))
                dve.wait_ge(q_done.sem, q_done.at(g.u - 1))
                dve.tensor_tensor(x_lo[:, j, :], xT_ps, x_hi[:, j, :].bitcast(F32),
                                  ALU.subtract).then_inc(xlo_done.sem, 1)

            turns(dve, GROUPS, DEPTH, step)


def program(nc, a, out):
    with ExitStack() as ctx:
        x = ctx.enter_context(nc.sbuf_tensor("x_resid", [P, UNITS, C], F32))
        stats = ctx.enter_context(nc.sbuf_tensor("x_stats", [P, UNITS, 6], F32))
        ident = ctx.enter_context(nc.sbuf_tensor("identity", [P, P], F32))
        headmask = ctx.enter_context(nc.sbuf_tensor("headmask", [P, H], F32))
        attention0(nc, x, stats, ident, headmask, a["x"], a["a_wqkvT"], a["a_wprojT"], a["a_bproj"],
                   a["a_ctx_kT"], a["a_ctx_v"], a)
        experts(nc, x, stats, ident, a, False, out)
        attention1(nc, x, stats, ident, a)
        experts(nc, x, stats, ident, a, True, out)


def layout(inp):
    f = lambda n: np.asarray(inp[n])
    x, c = f("x"), f("ctx_2048")
    d = {"x": x.reshape(B * N, C)}
    d["a_wqkvT"] = f("L0_xattn_w_qkv").reshape(3, P, C).transpose(2, 0, 1)
    wp = f("L0_xattn_w_proj").T.reshape(PAIRS, 2, D0, C).transpose(0, 2, 1, 3).reshape(N, 2, C)
    d["a_wprojT"] = np.concatenate([wp, wp])
    d["a_bproj"] = np.broadcast_to(f("L0_xattn_b_proj"), (P, C))
    d["a_ctx_kT"] = c[:, :, :C].reshape(B * N, C).T
    v = c[:, :, C:].reshape(UNITS, 2, N, C)[:, ::-1]
    d["a_ctx_v"] = v.reshape(UNITS, P, C).transpose(1, 0, 2).reshape(P, UNITS * C)
    gate, up = (f(n).reshape(E * 336, C).T for n in ("L0_ffn_gate_w", "L0_ffn_up_w"))
    d["b_w"] = np.stack([gate, up])
    d["b_wd"] = f("L0_ffn_down_w").transpose(0, 2, 1).reshape(E * 3, 112, C).transpose(1, 0, 2).reshape(112, -1)
    d["b_rw"] = f("L0_ffn_router_w").T
    aw1 = np.zeros((C, P), np.float32)
    aw1[:, :50] = f("L0_ffn_actor_w1").T
    d["b_aw1T"] = aw1
    d["b_ab1"] = f("L0_ffn_actor_b1").reshape(50, 1)
    d["b_aw2T"] = f("L0_ffn_actor_w2").T
    d["b_ab2"] = np.broadcast_to(f("L0_ffn_actor_b2"), (P, 6))
    d["kcode"] = np.broadcast_to(np.arange(1, 7, dtype=np.float32) - 100, (P, 6))
    d["before"] = np.broadcast_to(np.tril(np.ones((E, E), np.float32), -1), (P, E, E))
    sel = np.zeros((P, E, P), np.float32)
    for e in range(E):
        sel[e, e] = sel[E + e, e] = 1
    d["sel"] = sel.reshape(P, E * P)
    d["c_wq"] = f("L1_xattn_Wq")
    wkv = f("L1_xattn_Wkv").reshape(2, P, 2, H * 64)
    d["c_wk"], d["c_wv"] = wkv[:, :, 0], wkv[:, :, 1]
    d["c_wo"] = f("L1_xattn_Wout").reshape(PAIRS, P, C).transpose(1, 0, 2).reshape(P, PAIRS * C)
    null = f("L1_xattn_null_kv")
    d["c_null_k"] = np.broadcast_to(np.tile(null[0], 2)[:, None, None], (P, PAIRS, 2))
    d["c_null_v"] = np.tile(null[1], H)[None]
    d["c_ln_w"] = np.broadcast_to(f("L1_xattn_ln_scale"), (P, C))
    d["c_ln_b"] = np.broadcast_to(f("L1_xattn_ln_bias"), (P, C))
    d["c_ctxT"] = c.reshape(B * N, 2, P).transpose(2, 1, 0)
    w1 = np.concatenate([f("L1_ffn_sw1")[None], f("L1_ffn_ew1")])
    w2 = np.concatenate([f("L1_ffn_sw2")[None], f("L1_ffn_ew2")])
    d["d_w"] = w1.transpose(1, 0, 2).reshape(1, P, -1)
    d["d_wd"] = w2.reshape((E + 1) * 4, P, C).transpose(1, 0, 2).reshape(P, -1)
    d["d_rw"] = f("L1_ffn_router_w").T
    d["d_b1"] = np.concatenate([f("L1_ffn_sb1")[None], f("L1_ffn_eb1")]).reshape((E + 1) * 4, P).T
    d["d_b2"] = np.concatenate([f("L1_ffn_sb2")[None], f("L1_ffn_eb2")]).T
    d["d_norm"] = f("L1_ffn_norm_weight").reshape(P, 1)
    d["ident"] = np.eye(P, dtype=np.float32)
    d["headmask"] = np.repeat(np.eye(H, dtype=np.float32), D0, axis=0)
    return {k: np.ascontiguousarray(v) for k, v in d.items()}


def kernel(**inputs):
    import concourse.bacc as bacc
    from concourse.bass_utils import run_bass_kernel_spmd

    nc = bacc.Bacc("TRN2", target_bir_lowering=False, num_devices=1)
    arrays = {f"in_{k}_dram": v for k, v in layout(inputs).items()}
    args = {k[3:-5]: nc.dram_tensor(k, v.shape, mybir.dt.from_np(v.dtype), kind="ExternalInput").ap()
            for k, v in arrays.items()}
    out = nc.dram_tensor("out_dram", (B * N, C), F32, kind="ExternalOutput").ap()
    program(nc, args, out)
    got = run_bass_kernel_spmd(nc, [arrays], core_ids=[0])
    return got.results[0]["out_dram"].reshape(B, N, C)
```

```python
from contextlib import ExitStack, contextmanager

import numpy as np

import concourse.bass as bass
from concourse import mybir

F32 = mybir.dt.float32
F32R = mybir.dt.float32r
ALU = mybir.AluOpType
ACT = mybir.ActivationFunctionType
AX = mybir.AxisListType

P = 128
B, N, C = 64, 64, 128
UNITS = B * N // P
GROUP = 4
GROUPS = UNITS // GROUP
COLS = GROUP * P
H = 16
PAIRS = H // 2
D0, D1 = 8, 64
KEYS0 = 2 * N
KEYS1 = N + 1
VW = D0 + 1
E = 8
LN_EPS = 1e-5


@contextmanager
def stage(nc):
    with ExitStack() as ctx:
        taken = []
        ctx.sem = lambda name: taken.append(ctx.enter_context(nc.semaphore(name))) or taken[-1]
        with ExitStack() as blocks:
            ctx.block = lambda: blocks.enter_context(nc.Block())
            yield ctx
        with nc.Block() as block:
            @block.sync
            def _(sp):
                for s in taken:
                    sp.sem_clear(s)


class Mark:

    def __init__(self, ctx, nc, name, per=1):
        self.sem, self.per = ctx.sem(name), per

    def credit(self, eng):
        eng.sem_inc(self.sem, 2 * self.per)

    def at(self, u, j=None):
        return u * self.per + (2 * self.per + (self.per if j is None else j))


class At:

    def __init__(self, k, j, lag, width):
        m = j - lag
        self.u, self.half = width * k + m, width // 2 * k + m // 2
        self.slot, self.slot4 = m % 2, m % 4


def pipeline(eng, units, depth, step, width=2):
    for t in range(depth):
        step(lambda lag, t=t: At(t // width, t % width, lag, width), lambda lag, t=t: t - lag >= 0)
    with eng.Fori(depth // width, units // width) as k:
        for j in range(width):
            step(lambda lag, j=j: At(k, j, lag, width), lambda lag: True)
    for t in range(units, units + depth):
        step(lambda lag, t=t: At(t // width, t % width, lag, width), lambda lag, t=t: t - lag < units)


class Turn:

    def __init__(self, k, lag):
        self.u = k - lag


def turns(eng, groups, depth, step):
    for t in range(depth):
        step(lambda lag, t=t: Turn(t, lag), lambda lag, t=t: t - lag >= 0)
    with eng.Fori(depth, groups) as k:
        step(lambda lag: Turn(k, lag), lambda lag: True)
    for t in range(groups, groups + depth):
        step(lambda lag, t=t: Turn(t, lag), lambda lag, t=t: t - lag < groups)


def finish_stats(nc, ctx, tag, stats, mean, rstd, rms):
    var = ctx.enter_context(nc.sbuf_tensor(f"{tag}_var", [P, UNITS], F32))
    tmp = ctx.enter_context(nc.sbuf_tensor(f"{tag}_tmp", [P, 2, UNITS], F32))
    root = ctx.enter_context(nc.sbuf_tensor(f"{tag}_root", [P, 2, UNITS], F32))
    chain = ctx.sem(f"{tag}_stat_steps")
    rooted = ctx.sem(f"{tag}_rooted")
    asked = ctx.sem(f"{tag}_root_asked")
    ready = ctx.sem(f"{tag}_stats_ready")

    def vector(dve):
        n = [0]

        def link(ins):
            n[0] += 1
            ins.then_inc(chain, 1)
            dve.wait_ge(chain, n[0])

        even_mean, even_m2 = stats[:, :, 1], stats[:, :, 2]
        odd_mean, odd_m2 = stats[:, :, 4], stats[:, :, 5]
        link(dve.tensor_tensor(mean[:, :], even_mean, odd_mean, ALU.add))
        link(dve.tensor_scalar(mean[:, :], mean[:, :], 0.5, None, ALU.mult))
        link(dve.tensor_tensor(tmp[:, 0, :], even_mean, odd_mean, ALU.subtract))
        link(dve.tensor_tensor(tmp[:, 0, :], tmp[:, 0, :], tmp[:, 0, :], ALU.mult))
        link(dve.tensor_tensor(tmp[:, 1, :], even_m2, odd_m2, ALU.add))
        link(dve.tensor_scalar(tmp[:, 1, :], tmp[:, 1, :], 1.0 / C, None, ALU.mult))
        link(dve.scalar_tensor_tensor(out=var[:, :], in0=tmp[:, 0, :], scalar=0.25, in1=tmp[:, 1, :],
                                      op0=ALU.mult, op1=ALU.add))
        dve.tensor_scalar(tmp[:, 0, :], var[:, :], LN_EPS, None, ALU.add).then_inc(asked, 1)
        dve.wait_ge(rooted, 1)
        if not rms:
            dve.reciprocal(rstd[:, :], root[:, 0, :]).then_inc(ready, 1)
            return
        link(dve.reciprocal(rstd[:, :], root[:, 0, :]))
        link(dve.tensor_tensor(tmp[:, 1, :], rstd[:, :], rstd[:, :], ALU.mult))
        link(dve.tensor_tensor(tmp[:, 1, :], tmp[:, 1, :], var[:, :], ALU.mult))
        dve.tensor_scalar(tmp[:, 1, :], tmp[:, 1, :], 1e-8, None, ALU.add).then_inc(asked, 1)
        dve.wait_ge(rooted, 2)
        link(dve.reciprocal(root[:, 0, :], root[:, 1, :]))
        dve.tensor_tensor(rstd[:, :], rstd[:, :], root[:, 0, :], ALU.mult).then_inc(ready, 1)

    def scalar(act):
        for i in range(2 if rms else 1):
            act.wait_ge(asked, i + 1)
            act.activation(root[:, i, :], tmp[:, i, :], ACT.Sqrt).then_inc(rooted, 1)

    return vector, scalar, ready


def attention0(nc, x, stats, ident, headmask, x_in, w_qkvT, w_projT, b_proj, ctx_kT, ctx_v, consts):
    with stage(nc) as ctx:
        def sb(name, shape, dt=F32):
            return ctx.enter_context(nc.sbuf_tensor("a_" + name, shape, dt))

        def ps(name, shape):
            return ctx.enter_context(nc.psum_tensor("a_" + name, shape, F32))

        def sem(name):
            return ctx.sem("a_" + name)

        def mark(name, per=1):
            return Mark(ctx, nc, "a_" + name, per)

        wqkv = sb("wqkv", [P, 3, P])
        wproj = sb("wproj", [P, 2, P])
        bias_bc = sb("bias_bc", [P, C])
        mean = sb("mean", [P, UNITS])
        rstd = sb("rstd", [P, UNITS])
        xn = sb("xn", [P, 2, C])
        xnT = sb("xnT", [P, 2, P])
        qT = sb("qT", [P, 2, P])
        qx = sb("qx", [P, 2, 2, H, N])
        kT = sb("kT", [P, 2, 2, KEYS0])
        cv = sb("cv", [P, 2, C])
        vx = sb("vx", [P, 4, 2, PAIRS, 32])
        top = sb("top", [P, 2, PAIRS])
        prob = sb("prob", [P, 2, PAIRS, KEYS0])
        probT = sb("probT", [P, 2, PAIRS, P])
        recip = sb("recip", [P, 2, PAIRS])
        raw = sb("raw", [P, 2, 2, P])
        o = sb("o", [P, 2, PAIRS, D0])
        oT = sb("oT", [P, P])

        score_ps = ps("score_ps", [P, 2, PAIRS, KEYS0])
        probT_ps = ps("probT_ps", [P, PAIRS, P])
        in_ps = ps("in_ps", [P, 4, P])
        y_ps = in_ps[:, 3, :]
        out_ps = ps("out_ps", [P, 2, 2, P])
        raw_ps = out_ps[:, 0, :, :]
        o_ps = out_ps[:, 1, :, :].rearrange("p g (t c) -> p (g t) c", t=4)

        loaded, first_stats, zeroed = sem("loaded"), sem("first_stats"), sem("zeroed")
        x_loaded = [sem(f"x_loaded{s}") for s in range(4)]
        k_in = [sem(f"k_in{s}") for s in range(2)]
        v_in = [sem(f"v_in{s}") for s in range(2)]
        xn_done, biased = mark("xn_done"), mark("biased")
        xnT_ps_done, xnT_done = mark("xnT_ps_done"), mark("xnT_done")
        qkv_done, qkv_out = mark("qkv_done"), mark("qkv_out", 4)
        qx_done, cv_done = mark("qx_done"), mark("cv_done")
        scores_done, max_done, sub_done, exp_done = mark("scores", 2), mark("max", 2), mark("sub", 2), mark("exp", 2)
        probT_ps_done, probT_done = mark("probT_ps", 2), mark("probT", 4)
        raw_done, turned = mark("raw", 2), mark("turned", 2)
        pv_done, recip_done, o_done = mark("pv", 2), mark("recip", 4), mark("o", 4)
        oT_ps_done, oT_done, y_done, resid_done = mark("oT_ps"), mark("oT"), mark("y"), mark("resid")
        vec_stats, act_stats, stats_ready = finish_stats(nc, ctx, "a", stats, mean, rstd, False)

        def head_values(t, r=slice(0, P)):
            return t[r, :, 0:2 * VW].rearrange("p r (h c) -> p r h c", h=2)[:, :, :, 0:D0]

        DEPTH = 4
        block = ctx.block()

        @block.sync
        def _(sp):
            for s in range(4):
                n = UNITS // 4
                sp.dma_start(x[:, s * n:(s + 1) * n, :],
                             x_in[s * n * P:(s + 1) * n * P, :].rearrange("(u p) f -> p u f", p=P)
                             ).then_inc(x_loaded[s], 16)
            for dst, src in ((wqkv[:, :, :], w_qkvT), (wproj[:, :, :], w_projT), (bias_bc[:, :], b_proj),
                             (ident[:, :], consts["ident"]), (headmask[:, :], consts["headmask"])):
                sp.dma_start(dst, src).then_inc(loaded, 16)

            def step(at, on):
                if on(0):
                    a = at(0)
                    sp.wait_ge(scores_done.sem, scores_done.at(a.u - 2))
                    sp.dma_start(kT[:, a.slot, :, :].rearrange("p b k -> p (b k)")[:, N:3 * N],
                                 ctx_kT[:, bass.ds(a.u * P, P)]).then_inc(k_in[a.slot], 16)
                    sp.wait_ge(cv_done.sem, cv_done.at(a.u - 2))
                    sp.dma_start(cv[:, a.slot, :], ctx_v[:, bass.ds(a.u * P, P)]).then_inc(v_in[a.slot], 16)

            pipeline(sp, UNITS, DEPTH, step, 4)

        @block.gpsimd
        def _(pool):
            for m in (biased, qx_done, cv_done):
                m.credit(pool)
            pool.memset(vx[:, :, :, :, :], 1.0).then_inc(zeroed, 1)
            pool.wait_ge(loaded, 5 * 16)
            pool.wait_ge(zeroed, 1)

            def step(at, on):
                if on(1):
                    a = at(1)
                    pool.wait_ge(v_in[a.slot], a.half * 16 + 16)
                    if on(4):
                        pool.wait_ge(pv_done.sem, pv_done.at(a.u - 3))
                if on(0):
                    a = at(0)
                    pool.wait_ge(xn_done.sem, xn_done.at(a.u))
                    xu = x[:, bass.ds(a.u, 1), :].rearrange("p a f -> p (a f)")
                    pool.tensor_tensor(xu, xu, bias_bc[:, :], ALU.add).then_inc(biased.sem, 1)
                if on(1):
                    a = at(1)
                    for b in range(2):
                        last = pool.tensor_copy(head_values(vx[:, a.slot4, b, :, :]),
                                                cv[:, a.slot, :].rearrange("p (r h d) -> p r h d", r=PAIRS, h=2))
                    last.then_inc(cv_done.sem, 1)
                    pool.wait_ge(qkv_out.sem, qkv_out.at(a.u, 1))
                    pool.wait_ge(scores_done.sem, scores_done.at(a.u - 2))
                    for b in range(2):
                        last = pool.tensor_tensor(
                            qx[:, a.slot, b, :, :],
                            qT[:, a.slot, b * N:(b + 1) * N].unsqueeze(1).to_broadcast([P, H, N]),
                            headmask[:, :].unsqueeze(2).to_broadcast([P, H, N]), ALU.mult)
                    last.then_inc(qx_done.sem, 1)

            pipeline(pool, UNITS, DEPTH, step, 4)

        @block.scalar
        def _(act):
            for m in (xnT_done, qkv_out, exp_done, probT_done, raw_done, oT_done):
                m.credit(act)
            act_stats(act)

            def copy_probs(a, b):
                act.wait_ge(pv_done.sem, pv_done.at(a.u - 1, b + 1))
                act.wait_ge(probT_ps_done.sem, probT_ps_done.at(a.u, b + 1))
                for h in range(2):
                    act.activation(probT[:, b, 4 * h:4 * h + 4, :], probT_ps[:, 4 * h:4 * h + 4, :],
                                   ACT.Copy).then_inc(probT_done.sem, 1)

            def exps(a, b):
                act.wait_ge(sub_done.sem, sub_done.at(a.u, b + 1))
                act.activation(prob[:, b, :, :], prob[:, b, :, :], ACT.Exp).then_inc(exp_done.sem, 1)

            def copy_raw(a, b):
                act.wait_ge(pv_done.sem, pv_done.at(a.u, b + 1))
                act.wait_ge(turned.sem, turned.at(a.u - 1, b + 1))
                act.activation(raw[:, b, :, :], raw_ps, ACT.Copy).then_inc(raw_done.sem, 1)

            def step(at, on):
                if on(4):
                    a = at(4)
                    act.wait_ge(oT_ps_done.sem, oT_ps_done.at(a.u))
                    act.wait_ge(y_done.sem, y_done.at(a.u - 1))
                    act.activation(oT[:, :], y_ps, ACT.Copy).then_inc(oT_done.sem, 1)
                if on(3):
                    copy_raw(at(3), 0)
                if on(1):
                    a = at(1)
                    act.wait_ge(qkv_done.sem, qkv_done.at(a.u))
                    act.wait_ge(qx_done.sem, qx_done.at(a.u - 2))
                    act.activation(qT[:, a.slot, :], in_ps[:, 1, :], ACT.Copy,
                                   scale=float(D0) ** -0.5).then_inc(qkv_out.sem, 1)
                    act.wait_ge(scores_done.sem, scores_done.at(a.u - 2))
                    own = kT[:, a.slot, :, :].rearrange("p b (h k) -> p (b h) k", k=N)
                    act.activation(own[:, 0:4:3, :], in_ps[:, 2, :].rearrange("p (b k) -> p b k", b=2),
                                   ACT.Copy).then_inc(qkv_out.sem, 1)
                if on(3):
                    copy_probs(at(3), 1)
                if on(1):
                    a = at(1)
                    act.wait_ge(cv_done.sem, cv_done.at(a.u))
                    for b in range(2):
                        r = slice(b * N, (b + 1) * N)
                        act.activation(head_values(vx[:, a.slot4, b, :, :], r),
                                       in_ps[r, 0, :].rearrange("p (r h d) -> p r h d", r=PAIRS, h=2),
                                       ACT.Copy).then_inc(qkv_out.sem, 1)
                if on(2):
                    exps(at(2), 0)
                    copy_probs(at(2), 0)
                if on(3):
                    copy_raw(at(3), 1)
                if on(0):
                    a = at(0)
                    act.wait_ge(xnT_ps_done.sem, xnT_ps_done.at(a.u))
                    act.wait_ge(qkv_done.sem, qkv_done.at(a.u - 2))
                    act.activation(xnT[:, a.slot, :], in_ps[:, 0, :], ACT.Copy).then_inc(xnT_done.sem, 1)
                if on(2):
                    exps(at(2), 1)

            pipeline(act, UNITS, DEPTH, step, 4)

        @block.tensor
        def _(pe):
            for m in (xnT_ps_done, qkv_done, scores_done, probT_ps_done, pv_done, turned, oT_ps_done,
                      y_done):
                m.credit(pe)
            pe.wait_ge(loaded, 5 * 16)

            def scores(a, b):
                if b == 0:
                    pe.wait_ge(qx_done.sem, qx_done.at(a.u))
                    pe.wait_ge(qkv_out.sem, qkv_out.at(a.u, 2))
                    pe.wait_ge(k_in[a.slot], a.half * 16 + 16)
                pe.wait_ge(sub_done.sem, sub_done.at(a.u - 1, b + 1))
                for r in range(PAIRS):
                    m = pe.matmul(score_ps[:, b, r, :],
                                  qx[:, a.slot, b, 2 * r:2 * r + 2, :].rearrange("p h q -> p (h q)"),
                                  kT[:, a.slot, b, :], start=True, stop=True)
                m.then_inc(scores_done.sem, 1)

            def turn_probs(a, b):
                pe.wait_ge(exp_done.sem, exp_done.at(a.u, b + 1))
                pe.wait_ge(probT_done.sem, probT_done.at(a.u - 1 + b, 2 * (2 - b)))
                for r in range(PAIRS):
                    m = pe.transpose(probT_ps[:, r, :], prob[:, b, r, :], ident[:, :])
                m.then_inc(probT_ps_done.sem, 1)

            def values(a, b):
                pe.wait_ge(probT_done.sem, probT_done.at(a.u, 2 * b + 2))
                if b == 0:
                    pe.wait_ge(cv_done.sem, cv_done.at(a.u))
                    pe.wait_ge(qkv_out.sem, qkv_out.at(a.u))
                pe.wait_ge(o_done.sem, o_done.at(a.u, 2 * b))
                for r in range(PAIRS):
                    t = 32 * (r % 4)
                    m = pe.matmul(raw_ps[t:t + 32, r // 4, :], vx[:, a.slot4, b, r, :], probT[:, b, r, :],
                                  start=True, stop=True)
                m.then_inc(pv_done.sem, 1)

            def turn_values(a, b):
                pe.wait_ge(raw_done.sem, raw_done.at(a.u, b + 1))
                for i in range(2):
                    m = pe.transpose(out_ps[:, 1, i, :], raw[:, b, i, :], ident[:, :])
                m.then_inc(turned.sem, 1)

            def step(at, on):
                if on(2):
                    scores(at(2), 0)
                if on(4):
                    turn_values(at(4), 1)
                if on(3):
                    turn_probs(at(3), 1)
                if on(4):
                    a = at(4)
                    pe.wait_ge(o_done.sem, o_done.at(a.u))
                    pe.wait_ge(resid_done.sem, resid_done.at(a.u - 1))
                    if on(1):
                        pe.wait_ge(xnT_done.sem, xnT_done.at(at(1).u))
                    pe.transpose(y_ps, o[:, :, :, :].rearrange("p b r d -> p (b r d)"), ident[:, :]).then_inc(oT_ps_done.sem, 1)
                if on(3):
                    values(at(3), 0)
                if on(1):
                    a = at(1)
                    pe.wait_ge(xnT_done.sem, xnT_done.at(a.u))
                    if on(4):
                        pe.wait_ge(oT_done.sem, oT_done.at(at(4).u))
                    xu = xnT[:, a.slot, :]
                    pe.matmul(in_ps[:, 1, :], wqkv[:, 0, :], xu, start=True, stop=True)
                    pe.matmul(in_ps[:, 2, :], wqkv[:, 1, :], xu, start=True, stop=True)
                    pe.matmul(in_ps[:, 0, :], xu, wqkv[:, 2, :], start=True, stop=True).then_inc(qkv_done.sem, 1)
                if on(2):
                    scores(at(2), 1)
                if on(4):
                    pe.wait_ge(oT_done.sem, oT_done.at(at(4).u))
                    if on(1):
                        pe.wait_ge(qkv_out.sem, qkv_out.at(at(1).u))
                if on(3):
                    turn_values(at(3), 0)
                if on(4):
                    for b in range(2):
                        for par in range(2):
                            m = pe.matmul(y_ps[b * N:(b + 1) * N, :], oT[b * N:(b + 1) * N, par * N:(par + 1) * N],
                                          wproj[b * N:(b + 1) * N, par, :], start=(par == 0), stop=(par == 1))
                    m.then_inc(y_done.sem, 1)
                if on(2):
                    turn_probs(at(2), 0)
                if on(3):
                    values(at(3), 1)
                if on(0):
                    a = at(0)
                    pe.wait_ge(xn_done.sem, xn_done.at(a.u))
                    pe.wait_ge(qkv_out.sem, qkv_out.at(a.u - 1))
                    if on(4):
                        pe.wait_ge(resid_done.sem, resid_done.at(at(4).u))
                    pe.transpose(in_ps[:, 0, :], xn[:, a.slot, :], ident[:, :]).then_inc(xnT_ps_done.sem, 1)

            pipeline(pe, UNITS, DEPTH, step, 4)

        @block.vector
        def _(dve):
            for m in (xn_done, max_done, sub_done, recip_done, o_done, resid_done):
                m.credit(dve)
            for s in range(4):
                dve.wait_ge(x_loaded[s], 16)
                for u in range(s * UNITS // 4, (s + 1) * UNITS // 4):
                    m = dve.bn_stats(stats[:, u, :], x[:, u, :])
            m.then_inc(first_stats, 1)
            dve.wait_ge(first_stats, 1)
            vec_stats(dve)
            dve.wait_ge(stats_ready, 1)

            def shift(a, b):
                dve.wait_ge(scores_done.sem, scores_done.at(a.u, b + 1))
                dve.tensor_reduce(top[:, b, :], score_ps[:, b, :, :], AX.X, ALU.max).then_inc(max_done.sem, 1)
                dve.wait_ge(max_done.sem, max_done.at(a.u, b + 1))
                dve.wait_ge(probT_ps_done.sem, probT_ps_done.at(a.u - 1, b + 1))
                dve.tensor_tensor(prob[:, b, :, :], score_ps[:, b, :, :],
                                  top[:, b, :].unsqueeze(2).to_broadcast([P, PAIRS, KEYS0]),
                                  ALU.subtract).then_inc(sub_done.sem, 1)

            def normalise(a, b):
                dve.wait_ge(turned.sem, turned.at(a.u, b + 1))
                if b == 0:
                    dve.wait_ge(oT_ps_done.sem, oT_ps_done.at(a.u - 1))
                for par in range(2):
                    r = slice(par * N, (par + 1) * N)
                    dve.reciprocal(recip[r, b, :], o_ps[r, :, par * VW + D0]).then_inc(recip_done.sem, 1)
                dve.wait_ge(recip_done.sem, recip_done.at(a.u, 2 * b + 2))
                for par in range(2):
                    r = slice(par * N, (par + 1) * N)
                    dve.tensor_tensor(o[r, b, :, :], o_ps[r, :, par * VW:par * VW + D0],
                                      recip[r, b, :].unsqueeze(2).to_broadcast([N, PAIRS, D0]),
                                      ALU.mult).then_inc(o_done.sem, 1)

            def step(at, on):
                if on(0):
                    a = at(0)
                    dve.wait_ge(xnT_ps_done.sem, xnT_ps_done.at(a.u - 2))
                    dve.tensor_scalar(xn[:, a.slot, :], x[:, bass.ds(a.u, 1), :].rearrange("p a f -> p (a f)"),
                                      mean[:, bass.ds(a.u, 1)], rstd[:, bass.ds(a.u, 1)],
                                      ALU.subtract, ALU.mult).then_inc(xn_done.sem, 1)
                if on(4):
                    normalise(at(4), 1)
                if on(2):
                    shift(at(2), 0)
                if on(3):
                    normalise(at(3), 0)
                if on(4):
                    a = at(4)
                    xu = x[:, bass.ds(a.u, 1), :].rearrange("p a f -> p (a f)")
                    dve.wait_ge(y_done.sem, y_done.at(a.u))
                    dve.wait_ge(biased.sem, biased.at(a.u))
                    dve.tensor_tensor(xu, y_ps, xu, ALU.add).then_inc(resid_done.sem, 1)
                if on(2):
                    shift(at(2), 1)
                if on(4):
                    a = at(4)
                    dve.wait_ge(resid_done.sem, resid_done.at(a.u))
                    dve.bn_stats(stats[:, bass.ds(a.u, 1), :].rearrange("p a s -> p (a s)"),
                                 x[:, bass.ds(a.u, 1), :].rearrange("p a f -> p (a f)"))

            pipeline(dve, UNITS, DEPTH, step, 4)


class SplitWeights:

    def __init__(self, nc, ctx, tag, jobs):
        self.jobs, self.slots = jobs, 3
        widest = max(src.shape[1] for _, _, src in jobs)
        self.raw = ctx.enter_context(nc.sbuf_tensor(f"{tag}_raw", [P, self.slots, widest], F32))
        self.landed = [ctx.sem(f"{tag}_w_landed{s}") for s in range(self.slots)]
        self.hi_made = ctx.sem(f"{tag}_w_hi")
        self.pool_split, self.dve_split = ctx.sem(f"{tag}_w_pool"), ctx.sem(f"{tag}_w_dve")

    def source(self, i):
        rows, n = self.jobs[i][2].shape
        return self.raw[0:rows, i % self.slots, 0:n]

    def wait(self, eng, n):
        if n >= 3:
            eng.wait_ge(self.pool_split, n // 3)
        eng.wait_ge(self.dve_split, n - n // 3)

    def sync(self, sp):
        for i, (_, _, src) in enumerate(self.jobs):
            if i >= self.slots:
                self.wait(sp, i - self.slots + 1)
            sp.dma_start(self.source(i), src).then_inc(self.landed[i % self.slots], 16)

    def scalar(self, act, first, last):
        for i in range(first, last):
            act.wait_ge(self.landed[i % self.slots], 16 * (i // self.slots + 1))
            act.activation(self.jobs[i][0], self.source(i), ACT.Copy).then_inc(self.hi_made, 1)

    def rest(self, eng, first, last, third):
        for i in range(first, last):
            if (i % 3 == 2) == third:
                hi, lo, _ = self.jobs[i]
                eng.wait_ge(self.hi_made, i + 1)
                eng.tensor_tensor(lo, self.source(i), hi.bitcast(F32), ALU.subtract
                                  ).then_inc(self.pool_split if third else self.dve_split, 1)

    def share(self, s, steps):
        n = len(self.jobs)
        return n * s // steps, n * (s + 1) // steps


def pieces(hi, lo, src, most=1024):
    n = src.shape[1]
    return [(hi[:, i:min(i + most, n)], lo[:, i:min(i + most, n)], src[:, i:min(i + most, n)])
            for i in range(0, n, most)]


def experts(nc, x, stats, ident, a, shared, out):
    tag = "d_" if shared else "b_"
    CH = 4 if shared else 3
    R = 512 // CH if shared else 336 // CH
    NE = E + 1 if shared else E
    FIRST = NE - E
    S = NE * CH
    MATS = 1 if shared else 2
    ZS = 4 // MATS
    LAG = 5 if shared else 4
    WEIGH = LAG + 1
    HF, HS = 4, 6
    CS = 4
    AH = 50
    KMAX = 6
    hook = {name: p * S // 24 for name, p in dict(xT=3, router=6, hidden=9, logits=12, scT=19, finish=22).items()}
    hook.update(rank=hook["hidden"] + 1, count=hook["logits"] + 1, choose=hook["logits"] + 2,
                hi_score=hook["logits"] + 4, split_score=hook["logits"] + 5)

    with stage(nc) as ctx:
        def sb(name, shape, dt=F32):
            return ctx.enter_context(nc.sbuf_tensor(tag + name, shape, dt))

        def ps(name, shape):
            return ctx.enter_context(nc.psum_tensor(tag + name, shape, F32))

        def sem(name):
            return ctx.sem(tag + name)

        def mark(name, per=1):
            return Mark(ctx, nc, tag + name, per)

        w_hi, w_lo = (sb(f"w_{n}", [P, MATS, S, R], F32R) for n in ("hi", "lo"))
        wd_hi, wd_lo = (sb(f"wd_{n}", [P, S, C], F32R) for n in ("hi", "lo"))
        rw_hi, rw_lo = (sb(f"rw_{n}", [P, E], F32R) for n in ("hi", "lo"))
        sel_hi, sel_lo = (sb(f"sel_{n}", [P, E, P], F32R) for n in ("hi", "lo"))
        before = sb("before", [P, E, E])
        mean, rstd = sb("mean", [P, UNITS]), sb("rstd", [P, UNITS])
        xn = sb("xn", [P, GROUP, C])
        xf = sb("xf", [P, COLS])
        x_hi, x_lo = (sb(f"x_{n}", [P, 2, COLS], F32R) for n in ("hi", "lo"))
        h = sb("h", [P, HF, COLS])
        h_hi, h_lo = (sb(f"h_{n}", [P, HS, COLS], F32R) for n in ("hi", "lo"))
        cB = sb("cB", [P, CS, COLS])
        part = sb("part", [P, 2, COLS])
        acc = sb("acc", [P, 2, COLS])
        probs = sb("probs", [P, GROUP, E])
        red = sb("red", [P, GROUP])
        inv = sb("inv", [P, GROUP])
        gt, ge = sb("gt", [P, GROUP, E, E]), sb("ge", [P, GROUP, E, E])
        rank = sb("rank", [P, GROUP, E])
        mask = sb("mask", [P, GROUP, E])
        score = sb("score", [P, GROUP, E])
        score_hi = sb("score_hi", [P, GROUP, E], F32R)
        split_score = sb("split_score", [P, GROUP, P])
        scT = sb("scT", [P, 2, COLS], F32R)
        if shared:
            norm_w = sb("norm_w", [P, 1])
            b1, b2 = sb("b1", [P, S]), sb("b2", [P, NE])
            small = ((norm_w[:, :], a["d_norm"]), (b1[:, :], a["d_b1"]), (b2[:, :], a["d_b2"]))
        else:
            sg = sb("sg", [P, 2, COLS])
            aw_hi, aw_lo = (sb(f"aw_{n}", [P, P], F32R) for n in ("hi", "lo"))
            ab1, aw2, ab2 = sb("ab1", [AH, 1]), sb("aw2", [AH, KMAX]), sb("ab2", [P, KMAX])
            kcode = sb("kcode", [P, KMAX])
            ah = sb("ah", [AH, COLS])
            al, amax = sb("al", [P, GROUP, KMAX]), sb("amax", [P, GROUP])
            small = ((ab1[:, :], a["b_ab1"]), (aw2[:, :], a["b_aw2T"]), (ab2[:, :], a["b_ab2"]),
                     (kcode[:, :], a["kcode"]))
        small += ((before[:, :, :], a["before"]),)

        z_ps = ps("z", [P, MATS, ZS, COLS])
        y_ps = ps("y", [P, 2, COLS])
        t_ps = ps("t", [P, COLS])
        c_ps = ps("c", [P, COLS])

        loaded, zeroed = sem("loaded"), sem("zeroed")
        xn_done, xT_ps_done, xf_done, xhi_done, xlo_done = (mark(n) for n in ("xn", "xT_ps", "xf", "xhi", "xlo"))
        router_done, soft_done = mark("router"), mark("soft")
        hidden_done, gelu_done, logits_done, al_done = (mark(n) for n in ("hidden", "gelu", "logits", "al"))
        exp_done, scored, scT_ps_done, scT_done = (mark(n) for n in ("exp", "scored", "scT_ps", "scT"))
        hi_scored, max_done = mark("hi_scored"), mark("max")
        STEPS_R = 11 if shared else 16
        r_step = mark("r_step", STEPS_R)
        z_done, sg_done, h_done, hi_done = (mark(n, S) for n in ("z", "sg", "h", "hi"))
        lo_pool, lo_dve = mark("lo_pool", S // 2), mark("lo_dve", S // 2)
        down_done = mark("down", S)
        c_ps_done, cB_done = mark("c_ps", E), mark("cB", E)
        weighed, added = mark("weighed", NE), mark("added", NE - 1)
        fin_ps_done, resid_done = mark("fin_ps"), mark("resid")
        stored = sem("stored")
        vec_stats, act_stats, stats_ready = finish_stats(nc, ctx, tag + "s", stats, mean, rstd, shared)

        jobs = pieces(rw_hi[:, :], rw_lo[:, :], a[tag + "rw"])
        jobs += pieces(sel_hi[:, :, :].rearrange("p e c -> p (e c)"), sel_lo[:, :, :].rearrange("p e c -> p (e c)"), a["sel"])
        if not shared:
            jobs += pieces(aw_hi[:, :], aw_lo[:, :], a["b_aw1T"])
        PREP_JOBS = len(jobs)
        flat = lambda t, m: t[:, m, :, :].rearrange("p s r -> p (s r)")
        down_flat = lambda t: t[0:R, :, :].rearrange("p s c -> p (s c)")
        for q in range(3):
            lo_c, hi_c = q * S * R // 3, (q + 1) * S * R // 3
            for m in range(MATS):
                jobs += pieces(flat(w_hi, m)[:, lo_c:hi_c], flat(w_lo, m)[:, lo_c:hi_c], a[tag + "w"][m][:, lo_c:hi_c])
            lo_c, hi_c = q * S * C // 3, (q + 1) * S * C // 3
            jobs += pieces(down_flat(wd_hi)[:, lo_c:hi_c], down_flat(wd_lo)[:, lo_c:hi_c], a[tag + "wd"][:, lo_c:hi_c])
        weights = SplitWeights(nc, ctx, tag + "sw", jobs)

        DEPTH = 2
        block = ctx.block()

        def y_slot(g, e):
            return (g.slot * NE + e) % 2

        def behind(at, on, s, lag):
            n = 1 if s >= lag else 2
            return (at(n), (s - lag) % S) if on(n) else None

        def wait_lo(eng, g, s):
            m = lo_dve if s % 2 else lo_pool
            eng.wait_ge(m.sem, m.at(g.u, s // 2 + 1))

        def unit_tiles(g):
            return x[:, bass.ds(g.u * GROUP, GROUP), :]

        @block.sync
        def _(sp):
            for dst, src in small:
                sp.dma_start(dst, src).then_inc(loaded, 16)
            weights.sync(sp)
            if shared:
                def step(at, on):
                    if on(0):
                        g = at(0)
                        sp.wait_ge(resid_done.sem, resid_done.at(g.u))
                        sp.dma_start(out[bass.ds(g.u * COLS, COLS), :].rearrange("(u p) f -> p u f", p=P),
                                     unit_tiles(g)).then_inc(stored, 16)
                pipeline(sp, GROUPS, 0, step)
                sp.wait_ge(stored, 16 * GROUPS)

        @block.gpsimd
        def _(pool):
            for m in (lo_pool, added):
                m.credit(pool)
            pool.memset(split_score[:, :, :], 0.0).then_inc(zeroed, 1)
            def step(at, on):
                for s in range(S):
                    if on(0) and not on(1):
                        weights.rest(pool, *weights.share(s, S), True)
                    if s % 2 == 0 and on(1):
                        g = at(1)
                        pool.wait_ge(hi_done.sem, hi_done.at(g.u, s + 1))
                        pool.wait_ge(down_done.sem, down_done.at(g.u, s + 1 - HS))
                        pool.tensor_tensor(h_lo[0:R, s % HS, :], h[0:R, s % HF, :],
                                           h_hi[0:R, s % HS, :].bitcast(F32), ALU.subtract).then_inc(lo_pool.sem, 1)
                    found = behind(at, on, s, LAG + CH)
                    if found and found[1] % CH == 0 and found[1]:
                        g, e = found[0], found[1] // CH
                        pool.wait_ge(added.sem, added.at(g.u, e - 1))
                        pool.wait_ge(weighed.sem, weighed.at(g.u, e + 1))
                        pool.tensor_tensor(acc[:, g.slot, :], acc[:, g.slot, :], part[:, y_slot(g, e), :],
                                           ALU.add).then_inc(added.sem, 1)

            pipeline(pool, GROUPS, DEPTH, step)

        @block.scalar
        def _(act):
            for m in (xf_done, xhi_done, gelu_done, exp_done, hi_scored, scT_done, sg_done, hi_done, cB_done):
                m.credit(act)
            act_stats(act)

            def step(at, on):
                for s in range(S):
                    if on(0) and not on(1):
                        weights.scalar(act, *weights.share(s, S))
                    prev = behind(at, on, s, 1)
                    if prev:
                        g, q = prev
                        act.wait_ge(h_done.sem, h_done.at(g.u, q + 1))
                        act.wait_ge(down_done.sem, down_done.at(g.u, q + 1 - HS))
                        act.activation(h_hi[0:R, q % HS, :], h[0:R, q % HF, :], ACT.Copy).then_inc(hi_done.sem, 1)
                    if on(1) and not shared:
                        g = at(1)
                        act.wait_ge(z_done.sem, z_done.at(g.u, s + 1))
                        act.wait_ge(h_done.sem, h_done.at(g.u, s - 1))
                        act.activation(sg[0:R, s % 2, :], z_ps[0:R, 0, s % ZS, :], ACT.Silu).then_inc(sg_done.sem, 1)
                    if on(1) and s % CH == 0 and s // CH >= FIRST:
                        g, r = at(1), s // CH - FIRST
                        act.wait_ge(c_ps_done.sem, c_ps_done.at(g.u, r + 1))
                        act.wait_ge(weighed.sem, weighed.at(g.u, r + FIRST + 1 - CS))
                        act.activation(cB[:, r % CS, :], c_ps[:, :], ACT.Copy).then_inc(cB_done.sem, 1)
                    if not on(0):
                        continue
                    g = at(0)
                    if s == hook["xT"]:
                        act.wait_ge(xT_ps_done.sem, xT_ps_done.at(g.u))
                        act.wait_ge(xlo_done.sem, xlo_done.at(g.u - 1))
                        act.activation(xf[:, :], t_ps[:, :], ACT.Copy,
                                       scale=norm_w[:, 0:1] if shared else 1.0).then_inc(xf_done.sem, 1)
                        act.wait_ge(xf_done.sem, xf_done.at(g.u))
                        act.wait_ge(z_done.sem, z_done.at(g.u - 2))
                        act.activation(x_hi[:, g.slot, :], xf[:, :], ACT.Copy).then_inc(xhi_done.sem, 1)
                    if s == hook["router"] and shared:
                        act.wait_ge(router_done.sem, router_done.at(g.u))
                        act.wait_ge(scored.sem, scored.at(g.u - 1))
                        act.activation(probs[:, :, :], t_ps[:, 0:GROUP * E].rearrange("p (u e) -> p u e", e=E),
                                       ACT.Sigmoid).then_inc(exp_done.sem, 1)
                    if s == hook["hidden"] and not shared:
                        act.wait_ge(hidden_done.sem, hidden_done.at(g.u))
                        act.wait_ge(logits_done.sem, logits_done.at(g.u - 1))
                        act.activation(ah[:, :], t_ps[0:AH, :], ACT.Gelu_apprx_tanh,
                                       bias=ab1[:, 0:1]).then_inc(gelu_done.sem, 1)
                        act.wait_ge(soft_done.sem, soft_done.at(g.u))
                        act.activation(probs[:, :, :], probs[:, :, :], ACT.Exp).then_inc(exp_done.sem, 1)
                    if s == hook["hi_score"]:
                        act.wait_ge(r_step.sem, r_step.at(g.u))
                        act.activation(score_hi[:, :, :], score[:, :, :], ACT.Copy).then_inc(hi_scored.sem, 1)
                    if s == hook["scT"]:
                        act.wait_ge(scT_ps_done.sem, scT_ps_done.at(g.u))
                        act.wait_ge(c_ps_done.sem, c_ps_done.at(g.u - 2))
                        act.activation(scT[:, g.slot, :], t_ps[:, :], ACT.Copy).then_inc(scT_done.sem, 1)

            pipeline(act, GROUPS, DEPTH, step)

        @block.tensor
        def _(pe):
            for m in (xT_ps_done, router_done, hidden_done, logits_done, scT_ps_done, z_done, down_done, c_ps_done,
                      fin_ps_done):
                m.credit(pe)
            pe.wait_ge(loaded, 16 * len(small))

            def three(dst, hi, lo, m_hi, m_lo, start=True, stop=True):
                pe.matmul(dst, hi, m_hi, start=start, stop=False)
                pe.matmul(dst, hi, m_lo, start=False, stop=False)
                return pe.matmul(dst, lo, m_hi, start=False, stop=stop)

            def up(g, s):
                pe.wait_ge(h_done.sem, h_done.at(g.u, s + 1 - ZS))
                for m in range(MATS):
                    last = three(z_ps[0:R, m, s % ZS, :], w_hi[:, m, s, :], w_lo[:, m, s, :],
                                 x_hi[:, g.slot, :], x_lo[:, g.slot, :])
                last.then_inc(z_done.sem, 1)

            def down(g, s):
                e = s // CH
                if s % CH == 0:
                    pe.wait_ge(weighed.sem, weighed.at(g.u, e - 1))
                wait_lo(pe, g, s)
                three(y_ps[:, y_slot(g, e), :], wd_hi[0:R, s, :], wd_lo[0:R, s, :], h_hi[0:R, s % HS, :],
                      h_lo[0:R, s % HS, :], s % CH == 0, s % CH == CH - 1).then_inc(down_done.sem, 1)

            def prepare(g, s):
                x_of = lambda t, i: t[:, g.slot, i * P:(i + 1) * P]
                if s == hook["xT"]:
                    pe.wait_ge(xn_done.sem, xn_done.at(g.u))
                    pe.wait_ge(resid_done.sem, resid_done.at(g.u - 3))
                    pe.wait_ge(scT_done.sem, scT_done.at(g.u - 1))
                    for i in range(GROUP):
                        m = pe.transpose(t_ps[:, i * P:(i + 1) * P], xn[:, i, :], ident[:, :])
                    m.then_inc(xT_ps_done.sem, 1)
                if s == hook["router"]:
                    weights.wait(pe, PREP_JOBS)
                    pe.wait_ge(xlo_done.sem, xlo_done.at(g.u))
                    for i in range(GROUP):
                        m = three(t_ps[:, i * E:(i + 1) * E], x_of(x_hi, i), x_of(x_lo, i), rw_hi[:, :], rw_lo[:, :])
                    m.then_inc(router_done.sem, 1)
                if s == hook["hidden"] and not shared:
                    pe.wait_ge(soft_done.sem, soft_done.at(g.u))
                    three(t_ps[:, :], aw_hi[:, :], aw_lo[:, :], x_hi[:, g.slot, :], x_lo[:, g.slot, :]
                          ).then_inc(hidden_done.sem, 1)
                if s == hook["logits"] and not shared:
                    pe.wait_ge(gelu_done.sem, gelu_done.at(g.u))
                    for i in range(GROUP):
                        m = pe.matmul(t_ps[:, i * KMAX:(i + 1) * KMAX], ah[:, i * P:(i + 1) * P], aw2[:, :],
                                      start=True, stop=True)
                    m.then_inc(logits_done.sem, 1)
                if s == hook["scT"]:
                    pe.wait_ge(scored.sem, scored.at(g.u))
                    for i in range(GROUP):
                        m = pe.transpose(t_ps[:, i * P:(i + 1) * P], split_score[:, i, :], ident[:, :])
                    m.then_inc(scT_ps_done.sem, 1)

            def step(at, on):
                for s in range(S):
                    if on(0):
                        prepare(at(0), s)
                    if on(2) and s == hook["finish"]:
                        g = at(2)
                        pe.wait_ge(added.sem, added.at(g.u))
                        pe.wait_ge(scT_done.sem, scT_done.at(g.u + 2) if on(0) else scT_done.at(GROUPS - 1))
                        for i in range(GROUP):
                            m = pe.transpose(t_ps[:, i * P:(i + 1) * P], acc[:, g.slot, i * P:(i + 1) * P], ident[:, :])
                        m.then_inc(fin_ps_done.sem, 1)
                    if on(1):
                        g = at(1)
                        if s % CH == 0 and s // CH >= FIRST:
                            r = s // CH - FIRST
                            pe.wait_ge(scT_done.sem, scT_done.at(g.u))
                            pe.wait_ge(cB_done.sem, cB_done.at(g.u, r))
                            pe.matmul(c_ps[:, :], sel_hi[:, r, :], scT[:, g.slot, :], start=True, stop=True
                                      ).then_inc(c_ps_done.sem, 1)
                        if s % (S // 3) == 0:
                            weights.wait(pe, PREP_JOBS + (len(jobs) - PREP_JOBS) // 3 * (s // (S // 3) + 1))
                        up(g, s)
                    found = behind(at, on, s, LAG)
                    if found:
                        down(*found)

            pipeline(pe, GROUPS, DEPTH, step)

        @block.vector
        def _(dve):
            for m in (xn_done, xlo_done, soft_done, max_done, al_done, scored, r_step, h_done, lo_dve, weighed, resid_done):
                m.credit(dve)
            vec_stats(dve)
            dve.wait_ge(stats_ready, 1)
            dve.wait_ge(loaded, 16 * len(small))
            dve.wait_ge(zeroed, 1)

            steps_before = (0, 2, 5, 8) if shared else (0, 5, 8, 12)

            def route(g, n):
                count = [steps_before[n]]

                def link(ins):
                    count[0] += 1
                    ins.then_inc(r_step.sem, 1)
                    dve.wait_ge(r_step.sem, r_step.at(g.u, count[0]))

                wide = lambda t: t.unsqueeze(2).to_broadcast([P, GROUP, E])
                by_j = probs[:, :, :].unsqueeze(2).to_broadcast([P, GROUP, E, E])
                by_e = probs[:, :, :].unsqueeze(3).to_broadcast([P, GROUP, E, E])
                first = before[:, :, :].unsqueeze(1).to_broadcast([P, GROUP, E, E])
                if n == 0:
                    dve.wait_ge(exp_done.sem, exp_done.at(g.u))
                    if not shared:
                        link(dve.tensor_reduce(red[:, :], probs[:, :, :], AX.X, ALU.add))
                        link(dve.reciprocal(inv[:, :], red[:, :]))
                        link(dve.tensor_tensor(probs[:, :, :], probs[:, :, :], wide(inv[:, :]), ALU.mult))
                    link(dve.tensor_tensor(ge[:, :, :, :], by_j, by_e, ALU.is_ge))
                    link(dve.tensor_tensor(ge[:, :, :, :], ge[:, :, :, :], first, ALU.mult))
                if n == 1:
                    link(dve.tensor_tensor(gt[:, :, :, :], by_j, by_e, ALU.is_gt))
                    link(dve.tensor_tensor(gt[:, :, :, :], gt[:, :, :, :], ge[:, :, :, :], ALU.max))
                    link(dve.tensor_reduce(rank[:, :, :], gt[:, :, :, :], AX.X, ALU.add))
                if n == 2 and shared:
                    link(dve.tensor_scalar(mask[:, :, :], rank[:, :, :], 2.0, None, ALU.is_lt))
                    link(dve.tensor_tensor(mask[:, :, :], mask[:, :, :], probs[:, :, :], ALU.mult))
                    link(dve.tensor_reduce(red[:, :], mask[:, :, :], AX.X, ALU.add))
                if n == 3 and shared:
                    link(dve.tensor_scalar(red[:, :], red[:, :], 1e-6, None, ALU.add))
                    link(dve.reciprocal(inv[:, :], red[:, :]))
                    dve.tensor_tensor(score[:, :, :], mask[:, :, :], wide(inv[:, :]), ALU.mult).then_inc(r_step.sem, 1)
                wide_k = lambda t: t.unsqueeze(2).to_broadcast([P, GROUP, KMAX])
                over = lambda t: t.unsqueeze(1).to_broadcast([P, GROUP, KMAX])
                if n == 2 and not shared:
                    dve.wait_ge(logits_done.sem, logits_done.at(g.u))
                    dve.tensor_tensor(al[:, :, :], t_ps[:, 0:GROUP * KMAX].rearrange("p (u k) -> p u k", k=KMAX),
                                      over(ab2[:, :]), ALU.add).then_inc(al_done.sem, 1)
                    dve.wait_ge(al_done.sem, al_done.at(g.u))
                    link(dve.tensor_scalar(al[:, :, :], al[:, :, :], -30.0, 30.0, ALU.max, ALU.min))
                    link(dve.tensor_reduce(amax[:, :], al[:, :, :], AX.X, ALU.max))
                    link(dve.tensor_tensor(al[:, :, :], al[:, :, :], wide_k(amax[:, :]), ALU.is_equal))
                    link(dve.tensor_tensor(al[:, :, :], al[:, :, :], over(kcode[:, :]), ALU.mult))
                if n == 3 and not shared:
                    link(dve.tensor_reduce(amax[:, :], al[:, :, :], AX.X, ALU.min))
                    link(dve.tensor_scalar(rank[:, :, :], rank[:, :, :], -100.0, None, ALU.add))
                    link(dve.tensor_tensor(mask[:, :, :], rank[:, :, :], wide(amax[:, :]), ALU.is_lt))
                    dve.tensor_tensor(score[:, :, :], mask[:, :, :], probs[:, :, :], ALU.mult).then_inc(r_step.sem, 1)
                assert n == 3 or count[0] == steps_before[n + 1], (n, count)
                assert n < 3 or count[0] + 1 == STEPS_R, count

            def step(at, on):
                for s in range(S):
                    if on(0) and not on(1):
                        weights.rest(dve, *weights.share(s, S), False)
                    if on(1):
                        g = at(1)
                        dve.wait_ge(hi_done.sem, hi_done.at(g.u, s + 1 - HF))
                        wait_lo(dve, g, s - HF)
                        if shared:
                            dve.wait_ge(z_done.sem, z_done.at(g.u, s + 1))
                            dve.tensor_scalar(h[:, s % HF, :], z_ps[:, 0, s % ZS, :], b1[:, s:s + 1], 0.0,
                                              ALU.add, ALU.max).then_inc(h_done.sem, 1)
                        else:
                            dve.wait_ge(sg_done.sem, sg_done.at(g.u, s + 1))
                            dve.tensor_tensor(h[0:R, s % HF, :], z_ps[0:R, 1, s % ZS, :], sg[0:R, s % 2, :],
                                              ALU.mult).then_inc(h_done.sem, 1)
                    prev = behind(at, on, s, 1)
                    if prev and prev[1] % 2:
                        g, q = prev
                        dve.wait_ge(hi_done.sem, hi_done.at(g.u, q + 1))
                        dve.wait_ge(down_done.sem, down_done.at(g.u, q + 1 - HS))
                        dve.tensor_tensor(h_lo[0:R, q % HS, :], h[0:R, q % HF, :],
                                          h_hi[0:R, q % HS, :].bitcast(F32), ALU.subtract).then_inc(lo_dve.sem, 1)
                    found = behind(at, on, s, WEIGH)
                    if found and found[1] % CH == CH - 1:
                        g, e = found[0], found[1] // CH
                        yy = y_ps[:, y_slot(g, e), :]
                        dve.wait_ge(down_done.sem, down_done.at(g.u, found[1] + 1))
                        if e >= FIRST:
                            dve.wait_ge(cB_done.sem, cB_done.at(g.u, e - FIRST + 1))
                        if e == 0:
                            dve.wait_ge(fin_ps_done.sem, fin_ps_done.at(g.u - 2))
                            to = acc[:, g.slot, :]
                        else:
                            dve.wait_ge(added.sem, added.at(g.u, max(e - 2, 0)))
                            to = part[:, y_slot(g, e), :]
                        if not shared:
                            m = dve.tensor_tensor(to, yy, cB[:, e % CS, :], ALU.mult)
                        elif e == 0:
                            m = dve.tensor_scalar(to, yy, b2[:, 0:1], None, ALU.add)
                        else:
                            m = dve.scalar_tensor_tensor(out=to, in0=yy, scalar=b2[:, e:e + 1],
                                                         in1=cB[:, (e - FIRST) % CS, :], op0=ALU.add, op1=ALU.mult)
                        m.then_inc(weighed.sem, 1)
                    if on(2) and s == hook["finish"]:
                        g = at(2)
                        dve.wait_ge(fin_ps_done.sem, fin_ps_done.at(g.u))
                        tiles = unit_tiles(g)
                        dve.tensor_tensor(tiles, t_ps[:, :].rearrange("p (u f) -> p u f", f=C), tiles,
                                          ALU.add).then_inc(resid_done.sem, 1)
                        if not shared:
                            dve.wait_ge(resid_done.sem, resid_done.at(g.u))
                            for i in range(GROUP):
                                dve.bn_stats(stats[:, bass.ds(g.u * GROUP + i, 1), :].rearrange("p a s -> p (a s)"),
                                             x[:, bass.ds(g.u * GROUP + i, 1), :].rearrange("p a f -> p (a f)"))
                    if not on(0):
                        continue
                    g = at(0)
                    if s == 0:
                        dve.wait_ge(xT_ps_done.sem, xT_ps_done.at(g.u - 1))
                        for i in range(GROUP):
                            u = g.u * GROUP + i
                            m = dve.tensor_scalar(xn[:, i, :], x[:, bass.ds(u, 1), :].rearrange("p a f -> p (a f)"),
                                                  mean[:, bass.ds(u, 1)], rstd[:, bass.ds(u, 1)],
                                                  ALU.subtract, ALU.mult)
                        m.then_inc(xn_done.sem, 1)
                    if s == hook["xT"]:
                        dve.wait_ge(xhi_done.sem, xhi_done.at(g.u))
                        dve.wait_ge(z_done.sem, z_done.at(g.u - 2))
                        dve.tensor_tensor(x_lo[:, g.slot, :], xf[:, :], x_hi[:, g.slot, :].bitcast(F32),
                                          ALU.subtract).then_inc(xlo_done.sem, 1)
                    if s == hook["router"] and not shared:
                        logit = t_ps[:, 0:GROUP * E].rearrange("p (u e) -> p u e", e=E)
                        dve.wait_ge(router_done.sem, router_done.at(g.u))
                        dve.tensor_reduce(red[:, :], logit, AX.X, ALU.max).then_inc(max_done.sem, 1)
                        dve.wait_ge(max_done.sem, max_done.at(g.u))
                        dve.tensor_tensor(probs[:, :, :], logit, red[:, :].unsqueeze(2).to_broadcast([P, GROUP, E]),
                                          ALU.subtract).then_inc(soft_done.sem, 1)
                    for n, name in enumerate(("hidden", "rank", "count", "choose")):
                        if s == hook[name]:
                            route(g, n)
                    if s == hook["split_score"]:
                        dve.wait_ge(hi_scored.sem, hi_scored.at(g.u))
                        dve.wait_ge(scT_ps_done.sem, scT_ps_done.at(g.u - 1))
                        hi = score_hi[:, :, :].bitcast(F32)
                        dve.tensor_copy(split_score[:, :, 0:E], hi)
                        dve.tensor_tensor(split_score[:, :, E:2 * E], score[:, :, :], hi, ALU.subtract
                                          ).then_inc(scored.sem, 1)

            pipeline(dve, GROUPS, DEPTH, step)


def attention1(nc, x, stats, ident, a):
    with stage(nc) as ctx:
        def sb(name, shape, dt=F32):
            return ctx.enter_context(nc.sbuf_tensor("c_" + name, shape, dt))

        def ps(name, shape):
            return ctx.enter_context(nc.psum_tensor("c_" + name, shape, F32))

        def sem(name):
            return ctx.sem("c_" + name)

        def mark(name, per=1):
            return Mark(ctx, nc, "c_" + name, per)

        def split(name, shape):
            return sb(name + "_hi", shape, F32R), sb(name + "_lo", shape, F32R)

        CC = 2
        INNER = H * D1
        KW = N + 2
        wq_hi, wq_lo = split("wq", [P, PAIRS, P])
        wk_hi, wk_lo = split("wk", [P, CC, PAIRS, P])
        wv_hi, wv_lo = split("wv", [P, CC, INNER])
        wo = sb("wo", [P, 2, PAIRS, C], F32R)
        ln_w, ln_b = sb("ln_w", [P, C]), sb("ln_b", [P, C])
        mean, rstd = sb("mean", [P, UNITS]), sb("rstd", [P, UNITS])
        xn = sb("xn", [P, GROUP, C])
        x_hi, x_lo = split("x", [P, GROUP, P])
        craw = sb("craw", [P, CC, COLS])
        c_hi, c_lo = split("c", [P, CC, GROUP, P])
        qx = sb("qx", [P, GROUP, PAIRS, 2, 2, N])
        kx = sb("kx", [P, GROUP, PAIRS, 2 * KW])
        v = sb("v", [P, 2, 2, INNER])
        top, total, recip = (sb(n, [P, 2, PAIRS]) for n in ("top", "total", "recip"))
        prob = sb("prob", [P, 2, PAIRS, P])
        probT = sb("probT", [P, 2, PAIRS, P])
        oT_hi, oT_lo = split("oT", [P, PAIRS, 2, N])
        y_sb = sb("y_sb", [P, GROUP, C])
        y_stats, y_agg = sb("y_stats", [P, 6]), sb("y_agg", [P, GROUP, 2])
        y_var, y_root, y_rstd = (sb(n, [P, GROUP]) for n in ("y_var", "y_root", "y_rstd"))
        scratch, zero = sb("scratch", [P, 1]), sb("zero", [P, 1])

        s_ps = ps("s", [P, 2, PAIRS, P])
        p_ps = ps("p", [P, 2, COLS])
        t_ps = ps("t", [P, 512])
        o_ps = ps("o", [P, PAIRS, N])
        xT_ps = t_ps[:, 0:P]
        y_ps = t_ps[:, P:P + 2 * C].rearrange("p (n f) -> p n f", n=2)
        q_ps, k_ps = ((p_ps[:, n, :], s_ps[:, 0, 4 * n:4 * n + 4, :].rearrange("p r k -> p (r k)")) for n in range(2))

        small = ((ln_w[:, :], a["c_ln_w"]), (ln_b[:, :], a["c_ln_b"]))
        late = [(kx[:, j, :, N:N + 2], a["c_null_k"]) for j in range(GROUP)]
        late += [(v[row:row + 1, s, b, :], a["c_null_v"]) for s in range(2) for b, row in ((0, N), (1, N - 1))]
        late = tuple(late)
        loaded, late_loaded, zeroed, c_in = sem("loaded"), sem("late_loaded"), sem("zeroed"), sem("c_in")
        cleared = sem("cleared")
        xn_done, xT_done, xhi_done, xlo_done = mark("xn"), mark("xT", 4), mark("xhi", 4), mark("xlo", 4)
        chi_done, clo_done = mark("chi", 4), mark("clo", 4)
        q_done, k_done, v_done = mark("q", PAIRS), mark("k", PAIRS), mark("v", 8)
        q_act, q_dve, k_out = mark("q_act", PAIRS), mark("q_dve", PAIRS), mark("k_out", PAIRS)
        v_act, v_dve = mark("v_act", 8), mark("v_dve", 8)
        scores_done, max_done, sub_done, exp_done = mark("scores", 8), mark("max", 8), mark("sub", 8), mark("exp", 8)
        sum_done, recip_done, prob_done = mark("sum", 8), mark("recip", 8), mark("prob", 8)
        turned, probT_done = mark("turned", 8), mark("probT", 8)
        pv_done, ohi_done, olo_done = mark("pv", 8), mark("ohi", 8), mark("olo", 8)
        y_done, y_read, ln_step = mark("y", 4), mark("y_read", 4), mark("ln_step", 13)
        var_done, root_done, yn_done = mark("var"), mark("root"), mark("yn")
        scaled, resid_done = mark("scaled", 2), mark("resid")
        vec_stats, act_stats, stats_ready = finish_stats(nc, ctx, "c_s", stats, mean, rstd, False)

        flat = lambda t: t.rearrange("p r c -> p (r c)")
        jobs = pieces(flat(wq_hi[:, :, :]), flat(wq_lo[:, :, :]), a["c_wq"], 512)
        for cc in range(CC):
            jobs += pieces(flat(wk_hi[:, cc, :, :]), flat(wk_lo[:, cc, :, :]), a["c_wk"][cc], 512)
        EARLY = len(jobs)
        for cc in range(CC):
            jobs += pieces(wv_hi[:, cc, :], wv_lo[:, cc, :], a["c_wv"][cc], 512)
        jobs += pieces(flat(wo[:, 0, :, :]), flat(wo[:, 1, :, :]), a["c_wo"], 512)
        weights = SplitWeights(nc, ctx, "c_sw", jobs)

        DEPTH = 2
        block = ctx.block()
        keys = (slice(0, KEYS1), slice(P - KEYS1, P))

        v_order = (((1, 0), (1, 1)), ((2, 0),), ((2, 1), (3, 0)), ((3, 1),))

        def batch(j, b):
            return 2 * j + b + 1

        def group_x(g):
            return x[:, bass.ds(g.u * GROUP, GROUP), :]

        @block.sync
        def _(sp):
            def load_context(g):
                sp.wait_ge(clo_done.sem, clo_done.at(g.u - 1))
                sp.dma_start(craw[:, :, :], a["c_ctxT"][:, :, bass.ds(g.u * COLS, COLS)]).then_inc(c_in, 16)

            load_context(Turn(0, 0))
            weights.sync(sp)
            for dst, src in small:
                sp.dma_start(dst, src).then_inc(loaded, 16)
            sp.wait_ge(zeroed, 2)
            for dst, src in late:
                sp.dma_start(dst, src).then_inc(late_loaded, 16)

            def step(at, on):
                if on(0) and on(1):
                    load_context(at(0))

            turns(sp, GROUPS, DEPTH, step)

        @block.gpsimd
        def _(pool):
            for m in (chi_done, clo_done, prob_done, scaled, resid_done):
                m.credit(pool)
            pool.memset(zero[:, :], 0.0).then_inc(zeroed, 1)
            pool.memset(v[:, :, :, :], 0.0).then_inc(zeroed, 1)
            pool.wait_ge(zeroed, 2)

            def normalise(g, j, b):
                pool.wait_ge(recip_done.sem, recip_done.at(g.u, batch(j, b)))
                pool.tensor_tensor(prob[:, b, :, keys[b]], prob[:, b, :, keys[b]],
                                   recip[:, b, :].unsqueeze(2).to_broadcast([P, PAIRS, KEYS1]),
                                   ALU.mult).then_inc(prob_done.sem, 1)

            def context(g, j):
                raw = craw[:, :, j * P:(j + 1) * P]
                pool.wait_ge(v_done.sem, v_done.at(g.u - 1, 2 * j + 2))
                pool.wait_ge(k_done.sem, k_done.at(g.u - 1))
                pool.wait_ge(c_in, g.u * 16 + 16)
                pool.tensor_tensor(c_hi[:, :, j, :], raw, zero[:, 0:1].unsqueeze(2).to_broadcast([P, CC, P]),
                                   ALU.subtract).then_inc(chi_done.sem, 1)
                pool.wait_ge(chi_done.sem, chi_done.at(g.u, j + 1))
                pool.tensor_tensor(c_lo[:, :, j, :], raw, c_hi[:, :, j, :].bitcast(F32),
                                   ALU.subtract).then_inc(clo_done.sem, 1)

            def step(at, on):
                if on(1) and not on(2):
                    pool.memset(qx[:, 2:4, :, :, :, :], 0.0).then_inc(cleared, 1)
                    pool.memset(prob[:, :, :, :], 0.0).then_inc(cleared, 1)
                    pool.wait_ge(cleared, 3)
                for j in range(GROUP):
                    if on(0) and not on(1):
                        weights.rest(pool, *weights.share(j, GROUP), True)
                    if j == 0 and on(2):
                        g = at(2)
                        wide = lambda t: t[:, :].unsqueeze(1).to_broadcast([P, GROUP, C])
                        pool.wait_ge(loaded, 16 * len(small))
                        pool.wait_ge(yn_done.sem, yn_done.at(g.u))
                        pool.tensor_tensor(y_sb[:, :, :], y_sb[:, :, :], wide(ln_w), ALU.mult).then_inc(scaled.sem, 1)
                        pool.wait_ge(scaled.sem, scaled.at(g.u, 1))
                        pool.tensor_tensor(y_sb[:, :, :], y_sb[:, :, :], wide(ln_b), ALU.add).then_inc(scaled.sem, 1)
                        pool.wait_ge(scaled.sem, scaled.at(g.u))
                        pool.tensor_tensor(group_x(g), group_x(g), y_sb[:, :, :], ALU.add).then_inc(resid_done.sem, 1)
                    if on(1):
                        normalise(at(1), j, 0)
                        normalise(at(1), j, 1)
                    if on(0) and j == 1:
                        context(at(0), 0)
                    if on(0) and j:
                        context(at(0), j)

            turns(pool, GROUPS, DEPTH, step)

        @block.scalar
        def _(act):
            for m in (xhi_done, q_act, k_out, v_act, exp_done, probT_done, ohi_done, root_done):
                m.credit(act)
            act_stats(act)
            def copy_probs(g, j, b):
                act.wait_ge(turned.sem, turned.at(g.u, batch(j, b)))
                act.wait_ge(pv_done.sem, pv_done.at(g.u, batch(j - 1, b)))
                act.activation(probT[:, b, :, :], s_ps[:, b, :, :], ACT.Copy).then_inc(probT_done.sem, 1)

            def exps(g, j, b):
                act.wait_ge(sub_done.sem, sub_done.at(g.u, batch(j, b)))
                act.activation(prob[:, b, :, keys[b]], prob[:, b, :, keys[b]], ACT.Exp).then_inc(exp_done.sem, 1)

            def output_hi(g, j, b):
                act.wait_ge(pv_done.sem, pv_done.at(g.u, batch(j, b)))
                act.wait_ge(y_done.sem, y_done.at(g.u, j))
                act.activation(oT_hi[:, :, b, :], o_ps[:, :, :], ACT.Copy).then_inc(ohi_done.sem, 1)

            def queries_keys(g, r):
                act.wait_ge(q_done.sem, q_done.at(g.u, r + 1))
                act.wait_ge(scores_done.sem, scores_done.at(g.u - 1))
                act.activation(qx[0:N, :, r, :, 0, :], q_ps[r % 2][0:N, :].rearrange("p (u b q) -> p u b q", u=GROUP, b=2),
                               ACT.Copy, scale=float(D1) ** -0.5).then_inc(q_act.sem, 1)
                act.wait_ge(k_done.sem, k_done.at(g.u, r + 1))
                act.activation(kx[:, :, r, :].rearrange("p u (b k) -> p u b k", b=2)[:, :, :, 0:N],
                               k_ps[r % 2].rearrange("p (u b k) -> p u b k", u=GROUP, b=2), ACT.Copy
                               ).then_inc(k_out.sem, 1)

            def values_out(g, j):
                act.wait_ge(v_done.sem, v_done.at(g.u, 2 * j + 1))
                act.wait_ge(pv_done.sem, pv_done.at(g.u, batch(j - 2, 1)))
                for b in range(2):
                    r = slice(b * N, (b + 1) * N)
                    act.activation(v[r, j % 2, b, 0:512], p_ps[r, 0, :], ACT.Copy).then_inc(v_act.sem, 1)

            def x_part(g, j):
                act.wait_ge(xT_done.sem, xT_done.at(g.u, j + 1))
                act.wait_ge(q_done.sem, q_done.at(g.u - 1))
                act.activation(x_hi[:, j, :], xT_ps, ACT.Copy).then_inc(xhi_done.sem, 1)

            def step(at, on):
                if on(1) and not on(2):
                    act.wait_ge(zeroed, 2)
                    act.wait_ge(cleared, 3)
                if on(2):
                    output_hi(at(2), 3, 0)
                for r in range(PAIRS):
                    if on(1):
                        queries_keys(at(1), r)
                    if r == 1 and on(2):
                        output_hi(at(2), 3, 1)
                    if r == 5 and on(2):
                        g = at(2)
                        act.wait_ge(var_done.sem, var_done.at(g.u))
                        act.activation(y_root[:, :], y_var[:, :], ACT.Sqrt).then_inc(root_done.sem, 1)
                for j in range(GROUP):
                    if on(0) and not on(1):
                        weights.scalar(act, *weights.share(j, GROUP))
                    if j and on(0):
                        x_part(at(0), j)
                    if j and on(1):
                        output_hi(at(1), j - 1, 0)
                    if on(1):
                        if j == 0:
                            values_out(at(1), 0)
                        exps(at(1), j, 0)
                        if j:
                            output_hi(at(1), j - 1, 1)
                        exps(at(1), j, 1)
                        for unit, n in v_order[j]:
                            if n == 0:
                                values_out(at(1), unit)
                    if j == 0 and on(0):
                        x_part(at(0), 0)
                    if on(1):
                        copy_probs(at(1), j, 0)
                        copy_probs(at(1), j, 1)

            turns(act, GROUPS, DEPTH, step)

        @block.tensor
        def _(pe):
            for m in (xT_done, q_done, k_done, v_done, scores_done, turned, pv_done, y_done):
                m.credit(pe)

            def three(dst, hi, lo, m_hi, m_lo, start=True, stop=True):
                pe.matmul(dst, hi, m_hi, start=start, stop=False)
                pe.matmul(dst, hi, m_lo, start=False, stop=False)
                return pe.matmul(dst, lo, m_hi, start=False, stop=stop)

            def queries_keys(g, r):
                if r == 0:
                    weights.wait(pe, EARLY)
                    pe.wait_ge(xlo_done.sem, xlo_done.at(g.u))
                    pe.wait_ge(v_act.sem, v_act.at(g.u - 1))
                elif r == 1:
                    pe.wait_ge(probT_done.sem, probT_done.at(g.u - 1, batch(3, 0)))
                else:
                    pe.wait_ge(q_act.sem, q_act.at(g.u, r - 1))
                    pe.wait_ge(q_dve.sem, q_dve.at(g.u, r - 1))
                tokens = lambda t: t[:, :, :].rearrange("p u t -> p (u t)")
                three(q_ps[r % 2], wq_hi[:, r, :], wq_lo[:, r, :], tokens(x_hi), tokens(x_lo)).then_inc(q_done.sem, 1)
                if r == 0:
                    pe.wait_ge(clo_done.sem, clo_done.at(g.u))
                    pe.wait_ge(v_dve.sem, v_dve.at(g.u - 1))
                elif r > 1:
                    pe.wait_ge(k_out.sem, k_out.at(g.u, r - 1))
                for cc in range(CC):
                    m = three(k_ps[r % 2], wk_hi[:, cc, r, :], wk_lo[:, cc, r, :], tokens(c_hi[:, cc, :, :]),
                              tokens(c_lo[:, cc, :, :]), cc == 0, cc == CC - 1)
                m.then_inc(k_done.sem, 1)

            def v_product(g, j, n):
                if j == 0:
                    if n == 0:
                        pe.wait_ge(q_act.sem, q_act.at(g.u, PAIRS - 1))
                        pe.wait_ge(q_dve.sem, q_dve.at(g.u, PAIRS - 1))
                    else:
                        pe.wait_ge(k_out.sem, k_out.at(g.u, PAIRS - 1))
                else:
                    m = v_dve if n else v_act
                    pe.wait_ge(m.sem, m.at(g.u, 2 * j))
                for cc in range(CC):
                    cols = slice(n * 512, (n + 1) * 512)
                    m = three(p_ps[:, n, :], c_hi[:, cc, j, :], c_lo[:, cc, j, :],
                              wv_hi[:, cc, cols], wv_lo[:, cc, cols], cc == 0, cc == CC - 1)
                m.then_inc(v_done.sem, 1)

            def scores(g, j, b):
                if j == 0 and b == 0:
                    pe.wait_ge(late_loaded, 16 * len(late))
                    pe.wait_ge(q_act.sem, q_act.at(g.u))
                    pe.wait_ge(q_dve.sem, q_dve.at(g.u))
                    pe.wait_ge(k_out.sem, k_out.at(g.u))
                pe.wait_ge(probT_done.sem, probT_done.at(g.u, batch(j - 1, b)))
                first = b * (KW - 1)
                for r in range(PAIRS):
                    m = pe.matmul(s_ps[:, b, r, 0:KEYS1], qx[:, j, r, b, :, :].rearrange("p h q -> p (h q)"),
                                  kx[:, j, r, first:first + KEYS1], start=True, stop=True)
                m.then_inc(scores_done.sem, 1)

            def turn_probs(g, j, b):
                pe.wait_ge(prob_done.sem, prob_done.at(g.u, batch(j, b)))
                for r in range(PAIRS):
                    m = pe.transpose(s_ps[:, b, r, :], prob[:, b, r, :], ident[:, :])
                m.then_inc(turned.sem, 1)

            def values(g, j, b):
                pe.wait_ge(probT_done.sem, probT_done.at(g.u, batch(j, b)))
                pe.wait_ge(v_act.sem, v_act.at(g.u, 2 * j + 2))
                pe.wait_ge(v_dve.sem, v_dve.at(g.u, 2 * j + 2))
                pe.wait_ge(olo_done.sem, olo_done.at(g.u, batch(j, b) - 1))
                for r in range(PAIRS):
                    for par in range(2):
                        h = 2 * r + par
                        m = pe.matmul(o_ps[par * N:(par + 1) * N, r, :], v[:, j % 2, b, h * D1:(h + 1) * D1],
                                      probT[:, b, r, par * N:(par + 1) * N], start=True, stop=True)
                m.then_inc(pv_done.sem, 1)

            def output(g, j, following):
                pe.wait_ge(olo_done.sem, olo_done.at(g.u, batch(j, 1)))
                pe.wait_ge(y_read.sem, y_read.at(g.u, j))
                if following:
                    pe.wait_ge(xlo_done.sem, xlo_done.at(following.u, j + 2))
                rows = lambda t, r: t[:, r, :, :].rearrange("p b q -> p (b q)")
                for r in range(PAIRS):
                    if r:
                        pe.matmul(y_ps[:, 0, :], rows(oT_lo, r), wo[:, 0, r, :], start=False, stop=False)
                    m = pe.matmul(y_ps, rows(oT_hi, r), wo[:, :, r, :], start=(r == 0), stop=(r == PAIRS - 1))
                    if r == 0:
                        pe.matmul(y_ps[:, 0, :], rows(oT_lo, 0), wo[:, 0, 0, :], start=False, stop=False)
                m.then_inc(y_done.sem, 1)

            def turn_x(g, j):
                pe.wait_ge(xn_done.sem, xn_done.at(g.u))
                pe.wait_ge(y_read.sem, y_read.at(g.u - 1, max(j - 1, 0)))
                pe.wait_ge(xlo_done.sem, xlo_done.at(g.u, j))
                pe.transpose(xT_ps, xn[:, j, :], ident[:, :]).then_inc(xT_done.sem, 1)

            def step(at, on):
                if on(2):
                    values(at(2), 3, 0)
                for r in range(PAIRS):
                    if on(1):
                        queries_keys(at(1), r)
                    if r == 1 and on(2):
                        values(at(2), 3, 1)
                    if r == 3 and on(2):
                        output(at(2), 3, None)
                for j in range(GROUP):
                    if j == 0 and on(1):
                        weights.wait(pe, len(jobs))
                        v_product(at(1), 0, 0)
                        v_product(at(1), 0, 1)
                    if on(1):
                        scores(at(1), j, 0)
                    if j and on(0):
                        turn_x(at(0), j)
                    if on(1):
                        if j:
                            values(at(1), j - 1, 0)
                        scores(at(1), j, 1)
                        if j:
                            values(at(1), j - 1, 1)
                        for unit, n in v_order[j]:
                            v_product(at(1), unit, n)
                    if j == 0 and on(0):
                        turn_x(at(0), 0)
                    if on(1):
                        turn_probs(at(1), j, 0)
                        if j:
                            output(at(1), j - 1, at(0) if on(0) else None)
                        turn_probs(at(1), j, 1)

            turns(pe, GROUPS, DEPTH, step)

        @block.vector
        def _(dve):
            for m in (xn_done, xlo_done, q_dve, v_dve, max_done, sub_done, sum_done, recip_done, olo_done, y_read,
                      ln_step, var_done, yn_done):
                m.credit(dve)
            vec_stats(dve)
            dve.wait_ge(stats_ready, 1)
            def shift(g, j, b):
                raw = s_ps[:, b, :, 0:KEYS1]
                n = batch(j, b)
                dve.wait_ge(scores_done.sem, scores_done.at(g.u, n))
                dve.tensor_reduce(top[:, b, :], raw, AX.X, ALU.max).then_inc(max_done.sem, 1)
                dve.wait_ge(max_done.sem, max_done.at(g.u, n))
                dve.wait_ge(turned.sem, turned.at(g.u, batch(j - 1, b)))
                dve.tensor_tensor(prob[:, b, :, keys[b]], raw, top[:, b, :].unsqueeze(2).to_broadcast([P, PAIRS, KEYS1]),
                                  ALU.subtract).then_inc(sub_done.sem, 1)

            def denominators(g, j, b):
                n = batch(j, b)
                dve.wait_ge(exp_done.sem, exp_done.at(g.u, n))
                dve.tensor_reduce(total[:, b, :], prob[:, b, :, keys[b]], AX.X, ALU.add).then_inc(sum_done.sem, 1)
                dve.wait_ge(sum_done.sem, sum_done.at(g.u, n))
                dve.wait_ge(prob_done.sem, prob_done.at(g.u, batch(j - 1, b)))
                dve.reciprocal(recip[:, b, :], total[:, b, :]).then_inc(recip_done.sem, 1)

            def output_lo(g, j, b):
                dve.wait_ge(ohi_done.sem, ohi_done.at(g.u, batch(j, b)))
                dve.tensor_tensor(oT_lo[:, :, b, :], o_ps[:, :, :], oT_hi[:, :, b, :].bitcast(F32),
                                  ALU.subtract).then_inc(olo_done.sem, 1)

            def queries(g, r):
                dve.wait_ge(q_done.sem, q_done.at(g.u, r + 1))
                dve.wait_ge(scores_done.sem, scores_done.at(g.u - 1))
                dve.tensor_scalar(qx[N:P, :, r, :, 1, :], q_ps[r % 2][N:P, :].rearrange("p (u b q) -> p u b q", u=GROUP, b=2),
                                  float(D1) ** -0.5, None, ALU.mult).then_inc(q_dve.sem, 1)

            def values_out(g, j):
                dve.wait_ge(v_done.sem, v_done.at(g.u, 2 * j + 2))
                dve.wait_ge(pv_done.sem, pv_done.at(g.u, batch(j - 2, 1)))
                for b in range(2):
                    r = slice(b * N, (b + 1) * N)
                    dve.tensor_copy(v[r, j % 2, b, 512:1024], p_ps[r, 1, :]).then_inc(v_dve.sem, 1)

            def y_out(g, j):
                dve.wait_ge(y_done.sem, y_done.at(g.u, j + 1))
                dve.wait_ge(resid_done.sem, resid_done.at(g.u - 1))
                dve.tensor_copy(y_sb[:, j, :], y_ps[:, 0, :]).then_inc(ln_step.sem, 1)
                dve.wait_ge(ln_step.sem, ln_step.at(g.u, 3 * j + 1))
                dve.tensor_tensor(y_sb[:, j, :], y_ps[:, 1, :], y_sb[:, j, :], ALU.add).then_inc(y_read.sem, 1)
                dve.wait_ge(y_read.sem, y_read.at(g.u, j + 1))
                dve.bn_stats(y_stats[:, :], y_sb[:, j, :]).then_inc(ln_step.sem, 1)
                dve.wait_ge(ln_step.sem, ln_step.at(g.u, 3 * j + 2))
                dve.memset(scratch[:, :], 0.0)
                dve.bn_aggr(y_agg[:, j, :], y_stats[:, :]).then_inc(ln_step.sem, 1)


            def step(at, on):
                if on(1) and not on(2):
                    dve.wait_ge(zeroed, 2)
                    dve.wait_ge(cleared, 3)
                if on(2):
                    output_lo(at(2), 3, 0)
                for r in range(PAIRS):
                    if on(1):
                        queries(at(1), r)
                    if r == 1 and on(2):
                        output_lo(at(2), 3, 1)
                    if r == 2 and on(0):
                        g = at(0)
                        dve.wait_ge(xT_done.sem, xT_done.at(g.u - 1))
                        for j in range(GROUP):
                            u = g.u * GROUP + j
                            m = dve.tensor_scalar(xn[:, j, :], x[:, bass.ds(u, 1), :].rearrange("p a f -> p (a f)"),
                                                  mean[:, bass.ds(u, 1)], rstd[:, bass.ds(u, 1)],
                                                  ALU.subtract, ALU.mult)
                        m.then_inc(xn_done.sem, 1)
                    if r == 4 and on(2):
                        g = at(2)
                        y_out(g, 3)
                        dve.wait_ge(ln_step.sem, ln_step.at(g.u, 12))
                        dve.tensor_scalar(y_var[:, :], y_agg[:, :, 1], 1e-6, None, ALU.add).then_inc(var_done.sem, 1)
                    if r == 6 and on(2):
                        g = at(2)
                        dve.wait_ge(root_done.sem, root_done.at(g.u))
                        dve.reciprocal(y_rstd[:, :], y_root[:, :]).then_inc(ln_step.sem, 1)
                        dve.wait_ge(ln_step.sem, ln_step.at(g.u))
                        dve.wait_ge(y_read.sem, y_read.at(g.u))
                        for j in range(GROUP):
                            m = dve.tensor_scalar(y_sb[:, j, :], y_sb[:, j, :], y_agg[:, j, 0:1], y_rstd[:, j:j + 1],
                                                  ALU.subtract, ALU.mult)
                        m.then_inc(yn_done.sem, 1)
                for j in range(GROUP):
                    if on(0) and not on(1):
                        weights.rest(dve, *weights.share(j, GROUP), False)
                        if j == 2:
                            dve.memset(qx[:, 0:2, :, :, :, :], 0.0).then_inc(cleared, 1)
                    if on(1):
                        if j == 0:
                            values_out(at(1), 0)
                        shift(at(1), j, 0)
                    if j and on(0):
                        x_lo_part(dve, at(0), j)
                    if on(1):
                        g = at(1)
                        if j:
                            output_lo(g, j - 1, 0)
                            denominators(g, j, 0)
                        shift(g, j, 1)
                        if j == 0:
                            denominators(g, j, 0)
                        if j:
                            output_lo(g, j - 1, 1)
                        denominators(g, j, 1)
                        for unit, n in v_order[j]:
                            if n == 1:
                                values_out(g, unit)
                        if j:
                            y_out(g, j - 1)
                    if j == 0 and on(0):
                        x_lo_part(dve, at(0), 0)
                    if j == 2 and on(2):
                        g = at(2)
                        dve.wait_ge(resid_done.sem, resid_done.at(g.u))
                        for i in range(GROUP):
                            u = g.u * GROUP + i
                            dve.bn_stats(stats[:, bass.ds(u, 1), :].rearrange("p a s -> p (a s)"),
                                         x[:, bass.ds(u, 1), :].rearrange("p a f -> p (a f)"))

            def x_lo_part(dve, g, j):
                dve.wait_ge(xhi_done.sem, xhi_done.at(g.u, j + 1))
                dve.wait_ge(q_done.sem, q_done.at(g.u - 1))
                dve.tensor_tensor(x_lo[:, j, :], xT_ps, x_hi[:, j, :].bitcast(F32),
                                  ALU.subtract).then_inc(xlo_done.sem, 1)

            turns(dve, GROUPS, DEPTH, step)


def program(nc, a, out):
    with ExitStack() as ctx:
        x = ctx.enter_context(nc.sbuf_tensor("x_resid", [P, UNITS, C], F32))
        stats = ctx.enter_context(nc.sbuf_tensor("x_stats", [P, UNITS, 6], F32))
        ident = ctx.enter_context(nc.sbuf_tensor("identity", [P, P], F32))
        headmask = ctx.enter_context(nc.sbuf_tensor("headmask", [P, H], F32))
        attention0(nc, x, stats, ident, headmask, a["x"], a["a_wqkvT"], a["a_wprojT"], a["a_bproj"],
                   a["a_ctx_kT"], a["a_ctx_v"], a)
        experts(nc, x, stats, ident, a, False, out)
        attention1(nc, x, stats, ident, a)
        experts(nc, x, stats, ident, a, True, out)


def layout(inp):
    f = lambda n: np.asarray(inp[n])
    x, c = f("x"), f("ctx_2048")
    d = {"x": x.reshape(B * N, C)}
    d["a_wqkvT"] = f("L0_xattn_w_qkv").reshape(3, P, C).transpose(2, 0, 1)
    wp = f("L0_xattn_w_proj").T.reshape(PAIRS, 2, D0, C).transpose(0, 2, 1, 3).reshape(N, 2, C)
    d["a_wprojT"] = np.concatenate([wp, wp])
    d["a_bproj"] = np.broadcast_to(f("L0_xattn_b_proj"), (P, C))
    d["a_ctx_kT"] = c[:, :, :C].reshape(B * N, C).T
    v = c[:, :, C:].reshape(UNITS, 2, N, C)[:, ::-1]
    d["a_ctx_v"] = v.reshape(UNITS, P, C).transpose(1, 0, 2).reshape(P, UNITS * C)
    gate, up = (f(n).reshape(E * 336, C).T for n in ("L0_ffn_gate_w", "L0_ffn_up_w"))
    d["b_w"] = np.stack([gate, up])
    d["b_wd"] = f("L0_ffn_down_w").transpose(0, 2, 1).reshape(E * 3, 112, C).transpose(1, 0, 2).reshape(112, -1)
    d["b_rw"] = f("L0_ffn_router_w").T
    aw1 = np.zeros((C, P), np.float32)
    aw1[:, :50] = f("L0_ffn_actor_w1").T
    d["b_aw1T"] = aw1
    d["b_ab1"] = f("L0_ffn_actor_b1").reshape(50, 1)
    d["b_aw2T"] = f("L0_ffn_actor_w2").T
    d["b_ab2"] = np.broadcast_to(f("L0_ffn_actor_b2"), (P, 6))
    d["kcode"] = np.broadcast_to(np.arange(1, 7, dtype=np.float32) - 100, (P, 6))
    d["before"] = np.broadcast_to(np.tril(np.ones((E, E), np.float32), -1), (P, E, E))
    sel = np.zeros((P, E, P), np.float32)
    for e in range(E):
        sel[e, e] = sel[E + e, e] = 1
    d["sel"] = sel.reshape(P, E * P)
    d["c_wq"] = f("L1_xattn_Wq")
    wkv = f("L1_xattn_Wkv").reshape(2, P, 2, H * 64)
    d["c_wk"], d["c_wv"] = wkv[:, :, 0], wkv[:, :, 1]
    d["c_wo"] = f("L1_xattn_Wout").reshape(PAIRS, P, C).transpose(1, 0, 2).reshape(P, PAIRS * C)
    null = f("L1_xattn_null_kv")
    d["c_null_k"] = np.broadcast_to(np.tile(null[0], 2)[:, None, None], (P, PAIRS, 2))
    d["c_null_v"] = np.tile(null[1], H)[None]
    d["c_ln_w"] = np.broadcast_to(f("L1_xattn_ln_scale"), (P, C))
    d["c_ln_b"] = np.broadcast_to(f("L1_xattn_ln_bias"), (P, C))
    d["c_ctxT"] = c.reshape(B * N, 2, P).transpose(2, 1, 0)
    w1 = np.concatenate([f("L1_ffn_sw1")[None], f("L1_ffn_ew1")])
    w2 = np.concatenate([f("L1_ffn_sw2")[None], f("L1_ffn_ew2")])
    d["d_w"] = w1.transpose(1, 0, 2).reshape(1, P, -1)
    d["d_wd"] = w2.reshape((E + 1) * 4, P, C).transpose(1, 0, 2).reshape(P, -1)
    d["d_rw"] = f("L1_ffn_router_w").T
    d["d_b1"] = np.concatenate([f("L1_ffn_sb1")[None], f("L1_ffn_eb1")]).reshape((E + 1) * 4, P).T
    d["d_b2"] = np.concatenate([f("L1_ffn_sb2")[None], f("L1_ffn_eb2")]).T
    d["d_norm"] = f("L1_ffn_norm_weight").reshape(P, 1)
    d["ident"] = np.eye(P, dtype=np.float32)
    d["headmask"] = np.repeat(np.eye(H, dtype=np.float32), D0, axis=0)
    return {k: np.ascontiguousarray(v) for k, v in d.items()}


def kernel(**inputs):
    import concourse.bacc as bacc
    from concourse.bass_utils import run_bass_kernel_spmd

    nc = bacc.Bacc("TRN2", target_bir_lowering=False, num_devices=1)
    arrays = {f"in_{k}_dram": v for k, v in layout(inputs).items()}
    args = {k[3:-5]: nc.dram_tensor(k, v.shape, mybir.dt.from_np(v.dtype), kind="ExternalInput").ap()
            for k, v in arrays.items()}
    out = nc.dram_tensor("out_dram", (B * N, C), F32, kind="ExternalOutput").ap()
    program(nc, args, out)
    got = run_bass_kernel_spmd(nc, [arrays], core_ids=[0])
    return got.results[0]["out_dram"].reshape(B, N, C)
```
